# Optimizing a Trainium2 kernel written in Bass

```python
import numpy as np
import jax
import jax.numpy as jnp

def _softmax(x, axis=-1):
    return jax.nn.softmax(x, axis=axis)

def _gelu(x):
    return jax.nn.gelu(x, approximate=True)

def _silu(x):
    return jax.nn.silu(x)

def _sigmoid(x):
    return jax.nn.sigmoid(x)

def _layernorm(x, axis=-1, eps=1e-05):
    m = jnp.mean(x, axis=axis, keepdims=True)
    v = jnp.var(x, axis=axis, keepdims=True)
    return (x - m) / jnp.sqrt(v + eps)

def _scatter_add(tgt, idx, src, axis=0):
    return tgt.at[idx].add(src)

def _segment_sum(src, seg, n):
    return jax.ops.segment_sum(src, seg, n)
kernel_name = 'mk_gnn_ffn_d4_gnn_r32_c1dbd3'

def setup_inputs(seed: int=0):
    np.random.seed(seed)
    _w = jnp.asarray

    def _rec_inputs():
        import jax
        import jax.numpy as jnp
        _gk = jax.random.key(seed)
        x = -0.0003713 + 1 * jax.random.normal(jax.random.fold_in(_gk, 1), (3125, 256), jnp.float32)
        src = jax.random.randint(jax.random.fold_in(_gk, 2), (50000,), 0, 3125, jnp.int32)
        dst = jax.random.randint(jax.random.fold_in(_gk, 3), (50000,), 0, 3125, jnp.int32)
        _o = jnp.argsort(dst, stable=True)
        src = src[_o]
        dst = dst[_o]
        edge_type_6 = jax.random.randint(jax.random.fold_in(_gk, 14), (50000,), 0, 6, jnp.int32)
        edge_type_64 = jax.random.randint(jax.random.fold_in(_gk, 15), (50000,), 0, 64, jnp.int32)
        return (x, src, dst, edge_type_6, edge_type_64)
    x, src, dst, edge_type_6, edge_type_64 = _rec_inputs()

    def _L0_gnn_setup():
        import jax, jax.numpy as jnp
        import numpy as np
        N_NODES = 50000
        N_EDGES = 15625
        IN_DIM = 256
        HID = 64
        HEADS = 4
        N_REL = 64
        key = jax.random.key(seed)
        ks = jax.random.split(key, 16)
        s = 0.02
        return {'node_features': jax.random.normal(ks[0], (N_NODES, IN_DIM), jnp.float32), 'edge_index': jax.random.randint(ks[1], (2, N_EDGES), 0, N_NODES, jnp.int32), 'edge_relations': jax.random.randint(ks[2], (N_EDGES,), 0, N_REL, jnp.int32), 'query_emb': jax.random.normal(ks[3], (IN_DIM,), jnp.float32), 'Wq': jax.random.normal(ks[4], (IN_DIM, HID * HEADS), jnp.float32) * s, 'bq': jnp.zeros((HID * HEADS,), jnp.float32), 'Wk': jax.random.normal(ks[5], (IN_DIM, HID * HEADS), jnp.float32) * s, 'bk': jnp.zeros((HID * HEADS,), jnp.float32), 'Wv': jax.random.normal(ks[6], (IN_DIM, HID * HEADS), jnp.float32) * s, 'bv': jnp.zeros((HID * HEADS,), jnp.float32), 'rel_w': jax.random.normal(ks[7], (N_REL, HID), jnp.float32) * s, 'Wo': jax.random.normal(ks[8], (HID * HEADS, IN_DIM), jnp.float32) * s, 'bo': jnp.zeros((IN_DIM,), jnp.float32), 'gamma': jnp.ones((IN_DIM,), jnp.float32), 'beta': jnp.zeros((IN_DIM,), jnp.float32)}
    _L0_gnn_all = _L0_gnn_setup()
    _L0_gnn_in = {k: v for k, v in _L0_gnn_all.items() if k in ('query_emb', 'Wq', 'bq', 'Wk', 'bk', 'Wv', 'bv', 'rel_w', 'Wo', 'bo', 'gamma', 'beta')}
    del _L0_gnn_all

    def _L0_ffn_setup():
        import jax, jax.numpy as jnp
        import numpy as np
        NUM_EXPERTS = 8
        TOP_K = 2
        B, S, D = (8, 256, 256)

        def _moe(tokens, router_w, w1, b1, w2, b2):
            N = tokens.shape[0]
            E = router_w.shape[0]
            logits = tokens.astype(jnp.float32) @ router_w.astype(jnp.float32).T
            probs = jax.nn.softmax(logits, axis=-1)
            rw, re = jax.lax.top_k(probs, TOP_K)
            if TOP_K > 1:
                rw = rw / jnp.maximum(rw.sum(-1, keepdims=True), 1e-12)
            rw = rw.astype(tokens.dtype)
            combine = jnp.zeros((N, E), tokens.dtype).at[jnp.arange(N)[:, None], re].set(rw)
            out = tokens
            for e in range(E):
                h = jax.nn.gelu(tokens @ w1[e] + b1[e], approximate=False)
                y = h @ w2[e] + b2[e]
                out = out + combine[:, e:e + 1] * y
            return out
        key = jax.random.key(seed)
        ks = jax.random.split(key, 4)
        scale = 1.0 / np.sqrt(D).astype(np.float32)
        return {'input_embeddings': jax.random.normal(ks[0], (B, S, D), jnp.float32), 'router_w': jax.random.normal(ks[1], (NUM_EXPERTS, D), jnp.float32) * scale, 'w1': jax.random.normal(ks[2], (NUM_EXPERTS, D, D), jnp.float32) * scale, 'b1': jnp.zeros((NUM_EXPERTS, D), jnp.float32), 'w2': jax.random.normal(ks[3], (NUM_EXPERTS, D, D), jnp.float32) * scale, 'b2': jnp.zeros((NUM_EXPERTS, D), jnp.float32)}
    _L0_ffn_all = _L0_ffn_setup()
    _L0_ffn_in = {k: v for k, v in _L0_ffn_all.items() if k in ('router_w', 'w1', 'b1', 'w2', 'b2')}
    del _L0_ffn_all

    def _L1_gnn_setup():
        import jax, jax.numpy as jnp
        import numpy as np
        N_NODES = 50000
        N_EDGES = 12500
        D_IN = 256
        D_OUT = 256
        N_REL = 6
        N_HEADS = 4
        key = jax.random.key(seed)
        ks = jax.random.split(key, 12)
        s_in = 1.0 / np.sqrt(D_IN)
        s_out = 1.0 / np.sqrt(D_OUT)
        return {'x': jax.random.normal(ks[0], (N_NODES, D_IN), dtype=jnp.float32), 'edge_index': jax.random.randint(ks[1], (2, N_EDGES), 0, N_NODES, dtype=jnp.int64), 'edge_types': jax.random.randint(ks[2], (N_EDGES,), 0, N_REL, dtype=jnp.int64), 'W': jax.random.uniform(ks[3], (N_REL, D_IN, D_OUT), jnp.float32, -s_in, s_in), 'b': jax.random.uniform(ks[4], (N_REL, D_OUT), jnp.float32, -s_in, s_in), 'in_proj_w': jax.random.uniform(ks[5], (3 * D_OUT, D_OUT), jnp.float32, -s_out, s_out), 'in_proj_b': jnp.zeros((3 * D_OUT,), jnp.float32), 'attn_out_w': jax.random.uniform(ks[6], (D_OUT, D_OUT), jnp.float32, -s_out, s_out), 'attn_out_b': jnp.zeros((D_OUT,), jnp.float32), 'proj_w': jax.random.uniform(ks[7], (D_OUT, D_OUT), jnp.float32, -s_out, s_out), 'proj_b': jax.random.uniform(ks[8], (D_OUT,), jnp.float32, -s_out, s_out)}
    _L1_gnn_all = _L1_gnn_setup()
    _L1_gnn_in = {k: v for k, v in _L1_gnn_all.items() if k in ('W', 'b', 'in_proj_w', 'in_proj_b', 'attn_out_w', 'attn_out_b', 'proj_w', 'proj_b')}
    del _L1_gnn_all

    def _L1_ffn_setup():
        import jax, jax.numpy as jnp
        import numpy as np
        TOP_K = 2
        LN_EPS = 1e-05
        key = jax.random.key(seed)
        ks = jax.random.split(key, 8)
        B, S, D, E, H = (16, 1024, 256, 8, 1024)
        x = jax.random.normal(ks[0], (B, S, D), dtype=jnp.float32)
        Wr = jax.random.normal(ks[1], (D, E), dtype=jnp.float32) * 0.1
        br = jnp.zeros((E,), dtype=jnp.float32)
        ln_g = jnp.ones((E, D), dtype=jnp.float32)
        ln_b = jnp.zeros((E, D), dtype=jnp.float32)
        W1 = jax.random.normal(ks[2], (E, D, H), dtype=jnp.float32) * (1.0 / np.sqrt(D))
        b1 = jnp.zeros((E, H), dtype=jnp.float32)
        W2 = jax.random.normal(ks[3], (E, H, D), dtype=jnp.float32) * (1.0 / np.sqrt(H))
        b2 = jnp.zeros((E, D), dtype=jnp.float32)
        return {'x': x, 'Wr': Wr, 'br': br, 'ln_g': ln_g, 'ln_b': ln_b, 'W1': W1, 'b1': b1, 'W2': W2, 'b2': b2}
    _L1_ffn_all = _L1_ffn_setup()
    _L1_ffn_in = {k: v for k, v in _L1_ffn_all.items() if k in ('Wr', 'br', 'ln_g', 'ln_b', 'W1', 'b1', 'W2', 'b2')}
    del _L1_ffn_all

    def _L2_gnn_setup():
        import jax, jax.numpy as jnp
        import numpy as np
        N_NODES = 3125
        N_EDGES = 50000
        IN_FEATS = 256
        OUT_FEATS = 256
        key = jax.random.key(seed)
        k1, k2, k3, k4, k5, k6 = jax.random.split(key, 6)
        h = jax.random.normal(k1, (N_NODES, IN_FEATS), dtype=jnp.float32)
        norm = jax.random.uniform(k2, (N_NODES, 1), dtype=jnp.float32)
        W = jax.random.normal(k3, (OUT_FEATS, IN_FEATS), dtype=jnp.float32) * (1.0 / np.sqrt(IN_FEATS))
        b = jax.random.normal(k4, (OUT_FEATS,), dtype=jnp.float32) * 0.01
        src = jax.random.randint(k5, (N_EDGES,), 0, N_NODES, dtype=jnp.int32)
        dst = jax.random.randint(k6, (N_EDGES,), 0, N_NODES, dtype=jnp.int32)
        return {'h': h, 'norm': norm, 'W': W, 'b': b, 'src': src, 'dst': dst}
    _L2_gnn_all = _L2_gnn_setup()
    _L2_gnn_in = {k: v for k, v in _L2_gnn_all.items() if k in ('W', 'b')}
    del _L2_gnn_all

    def _L2_ffn_setup():
        import jax, jax.numpy as jnp
        import numpy as np
        BN_EPS = 0.001

        def _bn(h, g, b, m, v):
            return g * (h - m) * jax.lax.rsqrt(v + BN_EPS) + b
        key = jax.random.key(seed)
        ks = jax.random.split(key, 8)
        B, F, Df = (256, 64, 256)
        E, H, D = (8, 256, 256)
        s1 = 1.0 / np.sqrt(Df)
        s2 = 1.0 / np.sqrt(H)
        return {'x': jax.random.normal(ks[0], (B, F, Df), jnp.float32), 'Wr': jax.random.normal(ks[1], (Df, E), jnp.float32) * s1, 'br': jnp.zeros((E,), jnp.float32), 'W1': jax.random.normal(ks[2], (E, Df, H), jnp.float32) * s1, 'b1': jnp.zeros((E, H), jnp.float32), 'g1': jnp.ones((E, H), jnp.float32), 'be1': jnp.zeros((E, H), jnp.float32), 'm1': jnp.zeros((E, H), jnp.float32), 'v1': jnp.ones((E, H), jnp.float32), 'W2': jax.random.normal(ks[3], (E, H, H), jnp.float32) * s2, 'b2': jnp.zeros((E, H), jnp.float32), 'g2': jnp.ones((E, H), jnp.float32), 'be2': jnp.zeros((E, H), jnp.float32), 'm2': jnp.zeros((E, H), jnp.float32), 'v2': jnp.ones((E, H), jnp.float32), 'Wo': jax.random.normal(ks[4], (E, H, D), jnp.float32) * s2, 'bo': jnp.zeros((E, D), jnp.float32)}
    _L2_ffn_all = _L2_ffn_setup()
    _L2_ffn_in = {k: v for k, v in _L2_ffn_all.items() if k in ('Wr', 'br', 'W1', 'b1', 'g1', 'be1', 'm1', 'v1', 'W2', 'b2', 'g2', 'be2', 'm2', 'v2', 'Wo', 'bo')}
    del _L2_ffn_all

    def _L3_gnn_setup():
        import jax, jax.numpy as jnp
        import numpy as np
        N_NODES = 3125
        N_EDGES = 100000
        D_IN = 256
        D_OUT = 256
        key = jax.random.key(seed)
        k1, k2, k3, k4 = jax.random.split(key, 4)
        x = jax.random.normal(k1, (N_NODES, D_IN), dtype=jnp.float32)
        edge_index = jax.random.randint(k2, (2, N_EDGES), 0, N_NODES, dtype=jnp.int64)
        limit = np.sqrt(6.0 / (D_IN + D_OUT)).astype(np.float32)
        W = jax.random.uniform(k3, (D_IN, D_OUT), dtype=jnp.float32, minval=-limit, maxval=limit)
        b = jnp.zeros((D_OUT,), dtype=jnp.float32)
        return {'x': x, 'edge_index': edge_index, 'W': W, 'b': b}
    _L3_gnn_all = _L3_gnn_setup()
    _L3_gnn_in = {k: v for k, v in _L3_gnn_all.items() if k in ('W', 'b')}
    del _L3_gnn_all

    def _L3_ffn_setup():
        import jax, jax.numpy as jnp
        import numpy as np
        B, A = (128, 8)
        IN, OUT = (256, 256)
        SH1, SH2 = (256, 128)
        EH1, EH2 = (128, 64)
        E, TOPK = (4, 2)

        def _shared_mlp(x, W1, b1, W2, b2, W3, b3):
            h = jax.nn.relu(x @ W1 + b1)
            h = jax.nn.relu(h @ W2 + b2)
            return h @ W3 + b3

        def _experts_mlp(x, eW1, eb1, eW2, eb2, eW3, eb3):
            h = jax.nn.relu(jnp.einsum('baf,efh->ebah', x, eW1) + eb1[:, None, None, :])
            h = jax.nn.relu(jnp.einsum('ebah,ehg->ebag', h, eW2) + eb2[:, None, None, :])
            o = jnp.einsum('ebag,ego->ebao', h, eW3) + eb3[:, None, None, :]
            return jnp.moveaxis(o, 0, -1)
        key = jax.random.key(seed)
        ks = jax.random.split(key, 16)
        s = 0.05
        return {'x': jax.random.normal(ks[0], (B, A, IN), jnp.float32), 'sW1': jax.random.normal(ks[1], (IN, SH1), jnp.float32) * s, 'sb1': jnp.zeros((SH1,), jnp.float32), 'sW2': jax.random.normal(ks[2], (SH1, SH2), jnp.float32) * s, 'sb2': jnp.zeros((SH2,), jnp.float32), 'sW3': jax.random.normal(ks[3], (SH2, OUT), jnp.float32) * s, 'sb3': jnp.zeros((OUT,), jnp.float32), 'eW1': jax.random.normal(ks[4], (E, IN, EH1), jnp.float32) * s, 'eb1': jnp.zeros((E, EH1), jnp.float32), 'eW2': jax.random.normal(ks[5], (E, EH1, EH2), jnp.float32) * s, 'eb2': jnp.zeros((E, EH2), jnp.float32), 'eW3': jax.random.normal(ks[6], (E, EH2, OUT), jnp.float32) * s, 'eb3': jnp.zeros((E, OUT), jnp.float32), 'gW': jax.random.normal(ks[7], (IN, E), jnp.float32) * s, 'gb': jnp.zeros((E,), jnp.float32)}
    _L3_ffn_all = _L3_ffn_setup()
    _L3_ffn_in = {k: v for k, v in _L3_ffn_all.items() if k in ('sW1', 'sb1', 'sW2', 'sb2', 'sW3', 'sb3', 'eW1', 'eb1', 'eW2', 'eb2', 'eW3', 'eb3', 'gW', 'gb')}
    del _L3_ffn_all
    return {'x': x, 'src': src, 'dst': dst, 'edge_type_6': edge_type_6, 'edge_type_64': edge_type_64, 'L0_gnn_query_emb': _L0_gnn_in['query_emb'], 'L0_gnn_Wq': _L0_gnn_in['Wq'], 'L0_gnn_bq': _L0_gnn_in['bq'], 'L0_gnn_Wk': _L0_gnn_in['Wk'], 'L0_gnn_bk': _L0_gnn_in['bk'], 'L0_gnn_Wv': _L0_gnn_in['Wv'], 'L0_gnn_bv': _L0_gnn_in['bv'], 'L0_gnn_rel_w': _L0_gnn_in['rel_w'], 'L0_gnn_Wo': _L0_gnn_in['Wo'], 'L0_gnn_bo': _L0_gnn_in['bo'], 'L0_gnn_gamma': _L0_gnn_in['gamma'], 'L0_gnn_beta': _L0_gnn_in['beta'], 'L0_ffn_router_w': _L0_ffn_in['router_w'], 'L0_ffn_w1': _L0_ffn_in['w1'], 'L0_ffn_b1': _L0_ffn_in['b1'], 'L0_ffn_w2': _L0_ffn_in['w2'], 'L0_ffn_b2': _L0_ffn_in['b2'], 'L1_gnn_W': _L1_gnn_in['W'], 'L1_gnn_b': _L1_gnn_in['b'], 'L1_gnn_in_proj_w': _L1_gnn_in['in_proj_w'], 'L1_gnn_in_proj_b': _L1_gnn_in['in_proj_b'], 'L1_gnn_attn_out_w': _L1_gnn_in['attn_out_w'], 'L1_gnn_attn_out_b': _L1_gnn_in['attn_out_b'], 'L1_gnn_proj_w': _L1_gnn_in['proj_w'], 'L1_gnn_proj_b': _L1_gnn_in['proj_b'], 'L1_ffn_Wr': _L1_ffn_in['Wr'], 'L1_ffn_br': _L1_ffn_in['br'], 'L1_ffn_ln_g': _L1_ffn_in['ln_g'], 'L1_ffn_ln_b': _L1_ffn_in['ln_b'], 'L1_ffn_W1': _L1_ffn_in['W1'], 'L1_ffn_b1': _L1_ffn_in['b1'], 'L1_ffn_W2': _L1_ffn_in['W2'], 'L1_ffn_b2': _L1_ffn_in['b2'], 'L2_gnn_W': _L2_gnn_in['W'], 'L2_gnn_b': _L2_gnn_in['b'], 'L2_ffn_Wr': _L2_ffn_in['Wr'], 'L2_ffn_br': _L2_ffn_in['br'], 'L2_ffn_W1': _L2_ffn_in['W1'], 'L2_ffn_b1': _L2_ffn_in['b1'], 'L2_ffn_g1': _L2_ffn_in['g1'], 'L2_ffn_be1': _L2_ffn_in['be1'], 'L2_ffn_m1': _L2_ffn_in['m1'], 'L2_ffn_v1': _L2_ffn_in['v1'], 'L2_ffn_W2': _L2_ffn_in['W2'], 'L2_ffn_b2': _L2_ffn_in['b2'], 'L2_ffn_g2': _L2_ffn_in['g2'], 'L2_ffn_be2': _L2_ffn_in['be2'], 'L2_ffn_m2': _L2_ffn_in['m2'], 'L2_ffn_v2': _L2_ffn_in['v2'], 'L2_ffn_Wo': _L2_ffn_in['Wo'], 'L2_ffn_bo': _L2_ffn_in['bo'], 'L3_gnn_W': _L3_gnn_in['W'], 'L3_gnn_b': _L3_gnn_in['b'], 'L3_ffn_sW1': _L3_ffn_in['sW1'], 'L3_ffn_sb1': _L3_ffn_in['sb1'], 'L3_ffn_sW2': _L3_ffn_in['sW2'], 'L3_ffn_sb2': _L3_ffn_in['sb2'], 'L3_ffn_sW3': _L3_ffn_in['sW3'], 'L3_ffn_sb3': _L3_ffn_in['sb3'], 'L3_ffn_eW1': _L3_ffn_in['eW1'], 'L3_ffn_eb1': _L3_ffn_in['eb1'], 'L3_ffn_eW2': _L3_ffn_in['eW2'], 'L3_ffn_eb2': _L3_ffn_in['eb2'], 'L3_ffn_eW3': _L3_ffn_in['eW3'], 'L3_ffn_eb3': _L3_ffn_in['eb3'], 'L3_ffn_gW': _L3_ffn_in['gW'], 'L3_ffn_gb': _L3_ffn_in['gb']}

def reference(x, src, dst, edge_type_6, edge_type_64, L0_gnn_query_emb, L0_gnn_Wq, L0_gnn_bq, L0_gnn_Wk, L0_gnn_bk, L0_gnn_Wv, L0_gnn_bv, L0_gnn_rel_w, L0_gnn_Wo, L0_gnn_bo, L0_gnn_gamma, L0_gnn_beta, L0_ffn_router_w, L0_ffn_w1, L0_ffn_b1, L0_ffn_w2, L0_ffn_b2, L1_gnn_W, L1_gnn_b, L1_gnn_in_proj_w, L1_gnn_in_proj_b, L1_gnn_attn_out_w, L1_gnn_attn_out_b, L1_gnn_proj_w, L1_gnn_proj_b, L1_ffn_Wr, L1_ffn_br, L1_ffn_ln_g, L1_ffn_ln_b, L1_ffn_W1, L1_ffn_b1, L1_ffn_W2, L1_ffn_b2, L2_gnn_W, L2_gnn_b, L2_ffn_Wr, L2_ffn_br, L2_ffn_W1, L2_ffn_b1, L2_ffn_g1, L2_ffn_be1, L2_ffn_m1, L2_ffn_v1, L2_ffn_W2, L2_ffn_b2, L2_ffn_g2, L2_ffn_be2, L2_ffn_m2, L2_ffn_v2, L2_ffn_Wo, L2_ffn_bo, L3_gnn_W, L3_gnn_b, L3_ffn_sW1, L3_ffn_sb1, L3_ffn_sW2, L3_ffn_sb2, L3_ffn_sW3, L3_ffn_sb3, L3_ffn_eW1, L3_ffn_eb1, L3_ffn_eW2, L3_ffn_eb2, L3_ffn_eW3, L3_ffn_eb3, L3_ffn_gW, L3_ffn_gb):
    import jax
    import jax.numpy as jnp

    def _L0_gnn_ref(node_features, edge_index, edge_relations, query_emb, Wq, bq, Wk, bk, Wv, bv, rel_w, Wo, bo, gamma, beta):
        import jax, jax.numpy as jnp
        import numpy as np
        N_NODES = 50000
        N_EDGES = 15625
        IN_DIM = 256
        HID = 64
        HEADS = 4
        N_REL = 64
        N = node_features.shape[0]
        D = rel_w.shape[1]
        H = Wq.shape[1] // D
        enh = node_features + 0.1 * query_emb[None, :]
        Q = (enh @ Wq + bq).reshape(N, H, D)
        K = (enh @ Wk + bk).reshape(N, H, D)
        V = (enh @ Wv + bv).reshape(N, H, D)
        src, dst = (edge_index[0], edge_index[1])
        rel = rel_w[edge_relations]
        mod_k = K[src] + 0.2 * rel[:, None, :]
        scores = jnp.einsum('ehd,ehd->eh', Q[dst], mod_k) / D ** 0.5
        seg_max = jax.ops.segment_max(scores, dst, num_segments=N)
        ex = jnp.exp(scores - seg_max[dst])
        denom = jax.ops.segment_sum(ex, dst, num_segments=N)
        w = ex / denom[dst]
        agg = jax.ops.segment_sum(w[:, :, None] * V[src], dst, num_segments=N)
        deg = jax.ops.segment_sum(jnp.ones((src.shape[0],), jnp.float32), dst, num_segments=N)
        msgs = jnp.where(deg[:, None, None] > 0, agg, V)
        out = msgs.reshape(N, H * D) @ Wo + bo
        x = out + node_features
        mu = jnp.mean(x, axis=-1, keepdims=True)
        var = jnp.var(x, axis=-1, keepdims=True)
        return (x - mu) / jnp.sqrt(var + 1e-05) * gamma + beta

    def _L0_ffn_ref(input_embeddings, router_w, w1, b1, w2, b2):
        import jax, jax.numpy as jnp
        import numpy as np
        NUM_EXPERTS = 8
        TOP_K = 2
        B, S, D = (8, 256, 256)

        def _moe(tokens, router_w, w1, b1, w2, b2):
            N = tokens.shape[0]
            E = router_w.shape[0]
            logits = tokens.astype(jnp.float32) @ router_w.astype(jnp.float32).T
            probs = jax.nn.softmax(logits, axis=-1)
            rw, re = jax.lax.top_k(probs, TOP_K)
            if TOP_K > 1:
                rw = rw / jnp.maximum(rw.sum(-1, keepdims=True), 1e-12)
            rw = rw.astype(tokens.dtype)
            combine = jnp.zeros((N, E), tokens.dtype).at[jnp.arange(N)[:, None], re].set(rw)
            out = tokens
            for e in range(E):
                h = jax.nn.gelu(tokens @ w1[e] + b1[e], approximate=False)
                y = h @ w2[e] + b2[e]
                out = out + combine[:, e:e + 1] * y
            return out
        b, s, d = input_embeddings.shape
        tokens = input_embeddings.reshape(b * s, d)
        return _moe(tokens, router_w, w1, b1, w2, b2).reshape(b, s, d)

    def _L1_gnn_ref(x, edge_index, edge_types, W, b, in_proj_w, in_proj_b, attn_out_w, attn_out_b, proj_w, proj_b):
        import jax, jax.numpy as jnp
        import numpy as np
        N_NODES = 50000
        N_EDGES = 12500
        D_IN = 256
        D_OUT = 256
        N_REL = 6
        N_HEADS = 4
        num_nodes = x.shape[0]
        hd = D_OUT // N_HEADS
        transformed = jnp.einsum('ni,rio->rno', x, W) + b[:, None, :]
        src, dst = (edge_index[0], edge_index[1])
        msgs = transformed[edge_types, src]
        agg = jnp.zeros((N_REL, num_nodes, D_OUT), x.dtype).at[edge_types, dst].add(msgs)
        s = jnp.transpose(agg, (1, 0, 2))
        qkv = s @ in_proj_w.T + in_proj_b
        q, k, v = jnp.split(qkv, 3, axis=-1)
        q = q.reshape(num_nodes, N_REL, N_HEADS, hd)
        k = k.reshape(num_nodes, N_REL, N_HEADS, hd)
        v = v.reshape(num_nodes, N_REL, N_HEADS, hd)
        scores = jnp.einsum('nrhd,nshd->nhrs', q, k) / np.sqrt(hd)
        probs = jax.nn.softmax(scores, axis=-1)
        attn = jnp.einsum('nhrs,nshd->nrhd', probs, v).reshape(num_nodes, N_REL, D_OUT)
        attended = attn @ attn_out_w.T + attn_out_b
        aggregated_output = attended.mean(axis=1)
        out = (aggregated_output + x[:, :D_OUT]) @ proj_w.T + proj_b
        return out

    def _L1_ffn_ref(x, Wr, br, ln_g, ln_b, W1, b1, W2, b2):
        import jax, jax.numpy as jnp
        import numpy as np
        TOP_K = 2
        LN_EPS = 1e-05
        B, S, D = x.shape
        N = B * S
        xt = x.reshape(N, D)
        logits = xt @ Wr + br
        probs = jax.nn.softmax(logits, axis=-1)
        top_p, top_idx = jax.lax.top_k(probs, TOP_K)
        weights = top_p / top_p.sum(axis=-1, keepdims=True)
        mu = xt.mean(axis=-1, keepdims=True)
        var = ((xt - mu) ** 2).mean(axis=-1, keepdims=True)
        xn = (xt - mu) * jax.lax.rsqrt(var + LN_EPS)
        xe = xn[None, :, :] * ln_g[:, None, :] + ln_b[:, None, :]
        h = jax.nn.gelu(jnp.einsum('end,edh->enh', xe, W1) + b1[:, None, :], approximate=False)
        y = jnp.einsum('enh,ehd->end', h, W2) + b2[:, None, :]
        y_tok = jnp.transpose(y, (1, 0, 2))
        sel = jnp.take_along_axis(y_tok, top_idx[:, :, None], axis=1)
        out = (weights[:, :, None] * sel).sum(axis=1)
        return out.reshape(B, S, D)

    def _L2_gnn_ref(h, norm, W, b, src, dst):
        import jax, jax.numpy as jnp
        import numpy as np
        N_NODES = 3125
        N_EDGES = 50000
        IN_FEATS = 256
        OUT_FEATS = 256
        x = h @ W.T + b
        x = norm * x
        msg = x[src]
        agg = jax.ops.segment_sum(msg, dst, num_segments=h.shape[0])
        return agg * norm

    def _L2_ffn_ref(x, Wr, br, W1, b1, g1, be1, m1, v1, W2, b2, g2, be2, m2, v2, Wo, bo):
        import jax, jax.numpy as jnp
        import numpy as np
        BN_EPS = 0.001

        def _bn(h, g, b, m, v):
            return g * (h - m) * jax.lax.rsqrt(v + BN_EPS) + b
        feat = jnp.mean(x, axis=0)
        w = jax.nn.softmax(feat @ Wr + br, axis=-1)
        h = jnp.einsum('bfd,edh->bfeh', x, W1) + b1
        h = jax.nn.relu(_bn(h, g1, be1, m1, v1))
        h = jnp.einsum('bfeh,ehk->bfek', h, W2) + b2
        h = jax.nn.relu(_bn(h, g2, be2, m2, v2))
        y = jnp.einsum('bfeh,ehd->bfed', h, Wo) + bo
        return jnp.einsum('bfed,fe->bfd', y, w)

    def _L3_gnn_ref(x, edge_index, W, b):
        import jax, jax.numpy as jnp
        import numpy as np
        N_NODES = 3125
        N_EDGES = 100000
        D_IN = 256
        D_OUT = 256
        N = x.shape[0]
        h = x @ W
        loop = jnp.arange(N, dtype=edge_index.dtype)
        src = jnp.concatenate([edge_index[0], loop])
        dst = jnp.concatenate([edge_index[1], loop])
        deg = jax.ops.segment_sum(jnp.ones(dst.shape, dtype=h.dtype), dst, num_segments=N)
        dinv = jnp.where(deg > 0, jax.lax.rsqrt(deg), 0.0)
        norm = dinv[src] * dinv[dst]
        out = jax.ops.segment_sum(norm[:, None] * h[src], dst, num_segments=N) + b
        return jax.nn.leaky_relu(out, negative_slope=0.2)

    def _L3_ffn_ref(x, sW1, sb1, sW2, sb2, sW3, sb3, eW1, eb1, eW2, eb2, eW3, eb3, gW, gb):
        import jax, jax.numpy as jnp
        import numpy as np
        B, A = (128, 8)
        IN, OUT = (256, 256)
        SH1, SH2 = (256, 128)
        EH1, EH2 = (128, 64)
        E, TOPK = (4, 2)

        def _shared_mlp(x, W1, b1, W2, b2, W3, b3):
            h = jax.nn.relu(x @ W1 + b1)
            h = jax.nn.relu(h @ W2 + b2)
            return h @ W3 + b3

        def _experts_mlp(x, eW1, eb1, eW2, eb2, eW3, eb3):
            h = jax.nn.relu(jnp.einsum('baf,efh->ebah', x, eW1) + eb1[:, None, None, :])
            h = jax.nn.relu(jnp.einsum('ebah,ehg->ebag', h, eW2) + eb2[:, None, None, :])
            o = jnp.einsum('ebag,ego->ebao', h, eW3) + eb3[:, None, None, :]
            return jnp.moveaxis(o, 0, -1)
        all_out = _experts_mlp(x, eW1, eb1, eW2, eb2, eW3, eb3)
        shared = _shared_mlp(x, sW1, sb1, sW2, sb2, sW3, sb3)
        gates = jax.nn.softmax(x @ gW + gb, axis=-1)
        topv, topi = jax.lax.top_k(gates, TOPK)
        topw = jax.nn.softmax(topv, axis=-1)
        sel = jnp.take_along_axis(all_out, topi[:, :, None, :], axis=-1)
        gated = jnp.sum(sel * topw[:, :, None, :], axis=-1)
        return shared + gated
    edge_index = jnp.stack([src, dst])
    deg = jnp.maximum(jax.ops.segment_sum(jnp.ones(dst.shape, jnp.float32), dst, num_segments=3125), 1.0)
    deg_isqrt = deg ** (-0.5)
    x = x + _L0_gnn_ref(_layernorm(x, axis=-1), edge_index, edge_type_64, L0_gnn_query_emb, L0_gnn_Wq, L0_gnn_bq, L0_gnn_Wk, L0_gnn_bk, L0_gnn_Wv, L0_gnn_bv, L0_gnn_rel_w, L0_gnn_Wo, L0_gnn_bo, L0_gnn_gamma, L0_gnn_beta)
    x = x + _L0_ffn_ref(_layernorm(x, axis=-1)[None], L0_ffn_router_w, L0_ffn_w1, L0_ffn_b1, L0_ffn_w2, L0_ffn_b2)[0]
    x = x + _L1_gnn_ref(_layernorm(x, axis=-1), edge_index, edge_type_6, L1_gnn_W, L1_gnn_b, L1_gnn_in_proj_w, L1_gnn_in_proj_b, L1_gnn_attn_out_w, L1_gnn_attn_out_b, L1_gnn_proj_w, L1_gnn_proj_b)
    x = x + _L1_ffn_ref(_layernorm(x, axis=-1)[None], L1_ffn_Wr, L1_ffn_br, L1_ffn_ln_g, L1_ffn_ln_b, L1_ffn_W1, L1_ffn_b1, L1_ffn_W2, L1_ffn_b2)[0]
    x = x + _L2_gnn_ref(_layernorm(x, axis=-1), deg_isqrt[:, None], L2_gnn_W, L2_gnn_b, src, dst)
    x = x + _L2_ffn_ref(_layernorm(x, axis=-1)[None], L2_ffn_Wr, L2_ffn_br, L2_ffn_W1, L2_ffn_b1, L2_ffn_g1, L2_ffn_be1, L2_ffn_m1, L2_ffn_v1, L2_ffn_W2, L2_ffn_b2, L2_ffn_g2, L2_ffn_be2, L2_ffn_m2, L2_ffn_v2, L2_ffn_Wo, L2_ffn_bo)[0]
    x = x + _L3_gnn_ref(_layernorm(x, axis=-1), edge_index, L3_gnn_W, L3_gnn_b)
    x = x + _L3_ffn_ref(_layernorm(x, axis=-1)[None], L3_ffn_sW1, L3_ffn_sb1, L3_ffn_sW2, L3_ffn_sb2, L3_ffn_sW3, L3_ffn_sb3, L3_ffn_eW1, L3_ffn_eb1, L3_ffn_eW2, L3_ffn_eb2, L3_ffn_eW3, L3_ffn_eb3, L3_ffn_gW, L3_ffn_gb)[0]
    return x

_drawn_inputs = setup_inputs


def setup_inputs(seed=0):
    import zlib

    import numpy as np

    out = dict(_drawn_inputs(seed))
    spreads = {'L0_gnn_bq': (0.0, 0.8),
     'L0_gnn_bk': (0.0, 2.0),
     'L0_gnn_bv': (0.0, 0.295),
     'L0_gnn_bo': (0.0, 0.1),
     'L0_gnn_gamma': (1.0, 0.2),
     'L0_gnn_beta': (0.0, 0.1),
     'L0_ffn_b1': (0.0, 0.346),
     'L0_ffn_b2': (0.0, 0.1),
     'L1_gnn_in_proj_b': (0.0, 0.451),
     'L1_gnn_attn_out_b': (0.0, 0.349),
     'L1_ffn_br': (0.0, 0.302),
     'L1_ffn_ln_g': (1.0, 0.2),
     'L1_ffn_ln_b': (0.0, 0.442),
     'L1_ffn_b1': (0.0, 0.456),
     'L1_ffn_b2': (0.0, 0.31),
     'L2_ffn_br': (0.0, 0.8),
     'L2_ffn_b1': (0.0, 0.8),
     'L2_ffn_g1': (1.0, 0.6),
     'L2_ffn_be1': (0.0, 0.8),
     'L2_ffn_m1': (0.0, 0.8),
     'L2_ffn_v1': (1.0, 0.6),
     'L2_ffn_b2': (0.0, 0.696),
     'L2_ffn_g2': (1.0, 0.6),
     'L2_ffn_be2': (0.0, 0.738),
     'L2_ffn_m2': (0.0, 0.685),
     'L2_ffn_v2': (1.0, 0.6),
     'L2_ffn_bo': (0.0, 0.501),
     'L3_gnn_b': (0.0, 0.363),
     'L3_ffn_sb1': (0.0, 0.8),
     'L3_ffn_sb2': (0.0, 0.665),
     'L3_ffn_sb3': (0.0, 0.354),
     'L3_ffn_eb1': (0.0, 0.8),
     'L3_ffn_eb2': (0.0, 0.8),
     'L3_ffn_eb3': (0.0, 0.36),
     'L3_ffn_gb': (0.0, 0.8)}
    factors = {'L0_gnn_query_emb': 5.019,
     'L0_gnn_Wq': 8.0,
     'L0_gnn_Wk': 8.0,
     'L0_gnn_rel_w': 32.075,
     'L1_gnn_b': 6.64,
     'L1_gnn_proj_b': 3.661,
     'L2_gnn_b': 8.0,
     'L3_ffn_eW1': 4.022,
     'L3_ffn_eW2': 3.534,
     'L3_ffn_eW3': 2.83}
    for name, (base, spread) in spreads.items():
        noise = np.random.default_rng([zlib.crc32(name.encode()), seed]).standard_normal(out[name].shape)
        drawn = base * np.exp(spread * noise) if base else spread * noise
        out[name] = jnp.asarray(drawn.astype(out[name].dtype))
    for name, factor in factors.items():
        out[name] = (out[name] * factor).astype(out[name].dtype)
    return out
```

```python
from contextlib import ExitStack

import numpy as np
import concourse.bass as bass
from concourse import mybir

F32 = mybir.dt.float32
I32 = mybir.dt.int32
U32 = mybir.dt.uint32
ALU = mybir.AluOpType
ACT = mybir.ActivationFunctionType
AX = mybir.AxisListType
ds = bass.ds

N = 3125
D = 256
K2 = D // 128
P = 125
T = N // P
G = 5
GT = T // G
GN = GT * P
E = 50000
CH = 128
NQ = 4
CQ = 98
C = NQ * CQ
REAL = -(-E // CH)
HEADS = 4
HD = D // HEADS
R6 = 6
R64 = 64
WN = 20
NW = -(-N // WN)
WR = R6 * WN
VB = 4
FAR = 1000000


class Env:

    def __init__(self, nc, a, out):
        self.nc, self.a, self.out, self.phase = nc, a, out, 0

    def row(self, name):
        return self.a[name].rearrange("(o d) -> o d", o=1)


class ExpertSems:

    def __init__(self, ph):
        self.activated = ph.sem()
        self.multiplied = ph.sem()
        self.finished = ph.sem()
        self.mixed = ph.sem()
        self.hold = ph.sem()


def round_up(a, b):
    return -(-a // b) * b


VT = round_up(REAL + T - 1, 2 * VB)
VW = round_up(REAL + NW - 1, 2 * VB)
VT_PAD = VT + VB
VW_PAD = VW + VB


class Phase:

    def __init__(self, env):
        self.env = env
        self.nc = env.nc
        self.set = env.sem_sets[env.phase % 2]
        self.other = env.sem_sets[(env.phase + 1) % 2]
        self.first = env.phase == 0
        self.used = 0
        env.phase += 1

    def sem(self):
        s = self.set[self.used]
        self.used += 1
        return s

    def clear_other(self):
        if not self.first:
            lo = min(s.num for s in self.other)
            hi = max(s.num for s in self.other)
            self.nc.sync.sem_clear(range(lo, hi + 1))


def sb(env, stack, name, shape, dt=F32):
    return stack.enter_context(env.nc.sbuf_tensor(f"{name}_{env.phase}", shape, dt))


def ps(env, stack, name, shape, dt=F32):
    return stack.enter_context(env.nc.psum_tensor(f"{name}_{env.phase}", shape, dt))


def setup_phase(env, a):
    nc = env.nc
    ph = Phase(env)
    with ExitStack() as st:
        rows_i = sb(env, st, "rows_i", [CQ, 4, NQ, CH], I32)
        rows_f = sb(env, st, "rows_f", [CQ, 4, NQ, CH])
        chunk_max = sb(env, st, "chunk_max", [CQ, NQ])
        edges_t = sb(env, st, "edges_t", [CQ, 256])
        before = sb(env, st, "before", [CQ, NQ, 256])
        key = sb(env, st, "key", [128, 2])
        cmp_a = sb(env, st, "cmp_a", [128, 2, 640])
        tile_bc = sb(env, st, "tile_bc", [128, 640])
        chunk_bc = sb(env, st, "chunk_bc", [128, 640])
        chunk_id = sb(env, st, "chunk_id", [CQ, NQ])
        sel = sb(env, st, "sel", [CQ, NQ, 640])
        rel_w = sb(env, st, "rel_w", [128, 640])
        in_a = sb(env, st, "in_a", [128, 640])
        in_b = sb(env, st, "in_b", [128, 640])
        kk = sb(env, st, "kk", [128, 640])
        src_f = sb(env, st, "src_f", [128, 640])
        iota_i = sb(env, st, "iota_i", [128, 640], I32)
        part_i = sb(env, st, "part_i", [128, 1], I32)
        pc = ps(env, st, "pc", [128, 512])
        pb = ps(env, st, "pb", [128, 2, 512])
        pv = ps(env, st, "pv", [128, 2, 2, 512])
        rows_cleared, rows_landed, x_landed = ph.sem(), ph.sem(), ph.sem()
        made, step, on_pe, loaded = ph.sem(), ph.sem(), ph.sem(), ph.sem()
        names = ["dst", "src", "edge_type_6", "edge_type_64"]

        with nc.Block() as block:

            @block.sync
            def _(sp):
                sp.dma_start(env.x[:], a["x"].rearrange("(t p) d -> p t d", p=P)).then_inc(x_landed, 16)
                sp.wait_ge(rows_cleared, 2)
                for j, name in enumerate(names):
                    for q in range(NQ):
                        lo = q * CQ * CH
                        n = min(CQ, (E - lo) // CH)
                        sp.dma_start(rows_i[0:n, j, q, :], a[name][lo:lo + n * CH].rearrange(
                            "(c e) -> c e", e=CH)).then_inc(rows_landed, 16)
                    tail = E - (REAL - 1) * CH
                    r = REAL - 1 - (NQ - 1) * CQ
                    sp.dma_start(rows_i[r:r + 1, j, NQ - 1, 0:tail], a[name][E - tail:E].rearrange(
                        "(c e) -> c e", c=1)).then_inc(rows_landed, 16)
                sp.wait_ge(x_landed, 16)

            @block.gpsimd
            def _(pool):
                pool.memset(rows_i[:, 0, NQ - 1, :], FAR).then_inc(rows_cleared, 1)
                pool.memset(rows_i[:, 1:4, NQ - 1, :], 0).then_inc(rows_cleared, 1)
                pool.iota(iota_i[:], [[1, 640]], base=0, channel_multiplier=0).then_inc(made, 1)
                pool.iota(part_i[:], [[0, 1]], base=0, channel_multiplier=1).then_inc(made, 1)
                pool.memset(env.ones[:], 1.0).then_inc(made, 1)
                pool.memset(env.ident[:], 0.0).then_inc(made, 1)
                pool.wait_ge(made, 4)
                pool.affine_select(out=env.ident[:], in_=env.ident[:], compare_op=ALU.not_equal, fill=1.0,
                                   base=0, pattern=[[-1, 128]], channel_multiplier=1).then_inc(made, 1)

            @block.vector
            def _(v):
                n = [0]

                def done(ins):
                    n[0] += 1
                    ins.then_inc(step, 1)
                    v.wait_ge(step, n[0])

                v.wait_ge(made, 5)
                done(v.tensor_copy(env.iota[:], iota_i[:]))
                done(v.tensor_copy(env.part[:], part_i[:]))
                for q in range(NQ):
                    done(v.tensor_scalar(chunk_id[:, q:q + 1], env.part[0:CQ, :], float(q * CQ), None, ALU.add))
                v.wait_ge(rows_landed, 16 * 4 * (NQ + 1))
                done(v.tensor_copy(rows_f[:], rows_i[:]))
                done(v.tensor_reduce(chunk_max[:], rows_f[:, 0], AX.X, ALU.max))
                pe = [0]

                def after_pe():
                    pe[0] += 1
                    v.wait_ge(on_pe, pe[0])

                for width, count, visits in ((P, T, VT_PAD), (WN, NW, VW_PAD)):
                    half = visits // 2
                    done(v.tensor_scalar(edges_t[:, 0:count], env.iota[0:CQ, 0:count], float(width), None, ALU.mult))
                    for q in range(NQ):
                        done(v.tensor_scalar(before[:, q, 0:count], edges_t[:, 0:count],
                                             chunk_max[:, q:q + 1], None, ALU.is_gt))
                    sets = [(w0, min(128, count - w0)) for w0 in range(0, count, 128)]
                    after_pe()
                    for j, (w0, m) in enumerate(sets):
                        done(v.tensor_scalar(key[0:m, j:j + 1], pc[0:m, j:j + 1], env.part[0:m, :], float(w0),
                                             ALU.add, ALU.add))
                        done(v.tensor_scalar(cmp_a[0:m, j, 0:visits], env.iota[0:m, 0:visits],
                                             key[0:m, j:j + 1], None, ALU.is_ge))
                    after_pe()
                    for h in range(2):
                        done(v.tensor_scalar(tile_bc[:, h * half:(h + 1) * half], pb[:, h, 0:half], -1.0, None, ALU.add))
                    done(v.tensor_tensor(chunk_bc[:, 0:visits], env.iota[:, 0:visits], tile_bc[:, 0:visits], ALU.subtract))
                    for q in range(NQ):
                        done(v.tensor_scalar(sel[:, q, 0:visits], chunk_bc[0:CQ, 0:visits],
                                             chunk_id[:, q:q + 1], None, ALU.is_equal))
                    tiles = env.tile_of_visit if width == P else env.window_of_visit
                    done(v.tensor_copy(tiles[0:1, 0:visits], tile_bc[0:1, 0:visits]))
                    after_pe()
                    for h in range(2):
                        s = slice(h * half, (h + 1) * half)
                        rel = env.rel_dst if width == P else rel_w
                        done(v.scalar_tensor_tensor(out=rel[:, s], in0=tile_bc[:, s], scalar=float(-width),
                                                    in1=pv[:, 0, h, 0:half], op0=ALU.mult, op1=ALU.add))
                        if width == P:
                            done(v.tensor_copy(env.src_of_visit[:, s], pv[:, 1, h, 0:half]))
                        else:
                            done(v.tensor_copy(src_f[:, s], pv[:, 1, h, 0:half]))
                    after_pe()
                    for h in range(2):
                        s = slice(h * half, (h + 1) * half)
                        if width == P:
                            done(v.tensor_copy(env.type64[:, s], pv[:, 0, h, 0:half]))
                        else:
                            done(v.tensor_scalar(in_a[:, s], rel_w[:, s], 0.0, None, ALU.is_ge))
                            done(v.scalar_tensor_tensor(out=in_b[:, s], in0=rel_w[:, s], scalar=float(WN),
                                                        in1=in_a[:, s], op0=ALU.is_lt, op1=ALU.mult))
                            done(v.scalar_tensor_tensor(out=kk[:, s], in0=pv[:, 0, h, 0:half], scalar=float(WN),
                                                        in1=rel_w[:, s], op0=ALU.mult, op1=ALU.add))
                            done(v.scalar_tensor_tensor(out=in_a[:, s], in0=kk[:, s], scalar=1.0,
                                                        in1=in_b[:, s], op0=ALU.add, op1=ALU.mult))
                            done(v.tensor_scalar(env.row_of_edge[:, s], in_a[:, s], -1.0, None, ALU.add))
                            done(v.scalar_tensor_tensor(out=kk[:, s], in0=src_f[:, s], scalar=float(R6),
                                                        in1=pv[:, 0, h, 0:half], op0=ALU.mult, op1=ALU.add))
                            done(v.tensor_copy(env.message_of_visit[:, s], kk[:, s]))

            @block.tensor
            def _(pe):
                n = 2 + NQ + 2
                for width, count, visits in ((P, T, VT_PAD), (WN, NW, VW_PAD)):
                    half = visits // 2
                    sets = [(w0, min(128, count - w0)) for w0 in range(0, count, 128)]
                    n += 1 + NQ
                    pe.wait_ge(step, n)
                    for j, (w0, m) in enumerate(sets):
                        for q in range(NQ):
                            mm = pe.matmul(pc[0:m, j:j + 1], before[:, q, w0:w0 + m], env.ones[0:CQ, 0:1],
                                           start=q == 0, stop=q == NQ - 1)
                    mm.then_inc(on_pe, 1)
                    n += 2 * len(sets)
                    pe.wait_ge(step, n)
                    for h in range(2):
                        for j, (w0, m) in enumerate(sets):
                            mm = pe.matmul(pb[:, h, 0:half], env.ones[0:m, :], cmp_a[0:m, j, h * half:(h + 1) * half],
                                           start=j == 0, stop=j == len(sets) - 1)
                    mm.then_inc(on_pe, 1)
                    n += 2 + 1 + NQ
                    pe.wait_ge(step, n)
                    for k, j in enumerate((0, 1)):
                        for h in range(2):
                            for q in range(NQ):
                                mm = pe.matmul(pv[:, k, h, 0:half], rows_f[:, j, q, :], sel[:, q, h * half:(h + 1) * half],
                                               start=q == 0, stop=q == NQ - 1)
                    mm.then_inc(on_pe, 1)
                    n += 1 + 4
                    pe.wait_ge(step, n)
                    j = 3 if width == P else 2
                    for h in range(2):
                        for q in range(NQ):
                            mm = pe.matmul(pv[:, 0, h, 0:half], rows_f[:, j, q, :], sel[:, q, h * half:(h + 1) * half],
                                           start=q == 0, stop=q == NQ - 1)
                    mm.then_inc(on_pe, 1)
                    n += 2 if width == P else 14


def stats_phase(env, x, mean=None, rstd=None):
    nc = env.nc
    mean, rstd = mean or env.mean, rstd or env.rstd
    ph = Phase(env)
    with ExitStack() as st:
        moments = sb(env, st, "moments", [P, T, 6])
        mv = sb(env, st, "mv", [P, T, 2])
        std = sb(env, st, "std", [P, T])
        eps = sb(env, st, "eps", [P, 1])
        summed, whole, rooted, step = ph.sem(), ph.sem(), ph.sem(), ph.sem()
        with nc.Block() as block:

            @block.sync
            def _(sp):
                ph.clear_other()

            @block.gpsimd
            def _(pool):
                pool.memset(eps[:], 1e-5).then_inc(whole, 1)

            @block.vector
            def _(v):
                with v.Fori(0, T) as t:
                    v.bn_stats(moments[:, ds(t, 1), :], x[:, ds(t, 1), :]).then_inc(summed, 1)
                v.wait_ge(summed, T)
                for t in range(T):
                    v.bn_aggr(mv[:, t, :], moments[:, t, :]).then_inc(step, 1)
                v.wait_ge(step, T)
                v.tensor_copy(mean[:], mv[:, :, 0:1].rearrange("p t o -> p (t o)")).then_inc(whole, 1)
                v.wait_ge(rooted, 1)
                v.reciprocal(rstd[:], std[:]).then_inc(step, 1)

            @block.scalar
            def _(act):
                act.wait_ge(whole, 2)
                act.activation(std[:], mv[:, :, 1:2].rearrange("p t o -> p (t o)"), ACT.Sqrt,
                               bias=eps[:]).then_inc(rooted, 1)


def norm_phase(env):
    ph = Phase(env)
    step = ph.sem()
    with env.nc.Block() as block:

        @block.sync
        def _(sp):
            ph.clear_other()

        @block.vector
        def _(v):
            v.tensor_tensor(env.normed[:], env.x[:], env.mean[:].unsqueeze(2).to_broadcast([P, T, D]),
                            ALU.subtract).then_inc(step, 1)
            v.wait_ge(step, 1)
            v.tensor_tensor(env.normed[:], env.normed[:], env.rstd[:].unsqueeze(2).to_broadcast([P, T, D]),
                            ALU.mult).then_inc(step, 1)


def project_phase(env, w, bias, cols, kind, out_table=None):
    nc = env.nc
    ph = Phase(env)
    banks = -(-cols // 512)
    with ExitStack() as st:
        w_sb = sb(env, st, "w_sb", [128, K2, cols])
        bias_bc = sb(env, st, "bias_bc", [P, cols])
        normed = sb(env, st, "normed", [P, GT, D])
        x_t = sb(env, st, "x_t", [128, GT, K2, P])
        rows = sb(env, st, "rows", [P, GT, cols])
        query = sb(env, st, "query", [128, K2])
        query_s = sb(env, st, "query_s", [128, K2])
        turned = ps(env, st, "turned", [128, 2, K2 * 256])
        prod = ps(env, st, "prod", [128, 2, banks, 512])
        w_landed, query_scaled = ph.sem(), ph.sem()
        normed_ready, transposed, x_t_ready, multiplied = ph.sem(), ph.sem(), ph.sem(), ph.sem()
        added, rows_ready, stored = ph.sem(), ph.sem(), ph.sem()
        loads = 1 + (bias is not None) + (kind == "qkv")
        stores = 2 if kind == "qkv" else 1
        with nc.Block() as block:

            @block.sync
            def _(sp):
                ph.clear_other()
                sp.dma_start(w_sb[:], w).then_inc(w_landed, 16)
                if bias is not None:
                    sp.dma_start(bias_bc[:], bias).then_inc(w_landed, 16)
                if kind == "qkv":
                    sp.dma_start(query[:], env.a["L0_gnn_query_emb"]).then_inc(w_landed, 16)
                sp.sem_inc(stored, 1)
                with sp.Fori(0, G) as g:
                    for i in range(GT):
                        sp.wait_ge(rows_ready, g * GT + i + 1)
                        r = ds((g * GT + i) * P, P)
                        if kind == "qkv":
                            sp.dma_start(env.k_table[r, :], rows[:, i, D:2 * D]).then_inc(stored, 16)
                            sp.dma_start(env.v_table[r, :], rows[:, i, 2 * D:3 * D]).then_inc(stored, 16)
                        else:
                            sp.dma_start(out_table[r, :], rows[:, i, :]).then_inc(stored, 16)
                sp.wait_ge(stored, 16 * stores * T + 1)

            @block.vector
            def _(v):
                v.wait_ge(w_landed, 16 * loads)
                if kind == "qkv":
                    v.tensor_scalar(query_s[:], query[:], 0.1, None, ALU.mult).then_inc(query_scaled, 1)
                v.sem_inc(added, 2)
                with v.Fori(0, G) as g:
                    for i in range(GT):
                        t = g * GT + i
                        v.wait_ge(transposed, t + 1)
                        v.tensor_scalar(normed[:, i, :], env.x[:, ds(t, 1), :].rearrange("p o d -> p (o d)"),
                                        env.mean[:, ds(t, 1)], env.rstd[:, ds(t, 1)], ALU.subtract,
                                        ALU.mult).then_inc(normed_ready, 1)
                    v.wait_ge(stored, g * (16 * stores * GT) + 1)
                    for i in range(GT):
                        t = g * GT + i
                        v.wait_ge(multiplied, t + 1 + GT)
                        for b in range(banks):
                            s = slice(b * 512, min(cols, b * 512 + 512))
                            here = prod[0:P, i % 2, b, 0:s.stop - s.start]
                            if bias is None:
                                ins = v.tensor_copy(rows[:, i, s], here)
                            else:
                                ins = v.tensor_tensor(rows[:, i, s], here, bias_bc[:, s], ALU.add)
                        ins.then_inc(added, 1)
                        v.wait_ge(added, t + 1 + 2)
                        if kind == "qkv":
                            v.tensor_copy(env.q[:, ds(t, 1), :].rearrange("p o d -> p (o d)"),
                                          rows[:, i, 0:D]).then_inc(rows_ready, 1)
                        elif kind == "scaled":
                            v.tensor_scalar(rows[:, i, :], rows[:, i, :], env.scale[:, ds(t, 1)], None,
                                            ALU.mult).then_inc(rows_ready, 1)
                        else:
                            v.sem_inc(rows_ready, 1)

            @block.tensor
            def _(pe):
                pe.sem_inc(transposed, GT)
                pe.sem_inc(multiplied, GT)
                pe.wait_ge(w_landed, 16 * loads)
                with pe.Fori(0, G) as g:
                    for i in range(GT):
                        t = g * GT + i
                        pe.wait_ge(normed_ready, t + 1)
                        pe.wait_ge(x_t_ready, t + (1 + (i == 0)))
                        for k in range(K2):
                            mm = pe.transpose(turned[:, i % 2, k * P:(k + 1) * P],
                                              normed[:, i, k * 128:(k + 1) * 128], env.ident[0:P, 0:P])
                        mm.then_inc(transposed, 1)
                    for i in range(GT):
                        t = g * GT + i
                        pe.wait_ge(x_t_ready, t + 1 + 2)
                        pe.wait_ge(added, t + (1 + (i == 0)))
                        for b in range(banks):
                            s = slice(b * 512, min(cols, b * 512 + 512))
                            for k in range(K2):
                                mm = pe.matmul(prod[0:P, i % 2, b, 0:s.stop - s.start], x_t[:, i, k, :],
                                               w_sb[:, k, s], start=k == 0, stop=k == K2 - 1)
                        mm.then_inc(multiplied, 1)

            @block.scalar
            def _(act):
                act.sem_inc(x_t_ready, 2)
                if kind == "qkv":
                    act.wait_ge(query_scaled, 1)
                with act.Fori(0, G) as g:
                    for i in range(GT):
                        t = g * GT + i
                        act.wait_ge(multiplied, t + 1)
                        act.wait_ge(transposed, t + 1 + GT)
                        if kind == "qkv":
                            for k in range(K2):
                                ins = act.activation(x_t[:, i, k, :], turned[:, i % 2, k * P:(k + 1) * P],
                                                     ACT.Identity, bias=query_s[:, k:k + 1])
                            ins.then_inc(x_t_ready, 1)
                        else:
                            act.activation(x_t[:, i].rearrange("p k n -> p (k n)"), turned[:, i % 2, 0:K2 * P],
                                           ACT.Copy).then_inc(x_t_ready, 1)


def score_phase(env):
    nc = env.nc
    ph = Phase(env)
    with ExitStack() as st:
        rel_raw = sb(env, st, "rel_raw", [R64, HD])
        rel4 = sb(env, st, "rel4", [R64, D])
        index = sb(env, st, "index", [128, 2, VB], I32)
        k_rows = sb(env, st, "k_rows", [128, 2, VB, D])
        hit = sb(env, st, "hit", [128, 2, VB, 128])
        hit_type = sb(env, st, "hit_type", [128, 2, VB, R64])
        hit_t = sb(env, st, "hit_t", [128, 2, VB * 128])
        type_t = sb(env, st, "type_t", [R64, 2, VB * 128])
        terms = sb(env, st, "terms", [128, VB, D])
        ps_hit = ps(env, st, "ps_hit", [128, VB * 128])
        ps_type = ps(env, st, "ps_type", [128, VB * 128])
        q_rows = sb(env, st, "q_rows", [128, VB, D])
        ps_q = ps(env, st, "ps_q", [128, VB, D])
        ps_k = ps(env, st, "ps_k", [128, VB, D])
        rel_landed, rel_scaled = ph.sem(), ph.sem()
        indexed = ph.sem()
        gathered, base = env.gathered, env.gathered_base
        hits_made, turned, turned_copied, multiplied, termed, scored = [ph.sem() for _ in range(6)]
        q_copied, hold = ph.sem(), ph.sem()
        batches = VT // VB
        with nc.Block() as block:

            @block.sync
            def _(sp):
                ph.clear_other()
                sp.dma_start(rel_raw[:], env.a["L0_gnn_rel_w"]).then_inc(rel_landed, 16)

            @block.gpsimd
            def _(pool):
                with pool.Fori(0, batches // 2) as it:
                    for b in range(2):
                        pool.wait_ge(multiplied, it * 2 + b + 1)
                        pool.sem_inc(hold, 1)
                        pool.tensor_copy(index[:, b, :], env.src_of_visit[:, ds((it * 2 + b) * VB, VB)]).then_inc(indexed, 1)
                        pool.wait_ge(indexed, it * 2 + b + 1)
                        pool.sem_inc(hold, 1)
                        for i in range(VB):
                            pool.indirect_dma_start(k_rows[:, b, i, :], None, env.k_table,
                                                    bass.IndirectOffsetOnAxis(index[:, b, i:i + 1], 0)).then_inc(gathered[b], 16)

            @block.vector
            def _(v):
                v.wait_ge(rel_landed, 16)
                v.tensor_scalar(rel4[:].rearrange("p (h d) -> p h d", h=HEADS),
                                rel_raw[:].unsqueeze(1).to_broadcast([R64, HEADS, HD]), 0.2, None,
                                ALU.mult).then_inc(rel_scaled, 1)
                v.sem_inc(termed, 1)

                def hits(b, k):
                    visits = ds(k * VB, VB)
                    v.tensor_tensor(hit[:, b], env.iota[:, 0:128].unsqueeze(1).to_broadcast([128, VB, 128]),
                                    env.rel_dst[:, visits].unsqueeze(2).to_broadcast([128, VB, 128]), ALU.is_equal)
                    v.tensor_tensor(hit_type[:, b], env.iota[:, 0:R64].unsqueeze(1).to_broadcast([128, VB, R64]),
                                    env.type64[:, visits].unsqueeze(2).to_broadcast([128, VB, R64]),
                                    ALU.is_equal).then_inc(hits_made, 1)

                hits(0, 0)
                with v.Fori(0, batches // 2) as it:
                    for b in range(2):
                        k = it * 2 + b
                        v.wait_ge(turned, k + 1)
                        hits(1 - b, k + 1)
                        v.wait_ge(multiplied, k + 1 + 2)
                        v.wait_ge(q_copied, k + 1)
                        v.wait_ge(scored, k + 1)
                        v.tensor_tensor(terms[:], q_rows[:], ps_k[:], ALU.mult).then_inc(termed, 1)
                        v.wait_ge(termed, k + 1 + 1)
                        v.tensor_reduce(env.scores[:, ds(k * VB, VB), :], terms[:].rearrange("p v (h d) -> p v h d", h=HEADS),
                                        AX.X, ALU.add).then_inc(scored, 1)

            @block.tensor
            def _(pe):
                pe.sem_inc(multiplied, 2)
                pe.wait_ge(rel_scaled, 1)

                def turn(b, k):
                    pe.wait_ge(hits_made, k + 1)
                    pe.wait_ge(turned_copied, k + 1)
                    for i in range(VB):
                        pe.transpose(ps_hit[:, i * 128:(i + 1) * 128], hit[:, b, i, :], env.ident[:])
                        mm = pe.transpose(ps_type[0:R64, i * 128:(i + 1) * 128], hit_type[:, b, i, :], env.ident[:])
                    mm.then_inc(turned, 1)

                turn(0, 0)
                with pe.Fori(0, batches // 2) as it:
                    for b in range(2):
                        k = it * 2 + b
                        turn(1 - b, k + 1)
                        pe.wait_ge(turned_copied, k + 1 + 1)
                        pe.wait_ge(termed, k + 1)
                        pe.wait_ge(gathered[b], (it + 1) * (16 * VB) + base)
                        for i in range(VB):
                            tile = pe.value_load(env.tile_of_visit[0:1, ds(k * VB + i, 1)], min_val=0, max_val=T - 1)
                            pe.matmul(ps_q[:, i, :], hit_t[0:P, b, i * 128:(i + 1) * 128],
                                      env.q[:, ds(tile, 1), :].rearrange("p o d -> p (o d)"), start=True, stop=True)
                            pe.matmul(ps_k[:, i, :], type_t[:, b, i * 128:(i + 1) * 128], rel4[:], start=True, stop=False)
                            mm = pe.matmul(ps_k[:, i, :], env.ident[:], k_rows[:, b, i, :], start=False, stop=True)
                        mm.then_inc(multiplied, 1)

            @block.scalar
            def _(act):
                act.sem_inc(scored, 1)
                act.sem_inc(turned_copied, 1)

                def copy(b, k):
                    act.wait_ge(multiplied, k + 1)
                    act.wait_ge(turned, k + 1)
                    act.activation(hit_t[:, b], ps_hit[:], ACT.Copy)
                    act.activation(type_t[:, b], ps_type[0:R64, :], ACT.Copy).then_inc(turned_copied, 1)

                copy(0, 0)
                with act.Fori(0, batches // 2) as it:
                    for b in range(2):
                        k = it * 2 + b
                        copy(1 - b, k + 1)
                        act.wait_ge(termed, k + 1)
                        act.wait_ge(multiplied, k + 1 + 2)
                        act.activation(q_rows[:], ps_q[:], ACT.Copy).then_inc(q_copied, 1)
        env.gathered_base += 16 * VB * (batches // 2)


def peak_phase(env):
    nc = env.nc
    ph = Phase(env)
    with ExitStack() as st:
        low = sb(env, st, "low", [128, HEADS])
        low_h = sb(env, st, "low_h", [HEADS, 1])
        low_diag = sb(env, st, "low_diag", [HEADS, HEADS])
        low_bc = sb(env, st, "low_bc", [128, HEADS])
        hit = sb(env, st, "hit", [128, 2, VB, 128])
        masked = sb(env, st, "masked", [128, 2, VB * HEADS, 128])
        peak = sb(env, st, "peak", [P, VB * HEADS])
        ps_low = ps(env, st, "ps_low", [128, 512])
        ps_masked = ps(env, st, "ps_masked", [128, VB, 512])
        step, low_turned, hits_made, masked_made, turned, reduced, merged, zeroed, hold = [ph.sem() for _ in range(9)]
        batches = VT // VB
        with nc.Block() as block:

            @block.sync
            def _(sp):
                ph.clear_other()

            @block.gpsimd
            def _(pool):
                pool.memset(env.peaks[:], 0.0).then_inc(zeroed, 1)
                pool.wait_ge(step, 5)
                with pool.Fori(0, batches // 2) as it:
                    for b in range(2):
                        k = it * 2 + b
                        pool.wait_ge(hits_made, k + 1)
                        pool.wait_ge(turned, k + 1)
                        pool.sem_inc(hold, 1)
                        pool.tensor_tensor(masked[:, b].rearrange("p (v h) n -> p v h n", v=VB),
                                           hit[:, b].unsqueeze(2).to_broadcast([128, VB, HEADS, 128]),
                                           env.scores[:, ds(k * VB, VB), :].unsqueeze(3).to_broadcast([128, VB, HEADS, 128]),
                                           ALU.mult).then_inc(masked_made, 1)

            @block.vector
            def _(v):
                v.tensor_reduce(low[:], env.scores[:, 0:VT, :].rearrange("p v h -> p h v"), AX.X,
                                ALU.min).then_inc(step, 1)
                v.wait_ge(low_turned, 1)
                v.tensor_reduce(low_h[:], ps_low[0:HEADS, 0:128], AX.X, ALU.min).then_inc(step, 1)
                v.wait_ge(step, 2)
                v.tensor_scalar(low_diag[:], env.ident[0:HEADS, 0:HEADS], low_h[:], None, ALU.mult).then_inc(step, 1)
                v.wait_ge(low_turned, 2)
                v.tensor_copy(low_bc[:], ps_low[:, 128:128 + HEADS]).then_inc(step, 1)
                v.wait_ge(step, 4)
                v.tensor_tensor(env.scores[:, 0:VT, :], env.scores[:, 0:VT, :],
                                low_bc[:].unsqueeze(1).to_broadcast([128, VT, HEADS]), ALU.subtract).then_inc(step, 1)

                def hits(b, k):
                    v.tensor_tensor(hit[:, b], env.iota[:, 0:128].unsqueeze(1).to_broadcast([128, VB, 128]),
                                    env.rel_dst[:, ds(k * VB, VB)].unsqueeze(2).to_broadcast([128, VB, 128]),
                                    ALU.is_equal).then_inc(hits_made, 1)

                hits(0, 0)
                v.wait_ge(zeroed, 1)
                v.sem_inc(reduced, 1)
                v.sem_inc(merged, 1)
                with v.Fori(0, batches // 2) as it:
                    for b in range(2):
                        k = it * 2 + b
                        v.wait_ge(masked_made, k + 1)
                        hits(1 - b, k + 1)
                        v.wait_ge(turned, k + 1 + 2)
                        v.wait_ge(merged, k * VB + 1)
                        v.tensor_reduce(peak[:], ps_masked[0:P].rearrange("p v (h e) -> p (v h) e", h=HEADS),
                                        AX.X, ALU.max).then_inc(reduced, 1)
                        v.wait_ge(reduced, k + 1 + 1)
                        for i in range(VB):
                            tile = v.value_load(env.tile_of_visit[0:1, ds(k * VB + i, 1)], min_val=0, max_val=T - 1)
                            here = env.peaks[:, ds(tile, 1), :].rearrange("p o h -> p (o h)")
                            v.tensor_tensor(here, here, peak[:, i * HEADS:(i + 1) * HEADS], ALU.max).then_inc(merged, 1)
                            if i < VB - 1:
                                v.wait_ge(merged, k * VB + i + 1 + 1)

            @block.tensor
            def _(pe):
                pe.sem_inc(turned, 2)
                pe.wait_ge(step, 1)
                pe.transpose(ps_low[0:HEADS, 0:128], low[:], env.ident[:]).then_inc(low_turned, 1)
                pe.wait_ge(step, 3)
                pe.matmul(ps_low[:, 128:128 + HEADS], env.ones[0:HEADS, :], low_diag[:], start=True,
                          stop=True).then_inc(low_turned, 1)
                with pe.Fori(0, batches // 2) as it:
                    for b in range(2):
                        k = it * 2 + b
                        pe.wait_ge(masked_made, k + 1)
                        pe.wait_ge(reduced, k + 1)
                        for i in range(VB * HEADS):
                            mm = pe.transpose(ps_masked[:, i // HEADS, (i % HEADS) * 128:(i % HEADS + 1) * 128],
                                              masked[:, b, i, :], env.ident[:])
                        mm.then_inc(turned, 1)


VC = D + HEADS + 1


def attend_phase(env):
    nc = env.nc
    ph = Phase(env)
    with ExitStack() as st:
        index = sb(env, st, "index", [128, 2, VB], I32)
        v_rows = sb(env, st, "v_rows", [128, 2, VB, D])
        hit = sb(env, st, "hit", [128, 2, VB, 128])
        hit_t = sb(env, st, "hit_t", [128, 2, VB * 128])
        below = sb(env, st, "below", [128, 2, VB, HEADS])
        weight = sb(env, st, "weight", [128, 2, VB, HEADS])
        summand = sb(env, st, "summand", [128, 2, VB, VC])
        ps_hit = ps(env, st, "ps_hit", [128, VB * 128])
        ps_peak = ps(env, st, "ps_peak", [128, VB, HEADS])
        ps_sum = ps(env, st, "ps_sum", [128, VB, 512])
        indexed = ph.sem()
        gathered, base = env.gathered, env.gathered_base
        cleared, hits_made, turned, turned_copied, peaks_out, lowered, clipped, weighed = [ph.sem() for _ in range(8)]
        summand_made, multiplied, summed, hold = [ph.sem() for _ in range(4)]
        batches = VT // VB
        with nc.Block() as block:

            @block.sync
            def _(sp):
                ph.clear_other()

            @block.gpsimd
            def _(pool):
                pool.memset(env.sums[:], 0.0).then_inc(cleared, 1)
                pool.memset(summand[:], 1.0).then_inc(cleared, 1)
                with pool.Fori(0, batches // 2) as it:
                    for b in range(2):
                        pool.wait_ge(summand_made, it * 2 + b + 1)
                        pool.sem_inc(hold, 1)
                        pool.tensor_copy(index[:, b, :], env.src_of_visit[:, ds((it * 2 + b) * VB, VB)]).then_inc(indexed, 1)
                        pool.wait_ge(indexed, it * 2 + b + 1)
                        pool.sem_inc(hold, 1)
                        for i in range(VB):
                            pool.indirect_dma_start(v_rows[:, b, i, :], None, env.v_table,
                                                    bass.IndirectOffsetOnAxis(index[:, b, i:i + 1], 0)).then_inc(gathered[b], 16)

            @block.vector
            def _(v):
                def hits(b, k):
                    v.tensor_tensor(hit[:, b], env.iota[:, 0:128].unsqueeze(1).to_broadcast([128, VB, 128]),
                                    env.rel_dst[:, ds(k * VB, VB)].unsqueeze(2).to_broadcast([128, VB, 128]),
                                    ALU.is_equal).then_inc(hits_made, 1)

                v.wait_ge(cleared, 2)
                v.sem_inc(summand_made, 2)
                v.sem_inc(summed, 1)
                hits(0, 0)
                with v.Fori(0, batches // 2) as it:
                    for b in range(2):
                        k = it * 2 + b
                        v.wait_ge(peaks_out, k + 1)
                        v.wait_ge(weighed, k + 1)
                        v.tensor_tensor(below[:, b], env.scores[:, ds(k * VB, VB), :], ps_peak[:],
                                        ALU.subtract).then_inc(lowered, 1)
                        v.wait_ge(lowered, k + 1)
                        v.tensor_scalar(below[:, b], below[:, b], 0.0, None, ALU.min).then_inc(clipped, 1)
                        v.wait_ge(multiplied, k + 1)
                        hits(1 - b, k + 1)
                        v.wait_ge(gathered[b], (it + 1) * (16 * VB) + base)
                        v.wait_ge(weighed, k + 1 + 2)
                        v.tensor_tensor(summand[:, b, :, 0:D].rearrange("p v (h d) -> p v h d", h=HEADS),
                                        v_rows[:, b].rearrange("p v (h d) -> p v h d", h=HEADS),
                                        weight[:, b].unsqueeze(3).to_broadcast([128, VB, HEADS, HD]), ALU.mult)
                        v.tensor_copy(summand[:, b, :, D:D + HEADS], weight[:, b]).then_inc(summand_made, 1)
                        v.wait_ge(multiplied, k + 1 + 1)
                        for i in range(VB):
                            tile = v.value_load(env.tile_of_visit[0:1, ds(k * VB + i, 1)], min_val=0, max_val=T - 1)
                            v.wait_ge(summed, k * VB + i + 1)
                            here = env.sums[:, ds(tile, 1), :].rearrange("p o c -> p (o c)")
                            v.tensor_tensor(here, here, ps_sum[0:P, i, 0:VC], ALU.add).then_inc(summed, 1)

            @block.tensor
            def _(pe):
                pe.sem_inc(multiplied, 1)

                def turn(b, k):
                    pe.wait_ge(hits_made, k + 1)
                    pe.wait_ge(turned_copied, k + 1)
                    for i in range(VB):
                        mm = pe.transpose(ps_hit[:, i * 128:(i + 1) * 128], hit[:, b, i, :], env.ident[:])
                    mm.then_inc(turned, 1)

                def peaks(b, k):
                    pe.wait_ge(turned_copied, k + 1 + 1)
                    pe.wait_ge(lowered, k) if not isinstance(k, int) else None
                    for i in range(VB):
                        tile = pe.value_load(env.tile_of_visit[0:1, ds(k * VB + i, 1)], min_val=0, max_val=T - 1)
                        mm = pe.matmul(ps_peak[:, i, :], hit_t[0:P, b, i * 128:(i + 1) * 128],
                                       env.peaks[:, ds(tile, 1), :].rearrange("p o h -> p (o h)"), start=True, stop=True)
                    mm.then_inc(peaks_out, 1)

                turn(0, 0)
                peaks(0, 0)
                with pe.Fori(0, batches // 2) as it:
                    for b in range(2):
                        k = it * 2 + b
                        turn(1 - b, k + 1)
                        peaks(1 - b, k + 1)
                        pe.wait_ge(summand_made, k + 1 + 2)
                        pe.wait_ge(summed, k * VB + 1)
                        for i in range(VB):
                            mm = pe.matmul(ps_sum[0:P, i, 0:VC], hit[:, b, i, 0:P], summand[:, b, i, :], start=True, stop=True)
                        mm.then_inc(multiplied, 1)

            @block.scalar
            def _(act):
                act.sem_inc(turned_copied, 1)
                act.sem_inc(weighed, 2)

                def copy(b, k):
                    act.wait_ge(peaks_out, k) if not isinstance(k, int) else None
                    act.wait_ge(turned, k + 1)
                    act.activation(hit_t[:, b], ps_hit[:], ACT.Copy).then_inc(turned_copied, 1)

                copy(0, 0)
                with act.Fori(0, batches // 2) as it:
                    for b in range(2):
                        k = it * 2 + b
                        copy(1 - b, k + 1)
                        act.wait_ge(clipped, k + 1)
                        act.wait_ge(summand_made, k + 1)
                        act.activation(weight[:, b], below[:, b], ACT.Exp, scale=HD ** -0.5).then_inc(weighed, 1)
        env.gathered_base += 16 * VB * (batches // 2)


def message_phase(env):
    nc = env.nc
    ph = Phase(env)
    with ExitStack() as st:
        w_sb = sb(env, st, "w_sb", [128, K2, D])
        bias_bc = sb(env, st, "bias_bc", [P, D])
        rden = sb(env, st, "rden", [P, T, HEADS])
        alone = sb(env, st, "alone", [P, T])
        degree = sb(env, st, "degree", [P, 2, T])
        root = sb(env, st, "root", [P, 2, T])
        v_own = sb(env, st, "v_own", [P, T, D])
        msg = sb(env, st, "msg", [P, GT, D])
        msg_t = sb(env, st, "msg_t", [128, GT, K2 * P])
        turned_ps = ps(env, st, "turned_ps", [128, 2, 512])
        prod = ps(env, st, "prod", [128, 2, 512])
        w_landed, step, rooted, scaled, msg_ready = [ph.sem() for _ in range(5)]
        transposed, copied, multiplied, added, own = [ph.sem() for _ in range(5)]
        with nc.Block() as block:

            @block.sync
            def _(sp):
                ph.clear_other()
                sp.dma_start(w_sb[:], env.a["L0_gnn_Wo"].rearrange("(k p) n -> p k n", p=128)).then_inc(w_landed, 16)
                sp.dma_start(bias_bc[:], env.row("L0_gnn_bo").to_broadcast([P, D])).then_inc(w_landed, 16)
                sp.dma_start(v_own[:], env.v_table.rearrange("(t p) d -> p t d", p=P)).then_inc(w_landed, 16)

            @block.vector
            def _(v):
                deg = env.sums[:, :, D + HEADS:D + HEADS + 1].rearrange("p t o -> p (t o)")
                v.tensor_scalar(rden[:], env.sums[:, :, D:D + HEADS], 1e-30, None, ALU.max).then_inc(step, 1)
                v.tensor_scalar(alone[:], deg, 0.5, None, ALU.is_lt).then_inc(step, 1)
                v.tensor_scalar(degree[:, 0, :], deg, 1.0, None, ALU.max).then_inc(step, 1)
                v.tensor_scalar(degree[:, 1, :], deg, 1.0, None, ALU.add).then_inc(step, 1)
                v.wait_ge(step, 4)
                v.reciprocal(rden[:], rden[:]).then_inc(step, 1)
                v.wait_ge(rooted, 1)
                v.reciprocal(env.norm2[:], root[:, 0, :]).then_inc(step, 1)
                v.reciprocal(env.norm3[:], root[:, 1, :]).then_inc(step, 1)
                v.wait_ge(step, 7)
                v.wait_ge(w_landed, 48)
                v.sem_inc(added, 2)
                with v.Fori(0, G) as g:
                    for i in range(GT):
                        t = g * GT + i
                        v.wait_ge(transposed, t + 1)
                        v.tensor_tensor(msg[:, i, :].rearrange("p (h d) -> p h d", h=HEADS),
                                        env.sums[:, ds(t, 1), 0:D].rearrange("p o (h d) -> p (o h) d", h=HEADS),
                                        rden[:, ds(t, 1), :].rearrange("p o h -> p (o h)").unsqueeze(2).to_broadcast([P, HEADS, HD]),
                                        ALU.mult).then_inc(scaled, 1)
                        v.wait_ge(scaled, t + 1)
                        v.scalar_tensor_tensor(out=msg[:, i, :], in0=v_own[:, ds(t, 1), :].rearrange("p o d -> p (o d)"),
                                               scalar=alone[:, ds(t, 1)], in1=msg[:, i, :], op0=ALU.mult,
                                               op1=ALU.add).then_inc(msg_ready, 1)
                    for i in range(GT):
                        t = g * GT + i
                        here = env.sums[:, ds(t, 1), 0:D].rearrange("p o d -> p (o d)")
                        own_t = v_own[:, ds(t, 1), :].rearrange("p o d -> p (o d)")
                        v.tensor_scalar(own_t, env.x[:, ds(t, 1), :].rearrange("p o d -> p (o d)"),
                                        env.mean[:, ds(t, 1)], env.rstd[:, ds(t, 1)], ALU.subtract,
                                        ALU.mult).then_inc(own, 1)
                        v.wait_ge(own, 2 * t + 1)
                        v.tensor_tensor(own_t, own_t, bias_bc[:], ALU.add).then_inc(own, 1)
                        v.wait_ge(own, 2 * t + 2)
                        v.wait_ge(multiplied, t + 1 + GT)
                        v.tensor_tensor(here, prod[0:P, i % 2, 0:D], own_t, ALU.add).then_inc(added, 1)

            @block.tensor
            def _(pe):
                pe.sem_inc(transposed, GT)
                pe.sem_inc(multiplied, GT)
                pe.wait_ge(w_landed, 48)
                with pe.Fori(0, G) as g:
                    for i in range(GT):
                        t = g * GT + i
                        pe.wait_ge(msg_ready, t + 1)
                        pe.wait_ge(copied, t + (1 + (i == 0)))
                        for k in range(K2):
                            mm = pe.transpose(turned_ps[:, i % 2, k * P:(k + 1) * P],
                                              msg[:, i, k * 128:(k + 1) * 128], env.ident[0:P, 0:P])
                        mm.then_inc(transposed, 1)
                    for i in range(GT):
                        t = g * GT + i
                        pe.wait_ge(copied, t + 1 + 2)
                        pe.wait_ge(added, t + (1 + (i == 0)))
                        for k in range(K2):
                            mm = pe.matmul(prod[0:P, i % 2, 0:D], msg_t[:, i, k * P:(k + 1) * P], w_sb[:, k, :],
                                           start=k == 0, stop=k == K2 - 1)
                        mm.then_inc(multiplied, 1)

            @block.scalar
            def _(act):
                act.sem_inc(copied, 2)
                act.wait_ge(step, 4)
                act.activation(root[:], degree[:], ACT.Sqrt).then_inc(rooted, 1)
                with act.Fori(0, G) as g:
                    for i in range(GT):
                        t = g * GT + i
                        act.wait_ge(multiplied, t + 1)
                        act.wait_ge(transposed, t + 1 + GT)
                        act.activation(msg_t[:, i, :], turned_ps[:, i % 2, 0:K2 * P], ACT.Copy).then_inc(copied, 1)


def affine_phase(env):
    nc = env.nc
    ph = Phase(env)
    with ExitStack() as st:
        gamma = sb(env, st, "gamma", [P, D])
        beta = sb(env, st, "beta", [P, D])
        landed, step = ph.sem(), ph.sem()
        with nc.Block() as block:

            @block.sync
            def _(sp):
                ph.clear_other()
                sp.dma_start(gamma[:], env.row("L0_gnn_gamma").to_broadcast([P, D])).then_inc(landed, 16)
                sp.dma_start(beta[:], env.row("L0_gnn_beta").to_broadcast([P, D])).then_inc(landed, 16)

            @block.vector
            def _(v):
                v.wait_ge(landed, 32)
                y = env.sums[:, :, 0:D]

                def over(col):
                    return col[:].unsqueeze(2).to_broadcast([P, T, D])

                def along(row):
                    return row[:].unsqueeze(1).to_broadcast([P, T, D])

                v.tensor_tensor(y, y, over(env.mean), ALU.subtract).then_inc(step, 1)
                v.wait_ge(step, 1)
                v.tensor_tensor(y, y, over(env.rstd), ALU.mult).then_inc(step, 1)
                v.wait_ge(step, 2)
                v.tensor_tensor(y, y, along(gamma), ALU.mult).then_inc(step, 1)
                v.wait_ge(step, 3)
                v.tensor_tensor(y, y, along(beta), ALU.add).then_inc(step, 1)
                v.wait_ge(step, 4)
                v.tensor_tensor(env.x[:], env.x[:], y, ALU.add).then_inc(step, 1)


def store_phase(env):
    nc = env.nc
    ph = Phase(env)
    stored = ph.sem()
    with nc.Block() as block:

        @block.sync
        def _(sp):
            ph.clear_other()
            sp.dma_start(env.out.rearrange("(t p) d -> p t d", p=P), env.x[:]).then_inc(stored, 16)
            sp.wait_ge(stored, 16)


def router_phase(env, kind):
    nc = env.nc
    ph = Phase(env)
    ne = {"L0": 8, "L1": 8, "L2": 8, "L3": 4}[kind]
    twice = kind == "L1"
    w = env.a[{"L0": "L0_ffn_router_w", "L1": "L1_ffn_Wr", "L2": "L2_ffn_Wr", "L3": "L3_ffn_gW"}[kind]]
    b = {"L0": None, "L1": "L1_ffn_br", "L2": "L2_ffn_br", "L3": "L3_ffn_gb"}[kind]
    last_bias = env.a[{"L0": "L0_ffn_b2", "L1": "L1_ffn_b2", "L2": "L2_ffn_bo", "L3": "L3_ffn_eb3"}[kind]]
    shared_bias = "L3_ffn_sb3" if kind == "L3" else None
    with ExitStack() as st:
        w_sb = sb(env, st, "w_sb", [128, K2, ne])
        bias_bc = sb(env, st, "bias_bc", [P, ne])
        last_sb = sb(env, st, "last_sb", [ne, D])
        shared_bc = sb(env, st, "shared_bc", [P, D])
        normed = sb(env, st, "normed", [P, GT, D])
        again = sb(env, st, "again", [P, GT, D]) if twice else None
        a_t = sb(env, st, "a_t", [128, GT, K2 * P])
        logits = sb(env, st, "logits", [P, T, ne])
        probs = sb(env, st, "probs", [P, T, ne])
        one_a = sb(env, st, "one_a", [P, T, ne])
        one_b = sb(env, st, "one_b", [P, T, ne])
        rank = sb(env, st, "rank", [P, ne])
        top = sb(env, st, "top", [P, T])
        top2 = sb(env, st, "top2", [P, T])
        share = sb(env, st, "share", [P, T])
        pick = sb(env, st, "pick", [P, T])
        gate_s = sb(env, st, "gate_s", [P, GT, ne])
        gate_t = sb(env, st, "gate_t", [ne, GT, P])
        turned_ps = ps(env, st, "turned_ps", [128, 2, 512])
        again_ps = ps(env, st, "again_ps", [128, 2, 512])
        logit_ps = ps(env, st, "logit_ps", [128, 2, 512])
        landed, normed_ready, transposed, copied, kept, multiplied, added, own_added = [ph.sem() for _ in range(8)]
        step, exped, gated, gate_ready, gate_turned, gate_copied, biased, bias_added, hold = [ph.sem() for _ in range(9)]
        loads = 2 + (b is not None) + (shared_bias is not None)
        with nc.Block() as block:

            @block.sync
            def _(sp):
                ph.clear_other()
                sp.dma_start(w_sb[:], w.rearrange("(k p) e -> p k e", p=128)).then_inc(landed, 16)
                sp.dma_start(last_sb[:], last_bias).then_inc(landed, 16)
                if b is not None:
                    sp.dma_start(bias_bc[:], env.row(b).to_broadcast([P, ne])).then_inc(landed, 16)
                if shared_bias is not None:
                    sp.dma_start(shared_bc[:], env.row(shared_bias).to_broadcast([P, D])).then_inc(landed, 16)

            @block.vector
            def _(v):
                v.wait_ge(landed, 16 * loads)
                v.sem_inc(added, 2)
                with v.Fori(0, G) as g:
                    for i in range(GT):
                        t = g * GT + i
                        x_t = env.x[:, ds(t, 1), :].rearrange("p o d -> p (o d)")
                        v.wait_ge(transposed, t + 1)
                        v.tensor_scalar(normed[:, i, :], x_t, env.mean[:, ds(t, 1)], env.rstd[:, ds(t, 1)],
                                        ALU.subtract, ALU.mult).then_inc(normed_ready, 1)
                        if twice:
                            v.wait_ge(normed_ready, 2 * t + 1)
                            v.tensor_scalar(again[:, i, :], normed[:, i, :], env.mean2[:, ds(t, 1)],
                                            env.rstd2[:, ds(t, 1)], ALU.subtract, ALU.mult).then_inc(normed_ready, 1)
                        if kind == "L0":
                            v.wait_ge(normed_ready, t + 1)
                            v.tensor_tensor(x_t, x_t, normed[:, i, :], ALU.add).then_inc(own_added, 1)
                        if kind == "L3":
                            v.wait_ge(normed_ready, t + 1)
                            v.tensor_tensor(x_t, x_t, shared_bc[:], ALU.add).then_inc(own_added, 1)
                    for i in range(GT):
                        t = g * GT + i
                        v.wait_ge(multiplied, t + 1 + GT)
                        here = logits[:, ds(t, 1), :].rearrange("p o e -> p (o e)")
                        if b is None:
                            v.tensor_copy(here, logit_ps[0:P, i % 2, 0:ne]).then_inc(added, 1)
                        else:
                            v.tensor_tensor(here, logit_ps[0:P, i % 2, 0:ne], bias_bc[:], ALU.add).then_inc(added, 1)
                n = [0]

                def done(ins):
                    n[0] += 1
                    ins.then_inc(step, 1)
                    v.wait_ge(step, n[0])

                def wide(col):
                    return col[:].unsqueeze(2).to_broadcast([P, T, ne])

                v.wait_ge(added, 2 + T)
                done(v.tensor_reduce(top[:], logits[:], AX.X, ALU.max))
                done(v.tensor_tensor(logits[:], logits[:], wide(top), ALU.subtract))
                v.wait_ge(exped, 1)
                done(v.tensor_reduce(share[:], probs[:], AX.X, ALU.add))
                done(v.reciprocal(share[:], share[:]))
                if kind == "L2":
                    done(v.tensor_tensor(env.gates[:, :, 0:ne], probs[:], wide(share), ALU.mult))
                else:
                    done(v.tensor_tensor(probs[:], probs[:], wide(share), ALU.mult))
                    done(v.tensor_scalar(rank[:], env.iota[0:P, 0:ne], -1.0, float(ne), ALU.mult, ALU.add))

                    def first_largest(values, best, one):
                        done(v.tensor_reduce(best[:], values[:], AX.X, ALU.max))
                        done(v.tensor_tensor(one[:], values[:], wide(best), ALU.is_equal))
                        done(v.tensor_tensor(one[:], one[:], rank[:].unsqueeze(1).to_broadcast([P, T, ne]), ALU.mult))
                        done(v.tensor_reduce(pick[:], one[:], AX.X, ALU.max))
                        done(v.tensor_tensor(one[:], one[:], wide(pick), ALU.is_equal))

                    first_largest(probs, top, one_a)
                    done(v.scalar_tensor_tensor(out=probs[:], in0=one_a[:], scalar=-2.0, in1=probs[:], op0=ALU.mult,
                                                op1=ALU.add))
                    first_largest(probs, top2, one_b)
                    if kind == "L3":
                        done(v.tensor_tensor(top2[:], top2[:], top[:], ALU.subtract))
                        v.wait_ge(exped, 2)
                        done(v.memset(top[:], 1.0))
                    done(v.tensor_tensor(share[:], top[:], top2[:], ALU.add))
                    if kind == "L0":
                        done(v.tensor_scalar(share[:], share[:], 1e-12, None, ALU.max))
                    done(v.reciprocal(share[:], share[:]))
                    done(v.tensor_tensor(top[:], top[:], share[:], ALU.mult))
                    done(v.tensor_tensor(top2[:], top2[:], share[:], ALU.mult))
                    done(v.tensor_tensor(one_a[:], one_a[:], wide(top), ALU.mult))
                    done(v.tensor_tensor(one_b[:], one_b[:], wide(top2), ALU.mult))
                    done(v.tensor_tensor(env.gates[:, :, 0:ne], one_a[:], one_b[:], ALU.add))
                v.sem_inc(bias_added, 2)
                with v.Fori(0, G) as g:
                    for i in range(GT):
                        t = g * GT + i
                        v.wait_ge(gate_turned, t + 1)
                        v.tensor_copy(gate_s[:, i, :], env.gates[:, ds(t, 1), 0:ne].rearrange("p o e -> p (o e)")).then_inc(gate_ready, 1)
                    for i in range(GT):
                        t = g * GT + i
                        x_t = env.x[:, ds(t, 1), :].rearrange("p o d -> p (o d)")
                        v.wait_ge(biased, t + 1)
                        v.tensor_tensor(x_t, logit_ps[0:P, i % 2, 0:D], x_t, ALU.add).then_inc(bias_added, 1)

            @block.tensor
            def _(pe):
                pe.sem_inc(transposed, GT)
                pe.sem_inc(multiplied, GT)
                pe.sem_inc(gate_turned, GT)
                pe.wait_ge(landed, 16 * loads)
                with pe.Fori(0, G) as g:
                    for i in range(GT):
                        t = g * GT + i
                        pe.wait_ge(normed_ready, (2 * t + 2) if twice else t + 1)
                        pe.wait_ge(kept, t + (1 + (i == 0)))
                        for k in range(K2):
                            if twice:
                                pe.transpose(again_ps[:, i % 2, k * P:(k + 1) * P],
                                             again[:, i, k * 128:(k + 1) * 128], env.ident[0:P, 0:P])
                            mm = pe.transpose(turned_ps[:, i % 2, k * P:(k + 1) * P],
                                              normed[:, i, k * 128:(k + 1) * 128], env.ident[0:P, 0:P])
                        mm.then_inc(transposed, 1)
                    for i in range(GT):
                        t = g * GT + i
                        pe.wait_ge(copied, t + 1)
                        pe.wait_ge(added, t + (1 + (i == 0)))
                        for k in range(K2):
                            mm = pe.matmul(logit_ps[0:P, i % 2, 0:ne], a_t[:, i, k * P:(k + 1) * P], w_sb[:, k, :],
                                           start=k == 0, stop=k == K2 - 1)
                        mm.then_inc(multiplied, 1)
                pe.wait_ge(added, 2 + T)
                pe.wait_ge(kept, 2 + T)
                with pe.Fori(0, G) as g:
                    for i in range(GT):
                        t = g * GT + i
                        pe.wait_ge(gate_ready, t + 1)
                        pe.wait_ge(gate_copied, t + (1 + (i == 0)))
                        pe.transpose(turned_ps[0:ne, i % 2, 0:P], gate_s[:, i, :], env.ident[0:P, 0:P]).then_inc(gate_turned, 1)
                    for i in range(GT):
                        t = g * GT + i
                        pe.wait_ge(gate_copied, t + 1 + 2)
                        pe.wait_ge(bias_added, t + (1 + (i == 0)))
                        pe.matmul(logit_ps[0:P, i % 2, 0:D], gate_t[:, i, :], last_sb[:], start=True,
                                  stop=True).then_inc(biased, 1)

            @block.scalar
            def _(act):
                act.sem_inc(kept, 2)
                with act.Fori(0, G) as g:
                    for i in range(GT):
                        t = g * GT + i
                        act.wait_ge(multiplied, t + 1)
                        act.wait_ge(transposed, t + 1 + GT)
                        act.activation(a_t[:, i, :], turned_ps[:, i % 2, 0:K2 * P], ACT.Copy).then_inc(copied, 1)
                        src = again_ps if twice else turned_ps
                        act.activation(env.x_t[:, :, ds(t * P, P)], src[:, i % 2, 0:K2 * P].rearrange("p (k n) -> p k n", k=K2),
                                       ACT.Copy).then_inc(kept, 1)
                act.wait_ge(step, 2)
                act.activation(probs[:], logits[:], ACT.Exp).then_inc(exped, 1)
                if kind == "L3":
                    act.wait_ge(step, 18)
                    act.activation(top2[:], top2[:], ACT.Exp).then_inc(exped, 1)
                act.sem_inc(gate_copied, 2)
                with act.Fori(0, G) as g:
                    for i in range(GT):
                        t = g * GT + i
                        if i == 0:
                            act.wait_ge(bias_added, g * GT + 1)
                        act.wait_ge(gate_turned, t + 1 + GT)
                        act.activation(gate_t[:, i, :], turned_ps[0:ne, i % 2, 0:P], ACT.Copy).then_inc(gate_copied, 1)


PIECES = ((0, 320), (320, GN - 320))


def hidden_pieces(layers):
    return sum(-(-l["out"] // 128) for l in layers) * len(PIECES)


class Expert:

    def __init__(self, env, layers, w_last, k_last, ring, s):
        self.env, self.layers, self.w_last, self.k_last, self.ring, self.s = env, layers, w_last, k_last, ring, s
        self.pieces = hidden_pieces(layers)

    def tensor(self, pe, x_cols, first, tiles, hidden_ps, out_ps, offset=0):
        s, j, before = self.s, 0, 0
        for n, layer in enumerate(self.layers):
            for c, (lo, size) in enumerate(PIECES):
                for m in range(-(-layer["out"] // 128)):
                    rows = min(128, layer["out"] - m * 128)
                    pe.wait_ge(s.activated, first + (j + 1))
                    if n and m == 0:
                        pe.wait_ge(s.activated, first + (before + (c + 1) * (before_per) + self.ring))
                    kc = -(-layer["in"] // 128)
                    for k in range(kc):
                        kr = min(128, layer["in"] - k * 128)
                        rhs = x_cols(k, lo, size) if n == 0 else self.layers[n - 1]["h"][0:kr, k, lo:lo + size]
                        mm = pe.matmul(hidden_ps[0:rows, (offset + j) % self.ring, 0:size],
                                       layer["w"][0:kr, k, m * 128:m * 128 + rows], rhs, start=k == 0, stop=k == kc - 1)
                    mm.then_inc(s.multiplied, 1)
                    j += 1
            before_per = -(-layer["out"] // 128)
            before = j - before_per * len(PIECES)
        last = self.layers[-1]
        for i in range(GT):
            if i == 0:
                pe.wait_ge(s.activated, first + (before + before_per + self.ring))
            if i == 2:
                pe.wait_ge(s.activated, first + (before + 2 * before_per + self.ring))
            gap = {0: 1, 4: 4}.get(i, 5)
            pe.wait_ge(s.mixed, tiles + (i + 1 - gap + 5))
            kc = -(-last["out"] // 128)
            for k in range(kc):
                kr = min(128, last["out"] - k * 128)
                mm = pe.matmul(out_ps[0:P, i % 4, 0:D], last["h"][0:kr, k, i * P:(i + 1) * P],
                               self.w_last[0:kr, k, :], start=k == 0, stop=k == kc - 1)
            mm.then_inc(s.finished, 1)

    def scalar(self, act, column, first, hidden_ps, offset=0):
        s, j = self.s, 0
        for n, layer in enumerate(self.layers):
            for c, (lo, size) in enumerate(PIECES):
                for m in range(-(-layer["out"] // 128)):
                    rows = min(128, layer["out"] - m * 128)
                    act.wait_ge(s.multiplied, first + (j + 1))
                    act.sem_inc(s.hold, 1)
                    scale = layer["scale"](column, m, rows) if layer.get("scale") else 1.0
                    act.activation(layer["h"][0:rows, m, lo:lo + size], hidden_ps[0:rows, (offset + j) % self.ring, 0:size],
                                   layer["func"], bias=layer["bias"](column, m, rows), scale=scale).then_inc(s.activated, 1)
                    j += 1

    def vector(self, v, gate, tiles, g, out_ps):
        for i in range(GT):
            t = g * GT + i
            x_t = self.env.x[:, ds(t, 1), :].rearrange("p o d -> p (o d)")
            v.wait_ge(self.s.finished, tiles + (i + 1))
            v.scalar_tensor_tensor(out=x_t, in0=out_ps[0:P, i % 4, 0:D], scalar=gate(t), in1=x_t, op0=ALU.mult,
                                   op1=ALU.add).then_inc(self.s.mixed, 1)


def experts_phase(env, kind):
    nc = env.nc
    ph = Phase(env)
    a = env.a
    ne = 8
    hidden = 1024 if kind == "L1" else D
    hc = hidden // 128
    n_hidden = 2 if kind == "L2" else 1
    ring = 4
    with ExitStack() as st:
        names = {"L0": ["L0_ffn_w1", "L0_ffn_w2"], "L1": ["L1_ffn_W1", "L1_ffn_W2"],
                 "L2": ["L2_ffn_W1", "L2_ffn_W2", "L2_ffn_Wo"]}[kind]
        w_slots = []
        for s in range(2):
            ws = [sb(env, st, f"w{s}_0", [128, K2, hidden])]
            if n_hidden == 2:
                ws.append(sb(env, st, f"w{s}_1", [128, hc, hidden]))
            ws.append(sb(env, st, f"w{s}_last", [128, hc, D]))
            w_slots.append(ws)
        hs = [sb(env, st, f"h{n}", [128, hc, GN]) for n in range(n_hidden)]
        cols = ne * hc
        if kind == "L2":
            raw = {p: sb(env, st, f"raw_{p}", [128, cols]) for p in ("b1", "g1", "be1", "m1", "v1", "b2", "g2", "be2", "m2", "v2")}
            eps = sb(env, st, "eps", [128, 1])
        else:
            raw = {"b1": sb(env, st, "raw_b1", [128, cols])}
        if kind == "L1":
            raw["ln_g"] = sb(env, st, "raw_ln_g", [128, ne * K2])
            raw["ln_b"] = sb(env, st, "raw_ln_b", [128, ne * K2])
            x_e = sb(env, st, "x_e", [128, K2, GN])
        hidden_ps = ps(env, st, "hidden_ps", [128, ring, 512])
        out_ps = ps(env, st, "out_ps", [128, 4, 512])
        sems = ExpertSems(ph)
        w_landed = [ph.sem(), ph.sem()]
        params_landed, rooted, folded, shifted, pe_hold = [ph.sem() for _ in range(5)]
        func = ACT.Relu if kind == "L2" else ACT.Gelu

        def column(which):
            return lambda e, m, rows: raw[which][:, ds(e * hc + m, 1)]

        experts = []
        for s in range(2):
            layers = []
            for n in range(n_hidden):
                layers.append({"in": D, "out": hidden, "w": w_slots[s][n], "h": hs[n], "func": func,
                               "bias": column(f"b{n + 1}"), "scale": column(f"g{n + 1}") if kind == "L2" else None})
            experts.append(Expert(env, layers, w_slots[s][-1], hc, ring, sems))
        pieces = experts[0].pieces
        with nc.Block() as block:

            @block.sync
            def _(sp):
                ph.clear_other()
                for p, tile in raw.items():
                    sp.dma_start(tile[:], a[f"{kind}_ffn_{p}"]).then_inc(params_landed, 16)
                with sp.Fori(0, ne // 2) as pair:
                    for s in range(2):
                        e = pair * 2 + s
                        sp.wait_ge(sems.finished, (e + 1) * (G * GT))
                        for n, name in enumerate(names):
                            sp.dma_start(w_slots[s][n][:], a[name][ds(e, 1), :, :].rearrange("o (k p) n -> p (o k) n", p=128)).then_inc(w_landed[s], 16)
                sp.wait_ge(w_landed[0], 16 * len(names) * (ne // 2))
                sp.wait_ge(w_landed[1], 16 * len(names) * (ne // 2))

            @block.tensor
            def _(pe):
                pe.sem_inc(sems.finished, 2 * G * GT)
                with pe.Fori(0, ne // 2) as pair:
                    for s in range(2):
                        pe.wait_ge(w_landed[s], (pair + 1) * (16 * len(names)))
                        pe.sem_inc(pe_hold, 1)
                        with pe.Fori(0, G) as g:
                            unit = pair * (2 * G) + (s * G + g)
                            if kind == "L1":
                                pe.wait_ge(shifted, unit + 1)

                                def x_cols(k, lo, size):
                                    return x_e[:, k, lo:lo + size]
                            else:
                                def x_cols(k, lo, size):
                                    return env.x_t[:, k, ds(g * GN + lo, size)]
                            experts[s].tensor(pe, x_cols, unit * pieces, unit * GT, hidden_ps, out_ps)

            @block.scalar
            def _(act):
                act.wait_ge(params_landed, 16 * len(raw))
                act.sem_inc(sems.activated, ring)
                if kind == "L2":
                    act.wait_ge(folded, 1)
                    act.activation(raw["v1"][:], raw["v1"][:], ACT.Sqrt, bias=eps[:]).then_inc(rooted, 1)
                    act.activation(raw["v2"][:], raw["v2"][:], ACT.Sqrt, bias=eps[:]).then_inc(rooted, 1)
                    act.wait_ge(folded, 11)
                with act.Fori(0, ne // 2) as pair:
                    for s in range(2):
                        with act.Fori(0, G) as g:
                            unit = pair * (2 * G) + (s * G + g)
                            e = pair * 2 + s
                            if kind == "L1":
                                for k in range(K2):
                                    ins = act.activation(x_e[:, k, :], env.x_t[:, k, ds(g * GN, GN)], ACT.Identity,
                                                         bias=raw["ln_b"][:, ds(e * K2 + k, 1)],
                                                         scale=raw["ln_g"][:, ds(e * K2 + k, 1)])
                                ins.then_inc(shifted, 1)
                            experts[s].scalar(act, e, unit * pieces, hidden_ps)

            @block.vector
            def _(v):
                v.sem_inc(sems.mixed, 5)
                if kind == "L2":
                    v.memset(eps[:], 1e-3).then_inc(folded, 1)
                    v.wait_ge(rooted, 2)
                    n = 1
                    for j in "12":
                        for ins in (lambda: v.reciprocal(raw["v" + j][:], raw["v" + j][:]),
                                    lambda: v.tensor_tensor(raw["g" + j][:], raw["g" + j][:], raw["v" + j][:], ALU.mult),
                                    lambda: v.tensor_tensor(raw["b" + j][:], raw["b" + j][:], raw["m" + j][:], ALU.subtract),
                                    lambda: v.tensor_tensor(raw["b" + j][:], raw["b" + j][:], raw["g" + j][:], ALU.mult),
                                    lambda: v.tensor_tensor(raw["b" + j][:], raw["b" + j][:], raw["be" + j][:], ALU.add)):
                            ins().then_inc(folded, 1)
                            n += 1
                            v.wait_ge(folded, n)
                with v.Fori(0, ne // 2) as pair:
                    for s in range(2):
                        with v.Fori(0, G) as g:
                            unit = pair * (2 * G) + (s * G + g)
                            e = pair * 2 + s
                            experts[s].vector(v, lambda t: env.gates[:, ds(t, 1), ds(e, 1)].rearrange("p o e -> p (o e)"),
                                              unit * GT + 2 * G * GT, g, out_ps)


def gather_sum_phase(env, table, index_of_visit, key_of_edge, tile_of_visit, tiles, sums, rows, visits):
    nc = env.nc
    ph = Phase(env)
    batches = visits // VB
    with ExitStack() as st:
        index = sb(env, st, "index", [128, 2, VB], I32)
        gathered_rows = sb(env, st, "gathered_rows", [128, 2, VB, D])
        hit = sb(env, st, "hit", [128, 2, VB, 128])
        sum_ps = ps(env, st, "sum_ps", [128, 2, VB, D])
        indexed, cleared, hits_made, multiplied, summed, hold = [ph.sem() for _ in range(6)]
        gathered, base = env.gathered, env.gathered_base
        with nc.Block() as block:

            @block.sync
            def _(sp):
                ph.clear_other()

            @block.gpsimd
            def _(pool):
                pool.memset(sums[:], 0.0).then_inc(cleared, 1)
                with pool.Fori(0, batches // 2) as it:
                    for b in range(2):
                        pool.wait_ge(multiplied, it * 2 + b + 1)
                        pool.sem_inc(hold, 1)
                        pool.tensor_copy(index[:, b, :], index_of_visit[:, ds((it * 2 + b) * VB, VB)]).then_inc(indexed, 1)
                        pool.wait_ge(indexed, it * 2 + b + 1)
                        pool.sem_inc(hold, 1)
                        for i in range(VB):
                            pool.indirect_dma_start(gathered_rows[:, b, i, :], None, table,
                                                    bass.IndirectOffsetOnAxis(index[:, b, i:i + 1], 0)).then_inc(gathered[b], 16)

            @block.vector
            def _(v):
                def hits(b, k):
                    v.tensor_tensor(hit[:, b], env.iota[:, 0:128].unsqueeze(1).to_broadcast([128, VB, 128]),
                                    key_of_edge[:, ds(k * VB, VB)].unsqueeze(2).to_broadcast([128, VB, 128]),
                                    ALU.is_equal).then_inc(hits_made, 1)

                v.wait_ge(cleared, 1)
                v.sem_inc(summed, 2 * VB)
                hits(0, 0)
                with v.Fori(0, batches // 2) as it:
                    for b in range(2):
                        k = it * 2 + b
                        v.wait_ge(multiplied, k + 1 + 1)
                        hits(1 - b, k + 1)
                        v.wait_ge(multiplied, k + 1 + 2)
                        for i in range(VB):
                            tile = v.value_load(tile_of_visit[0:1, ds(k * VB + i, 1)], min_val=0, max_val=tiles - 1)
                            v.wait_ge(summed, k * VB + (i + 2 * VB))
                            here = sums[:, ds(tile, 1), :].rearrange("p o c -> p (o c)")
                            v.tensor_tensor(here, here, sum_ps[0:rows, b, i, :], ALU.add).then_inc(summed, 1)

            @block.tensor
            def _(pe):
                pe.sem_inc(multiplied, 2)
                with pe.Fori(0, batches // 2) as it:
                    for b in range(2):
                        k = it * 2 + b
                        pe.wait_ge(hits_made, k + 1)
                        pe.wait_ge(summed, k * VB + VB)
                        pe.wait_ge(gathered[b], (it + 1) * (16 * VB) + base)
                        for i in range(VB):
                            mm = pe.matmul(sum_ps[0:rows, b, i, :], hit[:, b, i, 0:rows], gathered_rows[:, b, i, :],
                                           start=True, stop=True)
                        mm.then_inc(multiplied, 1)
        env.gathered_base += 16 * VB * (batches // 2)


def move_phase(env, to_dram):
    ph = Phase(env)
    moved = ph.sem()
    with env.nc.Block() as block:

        @block.sync
        def _(sp):
            ph.clear_other()
            rows = env.x_table.rearrange("(t p) d -> p t d", p=P)
            if to_dram:
                sp.dma_start(rows, env.x[:]).then_inc(moved, 16)
            else:
                sp.dma_start(env.x[:], rows).then_inc(moved, 16)
            sp.wait_ge(moved, 16)


WB = 2
NWP = round_up(NW, 2 * WB)


def relation_attention_phase(env):
    nc = env.nc
    ph = Phase(env)
    a = env.a
    M = WB * WR
    batches = NWP // WB
    with ExitStack() as st:
        w_sb = sb(env, st, "w_sb", [128, K2, 3 * D])
        bias_col = sb(env, st, "bias_col", [128, 3 * D // 128])
        v_bias = sb(env, st, "v_bias", [WR, D])
        other = sb(env, st, "other", [WR, WR])
        share = sb(env, st, "share", [WR, WN])
        s_rows = sb(env, st, "s_rows", [WR, WB, D])
        s_t = sb(env, st, "s_t", [128, K2, M])
        qk_t = sb(env, st, "qk_t", [128, 4, M])
        v_sb = sb(env, st, "v_sb", [WR, 2, WB, D])
        score = sb(env, st, "score", [WR, WB * HEADS, WR])
        top = sb(env, st, "top", [WR, WB * HEADS])
        total = sb(env, st, "total", [WR, WB * HEADS])
        chooser = sb(env, st, "chooser", [WR, WB * HEADS, WN])
        weight = sb(env, st, "weight", [WR, WB * HEADS * WN])
        o_rows = sb(env, st, "o_rows", [WN, WB, D])
        turn_ps = ps(env, st, "turn_ps", [128, 512])
        qk_ps = ps(env, st, "qk_ps", [128, 2, 512])
        v_ps = ps(env, st, "v_ps", [128, 512])
        score_ps = ps(env, st, "score_ps", [128, WB, 512])
        weight_ps = ps(env, st, "weight_ps", [128, 512])
        o_ps = ps(env, st, "o_ps", [128, 512])
        landed, taken, turned, turned_copied, projected, qk_out, v_out = [ph.sem() for _ in range(7)]
        scored, masked, topped, lowered, exped, summed, inverted, chosen = [ph.sem() for _ in range(8)]
        weighed, weights_out, attended, o_out, stored, hold = [ph.sem() for _ in range(6)]
        with nc.Block() as block:

            @block.sync
            def _(sp):
                ph.clear_other()
                sp.dma_start(w_sb[:], a["L1_gnn_in_proj_w"].rearrange("(k p) n -> p k n", p=128)).then_inc(landed, 16)
                sp.dma_start(bias_col[:], a["L1_gnn_in_proj_b"]).then_inc(landed, 16)
                sp.dma_start(v_bias[:], env.row("in_proj_b_row")[:, 2 * D:3 * D].to_broadcast([WR, D])).then_inc(landed, 16)
                sp.dma_start(other[:], a["other_node"]).then_inc(landed, 16)
                sp.dma_start(share[:], a["node_share"]).then_inc(landed, 16)
                sp.sem_inc(stored, 1)
                with sp.Fori(0, batches) as k:
                    sp.wait_ge(o_out, k + 1 + 1)
                    sp.dma_start(env.o_table[ds(k * (WB * WN), WB * WN), :].rearrange("(j n) d -> n j d", n=WN),
                                 o_rows[:]).then_inc(stored, 16)
                sp.wait_ge(stored, 16 * batches + 1)

            @block.gpsimd
            def _(pool):
                def take(k):
                    pool.wait_ge(turned, k + 1)
                    pool.sem_inc(hold, 1)
                    pool.tensor_copy(s_rows[:], env.window_sums[:, ds(k * WB, WB), :]).then_inc(taken, 1)

                take(0)
                with pool.Fori(0, batches) as k:
                    take(k + 1)

            @block.tensor
            def _(pe):
                pe.sem_inc(turned, 1)
                pe.sem_inc(weighed, 1)
                pe.wait_ge(landed, 80)

                def turn(k):
                    pe.wait_ge(taken, k + 1)
                    pe.wait_ge(turned_copied, k + 1)
                    for c in range(K2):
                        for j in range(WB):
                            mm = pe.transpose(turn_ps[:, (c * WB + j) * WR:(c * WB + j + 1) * WR],
                                              s_rows[:, j, c * 128:(c + 1) * 128], env.ident[0:WR, 0:WR])
                    mm.then_inc(turned, 1)

                def project(k):
                    pe.wait_ge(turned_copied, k + 1 + 1)
                    pe.wait_ge(qk_out, k + 1)
                    pe.wait_ge(v_out, k + 1)
                    for m in range(4):
                        for c in range(K2):
                            pe.matmul(qk_ps[:, m // 2, (m % 2) * M:(m % 2 + 1) * M], w_sb[:, c, m * 128:(m + 1) * 128],
                                      s_t[:, c, :], start=c == 0, stop=c == K2 - 1)
                    for j in range(WB):
                        for c in range(K2):
                            mm = pe.matmul(v_ps[0:WR, j * D:(j + 1) * D], s_t[:, c, j * WR:(j + 1) * WR],
                                           w_sb[:, c, 2 * D:3 * D], start=c == 0, stop=c == K2 - 1)
                    mm.then_inc(projected, 1)

                turn(0)
                project(0)
                with pe.Fori(0, batches // 2) as it:
                    for b in range(2):
                        k = it * 2 + b
                        turn(k + 1)
                        pe.wait_ge(qk_out, k + 1 + 1)
                        pe.wait_ge(masked, k + 1)
                        for j in range(WB):
                            for h in range(HEADS):
                                f = slice((h % 2) * HD, (h % 2 + 1) * HD)
                                n = slice(j * WR, (j + 1) * WR)
                                at = (j * 2 + h // 2) * WR
                                mm = pe.matmul(score_ps[0:WR, h % 2, at:at + WR], qk_t[f, h // 2, n],
                                               qk_t[f, 2 + h // 2, n], start=True, stop=True)
                        mm.then_inc(scored, 1)
                        project(k + 1)
                        pe.wait_ge(chosen, k + 1)
                        pe.wait_ge(weights_out, k + 1)
                        for j in range(WB * HEADS):
                            mm = pe.matmul(weight_ps[0:WR, j * WN:(j + 1) * WN], score[:, j, :], chooser[:, j, :],
                                           start=True, stop=True)
                        mm.then_inc(weighed, 1)
                        pe.wait_ge(weights_out, k + 1 + 1)
                        pe.wait_ge(o_out, k + 1)
                        pe.wait_ge(v_out, k + 1 + 1)
                        for n in range(WB * HEADS):
                            j, h = n // 2 % WB, n % 2 * 2 + n // (2 * WB)
                            mm = pe.matmul(o_ps[0:WN, j * D + h * HD:j * D + (h + 1) * HD],
                                           weight[:, n * WN:(n + 1) * WN], v_sb[:, b, j, h * HD:(h + 1) * HD],
                                           start=True, stop=True)
                        mm.then_inc(attended, 1)

            @block.scalar
            def _(act):
                act.wait_ge(landed, 80)
                act.sem_inc(turned_copied, 1)
                act.sem_inc(qk_out, 1)
                act.sem_inc(weights_out, 1)
                act.sem_inc(o_out, 1)

                def copy_turned(k):
                    act.wait_ge(projected, k) if not isinstance(k, int) else None
                    act.wait_ge(turned, k + 1 + 1)
                    act.activation(s_t[:].rearrange("p c n -> p (c n)"), turn_ps[:, 0:K2 * M], ACT.Copy).then_inc(turned_copied, 1)

                def qk(k):
                    act.wait_ge(scored, k) if not isinstance(k, int) else None
                    act.wait_ge(projected, k + 1)
                    for m in range(4):
                        ins = act.activation(qk_t[:, m, :], qk_ps[:, m // 2, (m % 2) * M:(m % 2 + 1) * M], ACT.Identity,
                                             bias=bias_col[:, m:m + 1])
                    ins.then_inc(qk_out, 1)

                copy_turned(0)
                qk(0)
                with act.Fori(0, batches) as k:
                    copy_turned(k + 1)
                    act.wait_ge(lowered, k + 1)
                    act.activation(score[:], score[:], ACT.Exp, scale=HD ** -0.5).then_inc(exped, 1)
                    qk(k + 1)
                    act.wait_ge(weighed, k + 1 + 1)
                    act.activation(weight[:], weight_ps[0:WR, 0:WB * HEADS * WN], ACT.Copy).then_inc(weights_out, 1)
                    act.wait_ge(attended, k + 1)
                    act.wait_ge(stored, k * 16 + 1)
                    act.activation(o_rows[:].rearrange("p j d -> p (j d)"), o_ps[0:WN, 0:WB * D], ACT.Copy).then_inc(o_out, 1)

            @block.vector
            def _(v):
                v.wait_ge(landed, 80)
                v.sem_inc(v_out, 1)
                v.sem_inc(masked, 1)

                def values(b, k):
                    v.wait_ge(projected, k + 1)
                    v.tensor_tensor(v_sb[:, b], v_ps[0:WR].rearrange("p (j d) -> p j d", j=WB),
                                    v_bias[:].unsqueeze(1).to_broadcast([WR, WB, D]), ALU.add).then_inc(v_out, 1)

                values(0, 0)
                with v.Fori(0, batches // 2) as it:
                    for b in range(2):
                        k = it * 2 + b
                        v.wait_ge(scored, k + 1)
                        v.wait_ge(weighed, k + 1)
                        v.tensor_tensor(score[:].rearrange("p (u j) n -> p u j n", u=2),
                                        score_ps[0:WR, :, 0:HEADS * WR].rearrange("p u (j n) -> p u j n", j=HEADS),
                                        other[:].unsqueeze(1).unsqueeze(1).to_broadcast([WR, 2, HEADS, WR]),
                                        ALU.add).then_inc(masked, 1)
                        v.wait_ge(masked, k + 1 + 1)
                        v.tensor_reduce(top[:], score[:], AX.X, ALU.max).then_inc(topped, 1)
                        v.wait_ge(topped, k + 1)
                        v.tensor_tensor(score[:], score[:], top[:].unsqueeze(2).to_broadcast([WR, WB * HEADS, WR]),
                                        ALU.subtract).then_inc(lowered, 1)
                        v.wait_ge(exped, k + 1)
                        v.tensor_reduce(total[:], score[:], AX.X, ALU.add).then_inc(summed, 1)
                        v.wait_ge(summed, k + 1)
                        v.reciprocal(total[:], total[:]).then_inc(inverted, 1)
                        v.wait_ge(inverted, k + 1)
                        v.tensor_tensor(chooser[:], share[:].unsqueeze(1).to_broadcast([WR, WB * HEADS, WN]),
                                        total[:].unsqueeze(2).to_broadcast([WR, WB * HEADS, WN]), ALU.mult).then_inc(chosen, 1)
                        values(1 - b, k + 1)


def relation_output_phase(env):
    nc = env.nc
    ph = Phase(env)
    a = env.a
    with ExitStack() as st:
        out_w = sb(env, st, "out_w", [128, K2, D])
        proj_w = sb(env, st, "proj_w", [128, K2, D])
        out_b = sb(env, st, "out_b", [128, K2])
        proj_bc = sb(env, st, "proj_bc", [P, D])
        normed = sb(env, st, "normed", [P, GT, D])
        o_rows = sb(env, st, "o_rows", [P, GT, D])
        o_t = sb(env, st, "o_t", [128, GT, K2 * P])
        h_t = sb(env, st, "h_t", [128, GT, K2 * P])
        turn_ps = ps(env, st, "turn_ps", [128, 2, 512])
        h_ps = ps(env, st, "h_ps", [128, 2, 512])
        y_ps = ps(env, st, "y_ps", [128, 2, 512])
        w_landed, turned, turned_copied, mixed, h_out, projected, added, biased, normed_made = [ph.sem() for _ in range(9)]
        o_landed = [ph.sem() for _ in range(GT)]
        with nc.Block() as block:

            @block.sync
            def _(sp):
                ph.clear_other()
                sp.dma_start(out_w[:], a["L1_gnn_attn_out_w"].rearrange("(k p) n -> p k n", p=128)).then_inc(w_landed, 16)
                sp.dma_start(proj_w[:], a["L1_gnn_proj_w"].rearrange("(k p) n -> p k n", p=128)).then_inc(w_landed, 16)
                sp.dma_start(out_b[:], a["L1_gnn_attn_out_b"]).then_inc(w_landed, 16)
                sp.dma_start(proj_bc[:], env.row("L1_gnn_proj_b").to_broadcast([P, D])).then_inc(w_landed, 16)
                with sp.Fori(0, G) as g:
                    for i in range(GT):
                        t = g * GT + i
                        sp.wait_ge(turned, t + 1)
                        sp.dma_start(o_rows[:, i, :], env.o_table[ds(t * P, P), :]).then_inc(o_landed[i], 16)
                for i in range(GT):
                    sp.wait_ge(o_landed[i], 16 * G)

            @block.vector
            def _(v):
                v.wait_ge(w_landed, 64)
                v.sem_inc(added, 2)
                with v.Fori(0, G) as g:
                    for i in range(GT):
                        t = g * GT + i
                        x_t = env.x[:, ds(t, 1), :].rearrange("p o d -> p (o d)")
                        v.wait_ge(mixed, t + 1)
                        v.tensor_scalar(normed[:, i, :], x_t, env.mean[:, ds(t, 1)], env.rstd[:, ds(t, 1)],
                                        ALU.subtract, ALU.mult).then_inc(normed_made, 1)
                    for i in range(GT):
                        t = g * GT + i
                        x_t = env.x[:, ds(t, 1), :].rearrange("p o d -> p (o d)")
                        v.tensor_tensor(x_t, x_t, proj_bc[:], ALU.add).then_inc(biased, 1)
                        v.wait_ge(biased, t + 1)
                        v.wait_ge(projected, t + 1 + GT)
                        v.tensor_tensor(x_t, y_ps[0:P, i % 2, 0:D], x_t, ALU.add).then_inc(added, 1)

            @block.tensor
            def _(pe):
                pe.sem_inc(turned, GT)
                pe.sem_inc(mixed, GT)
                pe.sem_inc(projected, GT)
                pe.wait_ge(w_landed, 64)
                with pe.Fori(0, G) as g:
                    for i in range(GT):
                        t = g * GT + i
                        pe.wait_ge(o_landed[i], (g + 1) * 16)
                        pe.wait_ge(turned_copied, t + (1 + (i == 0)))
                        for k in range(K2):
                            mm = pe.transpose(turn_ps[:, i % 2, k * P:(k + 1) * P], o_rows[:, i, k * 128:(k + 1) * 128],
                                              env.ident[0:P, 0:P])
                        mm.then_inc(turned, 1)
                    for i in range(GT):
                        t = g * GT + i
                        pe.wait_ge(turned_copied, t + 1 + 2)
                        pe.wait_ge(normed_made, t + 1)
                        pe.wait_ge(h_out, t + (1 + (i == 0)))
                        for m in range(K2):
                            out = h_ps[:, i % 2, m * P:(m + 1) * P]
                            for k in range(K2):
                                pe.matmul(out, out_w[:, k, m * 128:(m + 1) * 128], o_t[:, i, k * P:(k + 1) * P],
                                          start=k == 0, stop=False)
                            mm = pe.matmul(out, normed[:, i, m * 128:(m + 1) * 128], env.ident[0:P, 0:P],
                                           start=False, stop=True)
                        mm.then_inc(mixed, 1)
                    for i in range(GT):
                        t = g * GT + i
                        pe.wait_ge(h_out, t + 1 + 2)
                        pe.wait_ge(added, t + (1 + (i == 0)))
                        for k in range(K2):
                            mm = pe.matmul(y_ps[0:P, i % 2, 0:D], h_t[:, i, k * P:(k + 1) * P], proj_w[:, k, :],
                                           start=k == 0, stop=k == K2 - 1)
                        mm.then_inc(projected, 1)

            @block.scalar
            def _(act):
                act.wait_ge(w_landed, 64)
                act.sem_inc(turned_copied, 2)
                act.sem_inc(h_out, 2)
                with act.Fori(0, G) as g:
                    for i in range(GT):
                        t = g * GT + i
                        act.wait_ge(mixed, t + 1)
                        act.wait_ge(turned, t + 1 + GT)
                        act.activation(o_t[:, i, :], turn_ps[:, i % 2, 0:K2 * P], ACT.Copy).then_inc(turned_copied, 1)
                    for i in range(GT):
                        t = g * GT + i
                        act.wait_ge(projected, t + 1)
                        act.wait_ge(mixed, t + 1 + GT)
                        for m in range(K2):
                            ins = act.activation(h_t[:, i, m * P:(m + 1) * P], h_ps[:, i % 2, m * P:(m + 1) * P],
                                                 ACT.Identity, bias=out_b[:, m:m + 1])
                        ins.then_inc(h_out, 1)


def spread_phase(env, kind):
    nc = env.nc
    ph = Phase(env)
    with ExitStack() as st:
        own = sb(env, st, "own", [P, T, D]) if kind == "L3" else None
        bias_bc = sb(env, st, "bias_bc", [P, D])
        landed, step = ph.sem(), ph.sem()
        with nc.Block() as block:

            @block.sync
            def _(sp):
                ph.clear_other()
                if kind == "L3":
                    sp.dma_start(own[:], env.k_table.rearrange("(t p) d -> p t d", p=P)).then_inc(landed, 16)
                    sp.dma_start(bias_bc[:], env.row("L3_gnn_b").to_broadcast([P, D])).then_inc(landed, 16)

            @block.vector
            def _(v):
                n = [0]

                def done(ins):
                    n[0] += 1
                    ins.then_inc(step, 1)
                    v.wait_ge(step, n[0])

                y, x = env.node_sums[:], env.x[:]
                scale = (env.norm2 if kind == "L2" else env.norm3)[:].unsqueeze(2).to_broadcast([P, T, D])
                if kind == "L3":
                    v.wait_ge(landed, 32)
                    done(v.tensor_tensor(y, y, own[:], ALU.add))
                done(v.tensor_tensor(y, y, scale, ALU.mult))
                if kind == "L3":
                    done(v.tensor_tensor(y, y, bias_bc[:].unsqueeze(1).to_broadcast([P, T, D]), ALU.add))
                    done(v.scalar_tensor_tensor(out=y, in0=y, scalar=0.2, in1=y, op0=ALU.mult, op1=ALU.max))
                done(v.tensor_tensor(x, x, y, ALU.add))


def small_experts_phase(env):
    nc = env.nc
    ph = Phase(env)
    a = env.a
    ring = 2
    with ExitStack() as st:
        sizes = [("s", None, 256, 128)] + [("e", e, 128, 64) for e in range(4)]
        sems = ExpertSems(ph)
        landed = ph.sem()
        hidden_ps = ps(env, st, "hidden_ps", [128, ring, 512])
        out_ps = ps(env, st, "out_ps", [128, 4, 512])
        h1 = sb(env, st, "h1", [128, 2, GN])
        h2 = sb(env, st, "h2", [128, 1, GN])
        bias = {"sb1": sb(env, st, "sb1", [128, 2]), "sb2": sb(env, st, "sb2", [128, 1]),
                "eb1": sb(env, st, "eb1", [128, 4]), "eb2": sb(env, st, "eb2", [64, 4])}
        loads, experts = [(tile, a[f"L3_ffn_{p}"]) for p, tile in bias.items()], []
        for which, e, d1, d2 in sizes:
            w1 = sb(env, st, f"w1_{which}{e}", [128, K2, d1])
            w2 = sb(env, st, f"w2_{which}{e}", [128, d1 // 128, d2])
            w3 = sb(env, st, f"w3_{which}{e}", [d2, 1, D])
            for j, tile in enumerate((w1, w2, w3)):
                src = a[f"L3_ffn_{which}W{j + 1}"]
                src = src if e is None else src[e]
                loads.append((tile, src.rearrange("(k p) n -> p k n", p=min(128, src.shape[0]))))
            def cols(b, first):
                return lambda g, m, rows: bias[b][0:rows, first + m:first + m + 1]
            experts.append(Expert(env, [
                {"in": D, "out": d1, "w": w1, "h": h1, "func": ACT.Relu, "bias": cols(which + "b1", e or 0)},
                {"in": d1, "out": d2, "w": w2, "h": h2, "func": ACT.Relu, "bias": cols(which + "b2", e or 0)},
            ], w3, 1, ring, sems))
        total = sum(x.pieces for x in experts)
        firsts = [sum(x.pieces for x in experts[:n]) for n in range(len(experts))]
        with nc.Block() as block:

            @block.sync
            def _(sp):
                ph.clear_other()
                for tile, src in loads:
                    sp.dma_start(tile[:], src).then_inc(landed, 16)

            @block.tensor
            def _(pe):
                pe.wait_ge(landed, 16 * len(loads))
                with pe.Fori(0, G) as g:
                    for n, x in enumerate(experts):
                        x.tensor(pe, lambda k, lo, size: env.x_t[:, k, ds(g * GN + lo, size)], g * total + firsts[n],
                                 g * (5 * GT) + n * GT, hidden_ps, out_ps, firsts[n])

            @block.scalar
            def _(act):
                act.wait_ge(landed, 16 * len(loads))
                act.sem_inc(sems.activated, ring)
                with act.Fori(0, G) as g:
                    for n, x in enumerate(experts):
                        x.scalar(act, g, g * total + firsts[n], hidden_ps, firsts[n])

            @block.vector
            def _(v):
                v.sem_inc(sems.mixed, 5)
                with v.Fori(0, G) as g:
                    for n, x in enumerate(experts):
                        x.vector(v, lambda t: env.ones[0:P, 0:1] if n == 0 else
                                 env.gates[:, ds(t, 1), n - 1:n].rearrange("p o e -> p (o e)"),
                                 g * (5 * GT) + n * GT, g, out_ps)


def build(nc, a, out, stop=99):
    env = Env(nc, a, out)
    with ExitStack() as st:
        env.sem_sets = [[st.enter_context(nc.semaphore(f"set{s}_{i}")) for i in range(24)] for s in range(2)]
        env.gathered = [st.enter_context(nc.semaphore(f"gathered_{s}")) for s in range(2)]
        env.gathered_base = 0
        env.mean = sb(env, st, "mean", [P, T])
        env.rstd = sb(env, st, "rstd", [P, T])
        env.mean2 = sb(env, st, "mean2", [P, T])
        env.rstd2 = sb(env, st, "rstd2", [P, T])
        env.norm2 = sb(env, st, "norm2", [P, T])
        env.norm3 = sb(env, st, "norm3", [P, T])
        env.ident = sb(env, st, "ident", [128, 128])
        env.ones = sb(env, st, "ones", [128, 128])
        env.iota = sb(env, st, "iota", [128, 640])
        env.part = sb(env, st, "part", [128, 1])
        env.tile_of_visit = sb(env, st, "tile_of_visit", [1, VT_PAD], I32)
        env.window_of_visit = sb(env, st, "window_of_visit", [1, VW_PAD], I32)
        env.src_of_visit = sb(env, st, "src_of_visit", [128, VT_PAD], I32)
        env.message_of_visit = sb(env, st, "message_of_visit", [128, VW_PAD], I32)
        env.rel_dst = sb(env, st, "rel_dst", [128, VT_PAD])
        env.type64 = sb(env, st, "type64", [128, VT_PAD])
        env.row_of_edge = sb(env, st, "row_of_edge", [128, VW_PAD])
        env.k_table = nc.dram_tensor("k_table", (N, D), F32).ap()
        env.v_table = nc.dram_tensor("v_table", (N, D), F32).ap()
        env.x_table = nc.dram_tensor("x_table", (N, D), F32).ap()
        env.o_table = nc.dram_tensor("o_table", (NWP * WN, D), F32).ap()
        env.messages = nc.dram_tensor("messages", (N * R6, D), F32).ap()

        x_stack = ExitStack()
        env.x = sb(env, x_stack, "x", [P, T, D])
        setup_phase(env, a)
        stats_phase(env, env.x)
        with ExitStack() as l0:
            env.sums = sb(env, l0, "sums", [P, T, VC])
            env.peaks = sb(env, l0, "peaks", [P, T, HEADS])
            env.scores = sb(env, l0, "scores", [128, VT_PAD, HEADS])
            with ExitStack() as sq:
                env.q = sb(env, sq, "q", [P, T, D])
                project_phase(env, a["qkv_w"].rearrange("(k p) n -> p k n", p=128),
                              env.row("qkv_b").to_broadcast([P, 3 * D]), 3 * D, "qkv")
                score_phase(env)
            peak_phase(env)
            attend_phase(env)
            message_phase(env)
            stats_phase(env, env.sums[:, :, 0:D])
            affine_phase(env)
        stats_phase(env, env.x)
        with ExitStack() as f0:
            env.gates = sb(env, f0, "gates", [P, T, 8])
            env.x_t = sb(env, f0, "x_t", [128, K2, N])
            router_phase(env, "L0")
            experts_phase(env, "L0")
        if stop == 1:
            store_phase(env)
            x_stack.close()
            return
        stats_phase(env, env.x)
        project_phase(env, a["L1_gnn_W"].rearrange("(k p) n -> p k n", p=128),
                      env.row("L1_gnn_b").to_broadcast([P, R6 * D]), R6 * D, "plain",
                      env.messages.rearrange("(n r) d -> n (r d)", r=R6))
        move_phase(env, True)
        x_stack.close()
        with ExitStack() as l1:
            env.window_sums = sb(env, l1, "window_sums", [WR, NWP + WB, D])
            gather_sum_phase(env, env.messages, env.message_of_visit, env.row_of_edge, env.window_of_visit, NW,
                             env.window_sums, WR, VW)
            relation_attention_phase(env)
        env.x = sb(env, x_stack, "x", [P, T, D])
        move_phase(env, False)
        relation_output_phase(env)
        if stop == 2:
            store_phase(env)
            x_stack.close()
            return
        stats_phase(env, env.x)
        with ExitStack() as f1:
            env.gates = sb(env, f1, "gates", [P, T, 8])
            env.x_t = sb(env, f1, "x_t", [128, K2, N])
            with ExitStack() as sn:
                env.normed = sb(env, sn, "normed_all", [P, T, D])
                norm_phase(env)
                stats_phase(env, env.normed, env.mean2, env.rstd2)
            router_phase(env, "L1")
            experts_phase(env, "L1")
        if stop == 3:
            store_phase(env)
            x_stack.close()
            return
        stats_phase(env, env.x)
        for kind in ("L2", "L3"):
            with ExitStack() as l2:
                env.node_sums = sb(env, l2, "node_sums", [P, T, D])
                env.scale = env.norm2 if kind == "L2" else env.norm3
                w = a[f"{kind}_gnn_W"].rearrange("(k p) n -> p k n", p=128)
                bias = env.row("L2_gnn_b").to_broadcast([P, D]) if kind == "L2" else None
                project_phase(env, w, bias, D, "scaled", env.k_table)
                gather_sum_phase(env, env.k_table, env.src_of_visit, env.rel_dst, env.tile_of_visit, T,
                                 env.node_sums, P, VT)
                spread_phase(env, kind)
            stats_phase(env, env.x)
            with ExitStack() as f2:
                env.gates = sb(env, f2, "gates", [P, T, 8])
                env.x_t = sb(env, f2, "x_t", [128, K2, N])
                router_phase(env, kind)
                if kind == "L2":
                    experts_phase(env, "L2")
                    stats_phase(env, env.x)
                else:
                    small_experts_phase(env)
        store_phase(env)
        x_stack.close()


def kernel(**inputs):
    import numpy as _np
    import concourse.bacc as _bacc
    from concourse import mybir as _mybir
    from concourse.bass_utils import run_bass_kernel_spmd as _run

    given = {n: _np.ascontiguousarray(v) for n, v in inputs.items()}
    given["qkv_w"] = _np.concatenate([given.pop(f"L0_gnn_W{c}") for c in "qkv"], axis=1)
    given["qkv_b"] = _np.concatenate([given.pop(f"L0_gnn_b{c}") for c in "qkv"])
    for n in ("L1_gnn_in_proj_w", "L1_gnn_attn_out_w", "L1_gnn_proj_w", "L2_gnn_W", "L0_ffn_router_w"):
        given[n] = _np.ascontiguousarray(given[n].T)
    given["L1_gnn_W"] = _np.ascontiguousarray(given["L1_gnn_W"].transpose(1, 0, 2).reshape(D, R6 * D))
    given["L1_gnn_b"] = given["L1_gnn_b"].reshape(-1)
    given["in_proj_b_row"] = given["L1_gnn_in_proj_b"]
    node = _np.arange(WR) % WN
    given["other_node"] = _np.where(node[:, None] == node[None, :], 0.0, -1e30).astype(_np.float32)
    given["node_share"] = _np.where(node[:, None] == _np.arange(WN)[None, :], 1.0 / R6, 0.0).astype(_np.float32)
    given["L0_gnn_query_emb"] = _np.ascontiguousarray(given["L0_gnn_query_emb"].reshape(-1, 128).T)
    for n in ["L1_gnn_in_proj_b", "L1_gnn_attn_out_b", "L0_ffn_b1", "L1_ffn_b1", "L1_ffn_ln_g", "L1_ffn_ln_b", "L3_ffn_sb1", "L3_ffn_sb2", "L3_ffn_eb1"] + [
            f"L2_ffn_{p}{j}" for p in ("b", "g", "be", "m", "v") for j in "12"]:
        given[n] = _np.ascontiguousarray(given[n].reshape(-1, 128).T)
    given["L3_ffn_eb2"] = _np.ascontiguousarray(given["L3_ffn_eb2"].T)
    nc = _bacc.Bacc("TRN2", target_bir_lowering=False, num_devices=1)
    arrays, args = {}, {}
    for n, v in given.items():
        arrays[f"in_{n}"] = v
        args[n] = nc.dram_tensor(f"in_{n}", v.shape, _mybir.dt.from_np(v.dtype), kind="ExternalInput").ap()
    out = nc.dram_tensor("out_0_dram", given["x"].shape, F32, kind="ExternalOutput").ap()
    build(nc, args, out)
    r = _run(nc, [arrays], core_ids=[0])
    return r.results[0]["out_0_dram"]
```

```python
from contextlib import ExitStack

import numpy as np
import concourse.bass as bass
from concourse import mybir

F32 = mybir.dt.float32
I32 = mybir.dt.int32
U32 = mybir.dt.uint32
ALU = mybir.AluOpType
ACT = mybir.ActivationFunctionType
AX = mybir.AxisListType
ds = bass.ds

N = 3125
D = 256
K2 = D // 128
P = 125
T = N // P
G = 5
GT = T // G
GN = GT * P
E = 50000
CH = 128
NQ = 4
CQ = 98
C = NQ * CQ
REAL = -(-E // CH)
HEADS = 4
HD = D // HEADS
R6 = 6
R64 = 64
WN = 20
NW = -(-N // WN)
WR = R6 * WN
VB = 4
FAR = 1000000


class Env:

    def __init__(self, nc, a, out):
        self.nc, self.a, self.out, self.phase = nc, a, out, 0

    def row(self, name):
        return self.a[name].rearrange("(o d) -> o d", o=1)


class ExpertSems:

    def __init__(self, ph):
        self.activated = ph.sem()
        self.multiplied = ph.sem()
        self.finished = ph.sem()
        self.mixed = ph.sem()
        self.hold = ph.sem()


def round_up(a, b):
    return -(-a // b) * b


VT = round_up(REAL + T - 1, VB)
VW = round_up(REAL + NW - 1, VB)
AHEAD = 3
VT_PAD = round_up(VT + AHEAD * VB, 2)
VW_PAD = round_up(VW + AHEAD * VB, 2)
SLOTS = 4


def batch_loop(engine, total, head, block):
    for k in range(head):
        block(k, k % SLOTS, k // SLOTS)
    laps = (total - head) // SLOTS
    with engine.Fori(0, laps) as it:
        for b in range(head, head + SLOTS):
            block(it * SLOTS + b, b % SLOTS, it + b // SLOTS)
    for k in range(head + laps * SLOTS, total):
        block(k, k % SLOTS, k // SLOTS)


class Gather:

    def __init__(self, env, st, ph, table, index_of_visit, batches):
        self.env, self.table, self.index_of_visit, self.batches = env, table, index_of_visit, batches
        self.index = sb(env, st, "index", [128, SLOTS, VB], I32)
        self.rows = sb(env, st, "gathered_rows", [128, SLOTS, VB, D])
        self.indexed = ph.sem()
        self.freed = ph.sem()
        self.hold = ph.sem()
        self.passed = ph.sem()
        self.base = list(env.gathered_base)
        for s in range(SLOTS):
            env.gathered_base[s] += 16 * VB * len(range(s, batches, SLOTS))

    def scalar(self, act, k, slot):
        act.wait_ge(self.freed, k + 1)
        act.sem_inc(self.hold, 1)
        act.activation(self.index[:, slot, :], self.index_of_visit[:, ds(k * VB, VB)], ACT.Copy).then_inc(self.indexed, 1)

    def gpsimd(self, pool):
        def start(k, slot, lap):
            pool.wait_ge(self.freed, k + 1)
            pool.wait_ge(self.indexed, k + 1)
            pool.sem_inc(self.passed, 1)
            for i in range(VB):
                pool.indirect_dma_start(self.rows[:, slot, i, :], None, self.table, bass.IndirectOffsetOnAxis(
                    self.index[:, slot, i:i + 1], 0)).then_inc(self.env.gathered[slot], 16)

        batch_loop(pool, self.batches, 0, start)

    def wait(self, engine, slot, lap):
        engine.wait_ge(self.env.gathered[slot], lap * (16 * VB) + (self.base[slot] + 16 * VB))


class Phase:

    def __init__(self, env):
        self.env = env
        self.nc = env.nc
        self.set = env.sem_sets[env.phase % 2]
        self.other = env.sem_sets[(env.phase + 1) % 2]
        self.first = env.phase == 0
        self.used = 0
        env.phase += 1

    def sem(self):
        s = self.set[self.used]
        self.used += 1
        return s

    def clear_other(self):
        if not self.first:
            lo = min(s.num for s in self.other)
            hi = max(s.num for s in self.other)
            self.nc.sync.sem_clear(range(lo, hi + 1))


def sb(env, stack, name, shape, dt=F32):
    return stack.enter_context(env.nc.sbuf_tensor(f"{name}_{env.phase}", shape, dt))


def ps(env, stack, name, shape, dt=F32):
    return stack.enter_context(env.nc.psum_tensor(f"{name}_{env.phase}", shape, dt))


def setup_phase(env, a):
    nc = env.nc
    ph = Phase(env)
    with ExitStack() as st:
        rows_i = sb(env, st, "rows_i", [CQ, 4, NQ, CH], I32)
        rows_f = sb(env, st, "rows_f", [CQ, 4, NQ, CH])
        chunk_max = sb(env, st, "chunk_max", [CQ, NQ])
        edges_t = sb(env, st, "edges_t", [CQ, 256])
        before = sb(env, st, "before", [CQ, NQ, 256])
        key = sb(env, st, "key", [128, 2])
        cmp_a = sb(env, st, "cmp_a", [128, 2, VW_PAD])
        tile_bc = sb(env, st, "tile_bc", [128, VW_PAD])
        chunk_bc = sb(env, st, "chunk_bc", [128, VW_PAD])
        chunk_id = sb(env, st, "chunk_id", [CQ, NQ])
        sel = sb(env, st, "sel", [CQ, NQ, VW_PAD])
        rel_w = sb(env, st, "rel_w", [128, VW_PAD])
        in_a = sb(env, st, "in_a", [128, VW_PAD])
        in_b = sb(env, st, "in_b", [128, VW_PAD])
        kk = sb(env, st, "kk", [128, VW_PAD])
        src_f = sb(env, st, "src_f", [128, VW_PAD])
        iota_i = sb(env, st, "iota_i", [128, VW_PAD], I32)
        part_i = sb(env, st, "part_i", [128, 1], I32)
        pc = ps(env, st, "pc", [128, 512])
        pb = ps(env, st, "pb", [128, 2, 512])
        pv = ps(env, st, "pv", [128, 2, 2, 512])
        rows_cleared, rows_landed, x_landed = ph.sem(), ph.sem(), ph.sem()
        made, step, on_pe, loaded = ph.sem(), ph.sem(), ph.sem(), ph.sem()
        names = ["dst", "src", "edge_type_6", "edge_type_64"]

        with nc.Block() as block:

            @block.sync
            def _(sp):
                sp.dma_start(env.x[:], a["x"].rearrange("(t p) d -> p t d", p=P)).then_inc(x_landed, 16)
                sp.wait_ge(rows_cleared, 2)
                for j, name in enumerate(names):
                    for q in range(NQ):
                        lo = q * CQ * CH
                        n = min(CQ, (E - lo) // CH)
                        sp.dma_start(rows_i[0:n, j, q, :], a[name][lo:lo + n * CH].rearrange(
                            "(c e) -> c e", e=CH)).then_inc(rows_landed, 16)
                    tail = E - (REAL - 1) * CH
                    r = REAL - 1 - (NQ - 1) * CQ
                    sp.dma_start(rows_i[r:r + 1, j, NQ - 1, 0:tail], a[name][E - tail:E].rearrange(
                        "(c e) -> c e", c=1)).then_inc(rows_landed, 16)
                sp.wait_ge(x_landed, 16)

            @block.gpsimd
            def _(pool):
                pool.memset(rows_i[:, 0, NQ - 1, :], FAR).then_inc(rows_cleared, 1)
                pool.memset(rows_i[:, 1:4, NQ - 1, :], 0).then_inc(rows_cleared, 1)
                pool.iota(iota_i[:], [[1, VW_PAD]], base=0, channel_multiplier=0).then_inc(made, 1)
                pool.iota(part_i[:], [[0, 1]], base=0, channel_multiplier=1).then_inc(made, 1)
                pool.memset(env.ones[:], 1.0).then_inc(made, 1)
                pool.memset(env.ident[:], 0.0).then_inc(made, 1)
                pool.wait_ge(made, 4)
                pool.affine_select(out=env.ident[:], in_=env.ident[:], compare_op=ALU.not_equal, fill=1.0,
                                   base=0, pattern=[[-1, 128]], channel_multiplier=1).then_inc(made, 1)

            @block.vector
            def _(v):
                n = [0]

                def done(ins):
                    n[0] += 1
                    ins.then_inc(step, 1)
                    v.wait_ge(step, n[0])

                v.wait_ge(made, 5)
                done(v.tensor_copy(env.iota[:], iota_i[:]))
                done(v.tensor_copy(env.part[:], part_i[:]))
                for q in range(NQ):
                    done(v.tensor_scalar(chunk_id[:, q:q + 1], env.part[0:CQ, :], float(q * CQ), None, ALU.add))
                v.wait_ge(rows_landed, 16 * 4 * (NQ + 1))
                done(v.tensor_copy(rows_f[:], rows_i[:]))
                done(v.tensor_reduce(chunk_max[:], rows_f[:, 0], AX.X, ALU.max))
                pe = [0]

                def after_pe():
                    pe[0] += 1
                    v.wait_ge(on_pe, pe[0])

                for width, count, visits in ((P, T, VT_PAD), (WN, NW, VW_PAD)):
                    half = visits // 2
                    done(v.tensor_scalar(edges_t[:, 0:count], env.iota[0:CQ, 0:count], float(width), None, ALU.mult))
                    for q in range(NQ):
                        done(v.tensor_scalar(before[:, q, 0:count], edges_t[:, 0:count],
                                             chunk_max[:, q:q + 1], None, ALU.is_gt))
                    sets = [(w0, min(128, count - w0)) for w0 in range(0, count, 128)]
                    after_pe()
                    for j, (w0, m) in enumerate(sets):
                        done(v.tensor_scalar(key[0:m, j:j + 1], pc[0:m, j:j + 1], env.part[0:m, :], float(w0),
                                             ALU.add, ALU.add))
                        done(v.tensor_scalar(cmp_a[0:m, j, 0:visits], env.iota[0:m, 0:visits],
                                             key[0:m, j:j + 1], None, ALU.is_ge))
                    after_pe()
                    for h in range(2):
                        done(v.tensor_scalar(tile_bc[:, h * half:(h + 1) * half], pb[:, h, 0:half], -1.0, None, ALU.add))
                    done(v.tensor_tensor(chunk_bc[:, 0:visits], env.iota[:, 0:visits], tile_bc[:, 0:visits], ALU.subtract))
                    for q in range(NQ):
                        done(v.tensor_scalar(sel[:, q, 0:visits], chunk_bc[0:CQ, 0:visits],
                                             chunk_id[:, q:q + 1], None, ALU.is_equal))
                    tiles = env.tile_of_visit if width == P else env.window_of_visit
                    done(v.tensor_copy(tiles[0:1, 0:visits], tile_bc[0:1, 0:visits]))
                    after_pe()
                    for h in range(2):
                        s = slice(h * half, (h + 1) * half)
                        rel = env.rel_dst if width == P else rel_w
                        done(v.scalar_tensor_tensor(out=rel[:, s], in0=tile_bc[:, s], scalar=float(-width),
                                                    in1=pv[:, 0, h, 0:half], op0=ALU.mult, op1=ALU.add))
                        if width == P:
                            done(v.tensor_copy(env.src_of_visit[:, s], pv[:, 1, h, 0:half]))
                        else:
                            done(v.tensor_copy(src_f[:, s], pv[:, 1, h, 0:half]))
                    after_pe()
                    for h in range(2):
                        s = slice(h * half, (h + 1) * half)
                        if width == P:
                            done(v.tensor_copy(env.type64[:, s], pv[:, 0, h, 0:half]))
                        else:
                            done(v.tensor_scalar(in_a[:, s], rel_w[:, s], 0.0, None, ALU.is_ge))
                            done(v.scalar_tensor_tensor(out=in_b[:, s], in0=rel_w[:, s], scalar=float(WN),
                                                        in1=in_a[:, s], op0=ALU.is_lt, op1=ALU.mult))
                            done(v.scalar_tensor_tensor(out=kk[:, s], in0=pv[:, 0, h, 0:half], scalar=float(WN),
                                                        in1=rel_w[:, s], op0=ALU.mult, op1=ALU.add))
                            done(v.scalar_tensor_tensor(out=in_a[:, s], in0=kk[:, s], scalar=1.0,
                                                        in1=in_b[:, s], op0=ALU.add, op1=ALU.mult))
                            done(v.tensor_scalar(env.row_of_edge[:, s], in_a[:, s], -1.0, None, ALU.add))
                            done(v.scalar_tensor_tensor(out=kk[:, s], in0=src_f[:, s], scalar=float(R6),
                                                        in1=pv[:, 0, h, 0:half], op0=ALU.mult, op1=ALU.add))
                            done(v.tensor_copy(env.message_of_visit[:, s], kk[:, s]))

            @block.tensor
            def _(pe):
                n = 2 + NQ + 2
                for width, count, visits in ((P, T, VT_PAD), (WN, NW, VW_PAD)):
                    half = visits // 2
                    sets = [(w0, min(128, count - w0)) for w0 in range(0, count, 128)]
                    n += 1 + NQ
                    pe.wait_ge(step, n)
                    for j, (w0, m) in enumerate(sets):
                        for q in range(NQ):
                            mm = pe.matmul(pc[0:m, j:j + 1], before[:, q, w0:w0 + m], env.ones[0:CQ, 0:1],
                                           start=q == 0, stop=q == NQ - 1)
                    mm.then_inc(on_pe, 1)
                    n += 2 * len(sets)
                    pe.wait_ge(step, n)
                    for h in range(2):
                        for j, (w0, m) in enumerate(sets):
                            mm = pe.matmul(pb[:, h, 0:half], env.ones[0:m, :], cmp_a[0:m, j, h * half:(h + 1) * half],
                                           start=j == 0, stop=j == len(sets) - 1)
                    mm.then_inc(on_pe, 1)
                    n += 2 + 1 + NQ
                    pe.wait_ge(step, n)
                    for k, j in enumerate((0, 1)):
                        for h in range(2):
                            for q in range(NQ):
                                mm = pe.matmul(pv[:, k, h, 0:half], rows_f[:, j, q, :], sel[:, q, h * half:(h + 1) * half],
                                               start=q == 0, stop=q == NQ - 1)
                    mm.then_inc(on_pe, 1)
                    n += 1 + 4
                    pe.wait_ge(step, n)
                    j = 3 if width == P else 2
                    for h in range(2):
                        for q in range(NQ):
                            mm = pe.matmul(pv[:, 0, h, 0:half], rows_f[:, j, q, :], sel[:, q, h * half:(h + 1) * half],
                                           start=q == 0, stop=q == NQ - 1)
                    mm.then_inc(on_pe, 1)
                    n += 2 if width == P else 14


def stats_phase(env, x, mean=None, rstd=None):
    nc = env.nc
    mean, rstd = mean or env.mean, rstd or env.rstd
    ph = Phase(env)
    with ExitStack() as st:
        moments = sb(env, st, "moments", [P, T, 6])
        mv = sb(env, st, "mv", [P, T, 2])
        std = sb(env, st, "std", [P, T])
        eps = sb(env, st, "eps", [P, 1])
        summed, whole, rooted, step = ph.sem(), ph.sem(), ph.sem(), ph.sem()
        with nc.Block() as block:

            @block.sync
            def _(sp):
                ph.clear_other()

            @block.gpsimd
            def _(pool):
                pool.memset(eps[:], 1e-5).then_inc(whole, 1)

            @block.vector
            def _(v):
                with v.Fori(0, T) as t:
                    v.bn_stats(moments[:, ds(t, 1), :], x[:, ds(t, 1), :]).then_inc(summed, 1)
                v.wait_ge(summed, T)
                for t in range(T):
                    v.bn_aggr(mv[:, t, :], moments[:, t, :]).then_inc(step, 1)
                v.wait_ge(step, T)
                v.tensor_copy(mean[:], mv[:, :, 0:1].rearrange("p t o -> p (t o)")).then_inc(whole, 1)
                v.wait_ge(rooted, 1)
                v.reciprocal(rstd[:], std[:]).then_inc(step, 1)

            @block.scalar
            def _(act):
                act.wait_ge(whole, 2)
                act.activation(std[:], mv[:, :, 1:2].rearrange("p t o -> p (t o)"), ACT.Sqrt,
                               bias=eps[:]).then_inc(rooted, 1)


def norm_phase(env):
    ph = Phase(env)
    step = ph.sem()
    with env.nc.Block() as block:

        @block.sync
        def _(sp):
            ph.clear_other()

        @block.vector
        def _(v):
            v.tensor_tensor(env.normed[:], env.x[:], env.mean[:].unsqueeze(2).to_broadcast([P, T, D]),
                            ALU.subtract).then_inc(step, 1)
            v.wait_ge(step, 1)
            v.tensor_tensor(env.normed[:], env.normed[:], env.rstd[:].unsqueeze(2).to_broadcast([P, T, D]),
                            ALU.mult).then_inc(step, 1)


def project_phase(env, w, bias, cols, kind, out_table=None):
    nc = env.nc
    ph = Phase(env)
    banks = -(-cols // 512)
    with ExitStack() as st:
        w_sb = sb(env, st, "w_sb", [128, K2, cols])
        bias_bc = sb(env, st, "bias_bc", [P, cols])
        normed = sb(env, st, "normed", [P, GT, D])
        x_t = sb(env, st, "x_t", [128, GT, K2, P])
        rows = sb(env, st, "rows", [P, GT, cols])
        query = sb(env, st, "query", [128, K2])
        query_s = sb(env, st, "query_s", [128, K2])
        turned = ps(env, st, "turned", [128, 2, K2 * 256])
        prod = ps(env, st, "prod", [128, 2, banks, 512])
        w_landed, query_scaled = ph.sem(), ph.sem()
        normed_ready, transposed, x_t_ready, multiplied = ph.sem(), ph.sem(), ph.sem(), ph.sem()
        added, rows_ready, stored = ph.sem(), ph.sem(), ph.sem()
        loads = 1 + (bias is not None) + (kind == "qkv")
        stores = 2 if kind == "qkv" else 1
        with nc.Block() as block:

            @block.sync
            def _(sp):
                ph.clear_other()
                sp.dma_start(w_sb[:], w).then_inc(w_landed, 16)
                if bias is not None:
                    sp.dma_start(bias_bc[:], bias).then_inc(w_landed, 16)
                if kind == "qkv":
                    sp.dma_start(query[:], env.a["L0_gnn_query_emb"]).then_inc(w_landed, 16)
                sp.sem_inc(stored, 1)
                with sp.Fori(0, G) as g:
                    for i in range(GT):
                        sp.wait_ge(rows_ready, g * GT + i + 1)
                        r = ds((g * GT + i) * P, P)
                        if kind == "qkv":
                            sp.dma_start(env.k_table[r, :], rows[:, i, D:2 * D]).then_inc(stored, 16)
                            sp.dma_start(env.v_table[r, :], rows[:, i, 2 * D:3 * D]).then_inc(stored, 16)
                        else:
                            sp.dma_start(out_table[r, :], rows[:, i, :]).then_inc(stored, 16)
                sp.wait_ge(stored, 16 * stores * T + 1)

            @block.vector
            def _(v):
                v.wait_ge(w_landed, 16 * loads)
                if kind == "qkv":
                    v.tensor_scalar(query_s[:], query[:], 0.1, None, ALU.mult).then_inc(query_scaled, 1)
                v.sem_inc(added, 2)
                with v.Fori(0, G) as g:
                    for i in range(GT):
                        t = g * GT + i
                        v.wait_ge(transposed, t + 1)
                        v.tensor_scalar(normed[:, i, :], env.x[:, ds(t, 1), :].rearrange("p o d -> p (o d)"),
                                        env.mean[:, ds(t, 1)], env.rstd[:, ds(t, 1)], ALU.subtract,
                                        ALU.mult).then_inc(normed_ready, 1)
                    v.wait_ge(stored, g * (16 * stores * GT) + 1)
                    for i in range(GT):
                        t = g * GT + i
                        v.wait_ge(multiplied, t + 1 + GT)
                        for b in range(banks):
                            s = slice(b * 512, min(cols, b * 512 + 512))
                            here = prod[0:P, i % 2, b, 0:s.stop - s.start]
                            if bias is None:
                                ins = v.tensor_copy(rows[:, i, s], here)
                            else:
                                ins = v.tensor_tensor(rows[:, i, s], here, bias_bc[:, s], ALU.add)
                        ins.then_inc(added, 1)
                        v.wait_ge(added, t + 1 + 2)
                        if kind == "qkv":
                            v.tensor_copy(env.q[:, ds(t, 1), :].rearrange("p o d -> p (o d)"),
                                          rows[:, i, 0:D]).then_inc(rows_ready, 1)
                        elif kind == "scaled":
                            v.tensor_scalar(rows[:, i, :], rows[:, i, :], env.scale[:, ds(t, 1)], None,
                                            ALU.mult).then_inc(rows_ready, 1)
                        else:
                            v.sem_inc(rows_ready, 1)

            @block.tensor
            def _(pe):
                pe.sem_inc(transposed, GT)
                pe.sem_inc(multiplied, GT)
                pe.wait_ge(w_landed, 16 * loads)
                with pe.Fori(0, G) as g:
                    for i in range(GT):
                        t = g * GT + i
                        pe.wait_ge(normed_ready, t + 1)
                        pe.wait_ge(x_t_ready, t + (1 + (i == 0)))
                        for k in range(K2):
                            mm = pe.transpose(turned[:, i % 2, k * P:(k + 1) * P],
                                              normed[:, i, k * 128:(k + 1) * 128], env.ident[0:P, 0:P])
                        mm.then_inc(transposed, 1)
                    for i in range(GT):
                        t = g * GT + i
                        pe.wait_ge(x_t_ready, t + 1 + 2)
                        pe.wait_ge(added, t + (1 + (i == 0)))
                        for b in range(banks):
                            s = slice(b * 512, min(cols, b * 512 + 512))
                            for k in range(K2):
                                mm = pe.matmul(prod[0:P, i % 2, b, 0:s.stop - s.start], x_t[:, i, k, :],
                                               w_sb[:, k, s], start=k == 0, stop=k == K2 - 1)
                        mm.then_inc(multiplied, 1)

            @block.scalar
            def _(act):
                act.sem_inc(x_t_ready, 2)
                if kind == "qkv":
                    act.wait_ge(query_scaled, 1)
                with act.Fori(0, G) as g:
                    for i in range(GT):
                        t = g * GT + i
                        act.wait_ge(multiplied, t + 1)
                        act.wait_ge(transposed, t + 1 + GT)
                        if kind == "qkv":
                            for k in range(K2):
                                ins = act.activation(x_t[:, i, k, :], turned[:, i % 2, k * P:(k + 1) * P],
                                                     ACT.Identity, bias=query_s[:, k:k + 1])
                            ins.then_inc(x_t_ready, 1)
                        else:
                            act.activation(x_t[:, i].rearrange("p k n -> p (k n)"), turned[:, i % 2, 0:K2 * P],
                                           ACT.Copy).then_inc(x_t_ready, 1)


def make_hits(v, env, out, key_of_edge, width, k):
    return v.tensor_tensor(out, env.iota[:, 0:width].unsqueeze(1).to_broadcast([128, VB, width]),
                           key_of_edge[:, ds(k * VB, VB)].unsqueeze(2).to_broadcast([128, VB, width]), ALU.is_equal)


def score_phase(env):
    nc = env.nc
    ph = Phase(env)
    batches = VT // VB
    with ExitStack() as st:
        rel_raw = sb(env, st, "rel_raw", [R64, HD])
        rel_w = sb(env, st, "rel_w", [R64, HD])
        gather = Gather(env, st, ph, env.k_table, env.src_of_visit, batches)
        hit = sb(env, st, "hit", [128, SLOTS, VB, 128])
        hit_type = sb(env, st, "hit_type", [128, SLOTS, VB, R64])
        hit_t = sb(env, st, "hit_t", [128, SLOTS, VB * 128])
        type_t = sb(env, st, "type_t", [R64, SLOTS, VB * 128])
        q_rows = sb(env, st, "q_rows", [128, SLOTS, VB, D])
        terms = sb(env, st, "terms", [128, VB, D])
        ps_hit = ps(env, st, "ps_hit", [128, VB * 128])
        ps_type = ps(env, st, "ps_type", [128, VB * 128])
        ps_q = ps(env, st, "ps_q", [128, 2, VB, D])
        ps_rel = ps(env, st, "ps_rel", [128, 2, 512])
        rel_landed, rel_scaled = ph.sem(), ph.sem()
        hits_made, turned, turned_copied, multiplied, q_copied, summed, scored = [ph.sem() for _ in range(7)]
        with nc.Block() as block:

            @block.sync
            def _(sp):
                ph.clear_other()
                sp.dma_start(rel_raw[:], env.a["L0_gnn_rel_w"]).then_inc(rel_landed, 16)

            @block.gpsimd
            def _(pool):
                gather.gpsimd(pool)

            @block.vector
            def _(v):
                v.wait_ge(rel_landed, 16)
                v.tensor_scalar(rel_w[:], rel_raw[:], 0.2, None, ALU.mult).then_inc(rel_scaled, 1)
                v.sem_inc(gather.freed, SLOTS)
                v.sem_inc(scored, 2)
                v.memset(env.scores[:, VT:VT_PAD, :], 0.0)

                def hits(k, slot):
                    make_hits(v, env, hit[:, slot], env.rel_dst, 128, k)
                    make_hits(v, env, hit_type[:, slot], env.type64, R64, k).then_inc(hits_made, 1)

                hits(0, 0)
                hits(1, 1)

                def one_batch(k, slot, lap):
                    v.wait_ge(turned, k + 1)
                    hits(k + 2, (slot + 2) % SLOTS)
                    gather.wait(v, slot, lap)
                    v.wait_ge(multiplied, k + 1)
                    k_rows = gather.rows[:, slot].rearrange("p v (h d) -> p v h d", h=HEADS)
                    rel = ps_rel[:, slot % 2, 0:VB * HD].rearrange("p (v d) -> p v d", v=VB)
                    v.tensor_tensor(terms[:].rearrange("p v (h d) -> p v h d", h=HEADS), k_rows,
                                    rel.unsqueeze(2).to_broadcast([128, VB, HEADS, HD]), ALU.add).then_inc(gather.freed, 1)
                    v.wait_ge(gather.freed, k + (1 + SLOTS))
                    v.wait_ge(q_copied, k + (1 + SLOTS))
                    v.tensor_tensor(terms[:], terms[:], q_rows[:, slot], ALU.mult).then_inc(summed, 1)
                    v.wait_ge(summed, k + 1)
                    v.tensor_reduce(env.scores[:, ds(k * VB, VB), :], terms[:].rearrange("p v (h d) -> p v h d", h=HEADS),
                                    AX.X, ALU.add).then_inc(scored, 1)
                    v.wait_ge(scored, k + (1 + 2))

                batch_loop(v, batches, 0, one_batch)

            @block.tensor
            def _(pe):
                pe.wait_ge(rel_scaled, 1)

                def turn(k, slot):
                    pe.wait_ge(hits_made, k + 1)
                    pe.wait_ge(turned_copied, k + 1)
                    for i in range(VB):
                        pe.transpose(ps_hit[:, i * 128:(i + 1) * 128], hit[:, slot, i, :], env.ident[:])
                        mm = pe.transpose(ps_type[0:R64, i * 128:(i + 1) * 128], hit_type[:, slot, i, :], env.ident[:])
                    mm.then_inc(turned, 1)

                turn(0, 0)

                def one_batch(k, slot, lap):
                    turn(k + 1, (slot + 1) % SLOTS)
                    pe.wait_ge(turned_copied, k + 1 + 1)
                    pe.wait_ge(q_copied, k + (1 + SLOTS - 2))
                    pe.wait_ge(scored, k + 1)
                    for i in range(VB):
                        tile = pe.value_load(env.tile_of_visit[0:1, ds(k * VB + i, 1)], min_val=0, max_val=T - 1)
                        pe.matmul(ps_q[:, slot % 2, i, :], hit_t[0:P, slot, i * 128:(i + 1) * 128],
                                  env.q[:, ds(tile, 1), :].rearrange("p o d -> p (o d)"), start=True, stop=True)
                        mm = pe.matmul(ps_rel[:, slot % 2, i * HD:(i + 1) * HD], type_t[:, slot, i * 128:(i + 1) * 128],
                                       rel_w[:], start=True, stop=True)
                    mm.then_inc(multiplied, 1)

                batch_loop(pe, batches, 0, one_batch)

            @block.scalar
            def _(act):
                act.sem_inc(turned_copied, 1)
                act.sem_inc(q_copied, SLOTS)

                def copy(k, slot):
                    if not isinstance(k, int) or k >= SLOTS:
                        act.wait_ge(multiplied, k - (SLOTS - 1))
                    act.wait_ge(turned, k + 1)
                    act.activation(hit_t[:, slot], ps_hit[:], ACT.Copy)
                    act.activation(type_t[:, slot], ps_type[0:R64, :], ACT.Copy).then_inc(turned_copied, 1)

                for k in range(2):
                    gather.scalar(act, k, k)
                copy(0, 0)

                def one_batch(k, slot, lap):
                    gather.scalar(act, k + 2, (slot + 2) % SLOTS)
                    copy(k + 1, (slot + 1) % SLOTS)
                    act.wait_ge(multiplied, k + 1)
                    if not isinstance(k, int) or k >= SLOTS:
                        act.wait_ge(scored, k + (1 + 2 - SLOTS))
                    act.activation(q_rows[:, slot], ps_q[:, slot % 2], ACT.Copy).then_inc(q_copied, 1)

                batch_loop(act, batches, SLOTS, one_batch)


def peak_phase(env):
    nc = env.nc
    ph = Phase(env)
    with ExitStack() as st:
        low = sb(env, st, "low", [128, HEADS])
        low_h = sb(env, st, "low_h", [HEADS, 1])
        low_diag = sb(env, st, "low_diag", [HEADS, HEADS])
        low_bc = sb(env, st, "low_bc", [128, HEADS])
        hit = sb(env, st, "hit", [128, SLOTS, VB, 128])
        masked = sb(env, st, "masked", [128, SLOTS, VB * HEADS, 128])
        peak = sb(env, st, "peak", [P, VB * HEADS])
        ps_low = ps(env, st, "ps_low", [128, 512])
        ps_masked = ps(env, st, "ps_masked", [128, VB, 512])
        step, low_turned, hits_made, masked_made, turned, reduced, merged, zeroed, hold = [ph.sem() for _ in range(9)]
        batches = VT // VB
        with nc.Block() as block:

            @block.sync
            def _(sp):
                ph.clear_other()

            @block.gpsimd
            def _(pool):
                pool.memset(env.peaks[:], 0.0).then_inc(zeroed, 1)
                pool.wait_ge(step, 5)

                def one_batch(k, slot, lap):
                    pool.wait_ge(hits_made, k + 1)
                    pool.wait_ge(turned, k + 1)
                    pool.sem_inc(hold, 1)
                    pool.tensor_tensor(masked[:, slot].rearrange("p (v h) n -> p v h n", v=VB),
                                       hit[:, slot].unsqueeze(2).to_broadcast([128, VB, HEADS, 128]),
                                       env.scores[:, ds(k * VB, VB), :].unsqueeze(3).to_broadcast([128, VB, HEADS, 128]),
                                       ALU.mult).then_inc(masked_made, 1)

                batch_loop(pool, batches, 0, one_batch)

            @block.vector
            def _(v):
                v.tensor_reduce(low[:], env.scores[:, 0:VT, :].rearrange("p v h -> p h v"), AX.X,
                                ALU.min).then_inc(step, 1)
                v.wait_ge(low_turned, 1)
                v.tensor_reduce(low_h[:], ps_low[0:HEADS, 0:128], AX.X, ALU.min).then_inc(step, 1)
                v.wait_ge(step, 2)
                v.tensor_scalar(low_diag[:], env.ident[0:HEADS, 0:HEADS], low_h[:], None, ALU.mult).then_inc(step, 1)
                v.wait_ge(low_turned, 2)
                v.tensor_copy(low_bc[:], ps_low[:, 128:128 + HEADS]).then_inc(step, 1)
                v.wait_ge(step, 4)
                v.tensor_tensor(env.scores[:, 0:VT, :], env.scores[:, 0:VT, :],
                                low_bc[:].unsqueeze(1).to_broadcast([128, VT, HEADS]), ALU.subtract).then_inc(step, 1)

                for k in range(AHEAD):
                    make_hits(v, env, hit[:, k], env.rel_dst, 128, k).then_inc(hits_made, 1)
                v.wait_ge(zeroed, 1)
                v.sem_inc(reduced, 1)
                v.sem_inc(merged, 1)

                def one_batch(k, slot, lap):
                    v.wait_ge(turned, k + (1 + SLOTS))
                    v.wait_ge(merged, k * VB + 1)
                    v.tensor_reduce(peak[:], ps_masked[0:P].rearrange("p v (h e) -> p (v h) e", h=HEADS),
                                    AX.X, ALU.max).then_inc(reduced, 1)
                    make_hits(v, env, hit[:, (slot + AHEAD) % SLOTS], env.rel_dst, 128, k + AHEAD).then_inc(hits_made, 1)
                    v.wait_ge(reduced, k + 1 + 1)
                    for i in range(VB):
                        tile = v.value_load(env.tile_of_visit[0:1, ds(k * VB + i, 1)], min_val=0, max_val=T - 1)
                        here = env.peaks[:, ds(tile, 1), :].rearrange("p o h -> p (o h)")
                        v.tensor_tensor(here, here, peak[:, i * HEADS:(i + 1) * HEADS], ALU.max).then_inc(merged, 1)
                        if i < VB - 1:
                            v.wait_ge(merged, k * VB + (i + 1 + 1))

                batch_loop(v, batches, 0, one_batch)

            @block.tensor
            def _(pe):
                pe.sem_inc(turned, SLOTS)
                pe.wait_ge(step, 1)
                pe.transpose(ps_low[0:HEADS, 0:128], low[:], env.ident[:]).then_inc(low_turned, 1)
                pe.wait_ge(step, 3)
                pe.matmul(ps_low[:, 128:128 + HEADS], env.ones[0:HEADS, :], low_diag[:], start=True,
                          stop=True).then_inc(low_turned, 1)

                def one_batch(k, slot, lap):
                    pe.wait_ge(masked_made, k + 1)
                    pe.wait_ge(reduced, k + 1)
                    for i in range(VB * HEADS):
                        mm = pe.transpose(ps_masked[:, i // HEADS, (i % HEADS) * 128:(i % HEADS + 1) * 128],
                                          masked[:, slot, i, :], env.ident[:])
                    mm.then_inc(turned, 1)

                batch_loop(pe, batches, 0, one_batch)


VC = D + HEADS + 1


def attend_phase(env):
    nc = env.nc
    ph = Phase(env)
    batches = VT // VB
    with ExitStack() as st:
        gather = Gather(env, st, ph, env.v_table, env.src_of_visit, batches)
        hit = sb(env, st, "hit", [128, SLOTS, VB, 128])
        hit_t = sb(env, st, "hit_t", [128, SLOTS, VB * 128])
        below = sb(env, st, "below", [128, SLOTS, VB, HEADS])
        weight = sb(env, st, "weight", [128, SLOTS, VB, HEADS])
        summand = sb(env, st, "summand", [128, SLOTS, VB, VC])
        ps_hit = ps(env, st, "ps_hit", [128, VB * 128])
        ps_peak = ps(env, st, "ps_peak", [128, VB, HEADS])
        ps_sum = ps(env, st, "ps_sum", [128, VB, 512])
        cleared, hits_made, turned, turned_copied, peaks_out, lowered, clipped, weighed = [ph.sem() for _ in range(8)]
        multiplied, summed = ph.sem(), ph.sem()
        with nc.Block() as block:

            @block.sync
            def _(sp):
                ph.clear_other()

            @block.gpsimd
            def _(pool):
                pool.memset(env.sums[:], 0.0).then_inc(cleared, 1)
                pool.memset(summand[:], 1.0).then_inc(cleared, 1)
                gather.gpsimd(pool)

            @block.vector
            def _(v):
                def lower(k, slot):
                    v.wait_ge(peaks_out, k + 1)
                    v.tensor_tensor(below[:, slot], env.scores[:, ds(k * VB, VB), :], ps_peak[:],
                                    ALU.subtract).then_inc(lowered, 1)
                    v.wait_ge(lowered, k + 1)
                    v.tensor_scalar(below[:, slot], below[:, slot], 0.0, None, ALU.min).then_inc(clipped, 1)

                def add(k):
                    v.wait_ge(multiplied, k + 1)
                    for i in range(VB):
                        tile = v.value_load(env.tile_of_visit[0:1, ds(k * VB + i, 1)], min_val=0, max_val=T - 1)
                        v.wait_ge(summed, k * VB + (i + 1))
                        here = env.sums[:, ds(tile, 1), :].rearrange("p o c -> p (o c)")
                        v.tensor_tensor(here, here, ps_sum[0:P, i, 0:VC], ALU.add).then_inc(summed, 1)

                v.wait_ge(cleared, 2)
                v.sem_inc(gather.freed, SLOTS)
                v.sem_inc(summed, 1)
                for k in range(AHEAD):
                    make_hits(v, env, hit[:, k], env.rel_dst, 128, k).then_inc(hits_made, 1)
                lower(0, 0)

                def one_batch(k, slot, lap):
                    lower(k + 1, (slot + 1) % SLOTS)
                    gather.wait(v, slot, lap)
                    v.wait_ge(weighed, k + 1)
                    v.tensor_tensor(summand[:, slot, :, 0:D].rearrange("p v (h d) -> p v h d", h=HEADS),
                                    gather.rows[:, slot].rearrange("p v (h d) -> p v h d", h=HEADS),
                                    weight[:, slot].unsqueeze(3).to_broadcast([128, VB, HEADS, HD]), ALU.mult)
                    v.tensor_copy(summand[:, slot, :, D:D + HEADS], weight[:, slot]).then_inc(gather.freed, 1)
                    if not isinstance(k, int) or k > 0:
                        add(k - 1)
                    make_hits(v, env, hit[:, (slot + AHEAD) % SLOTS], env.rel_dst, 128, k + AHEAD).then_inc(hits_made, 1)

                batch_loop(v, batches, 1, one_batch)
                add(batches - 1)

            @block.tensor
            def _(pe):
                def turn(k, slot):
                    pe.wait_ge(hits_made, k + 1)
                    pe.wait_ge(turned_copied, k + 1)
                    for i in range(VB):
                        mm = pe.transpose(ps_hit[:, i * 128:(i + 1) * 128], hit[:, slot, i, :], env.ident[:])
                    mm.then_inc(turned, 1)

                def peaks(k, slot):
                    pe.wait_ge(turned_copied, k + 1 + 1)
                    if not isinstance(k, int) or k > 0:
                        pe.wait_ge(lowered, k)
                    for i in range(VB):
                        tile = pe.value_load(env.tile_of_visit[0:1, ds(k * VB + i, 1)], min_val=0, max_val=T - 1)
                        mm = pe.matmul(ps_peak[:, i, :], hit_t[0:P, slot, i * 128:(i + 1) * 128],
                                       env.peaks[:, ds(tile, 1), :].rearrange("p o h -> p (o h)"), start=True, stop=True)
                    mm.then_inc(peaks_out, 1)

                turn(0, 0)
                peaks(0, 0)
                turn(1, 1)
                peaks(1, 1)

                def one_batch(k, slot, lap):
                    turn(k + 2, (slot + 2) % SLOTS)
                    pe.wait_ge(gather.freed, k + (1 + SLOTS))
                    pe.wait_ge(summed, k * VB + 1)
                    for i in range(VB):
                        mm = pe.matmul(ps_sum[0:P, i, 0:VC], hit[:, slot, i, 0:P], summand[:, slot, i, :], start=True, stop=True)
                    mm.then_inc(multiplied, 1)
                    peaks(k + 2, (slot + 2) % SLOTS)

                batch_loop(pe, batches, 1, one_batch)

            @block.scalar
            def _(act):
                act.sem_inc(turned_copied, 1)

                def copy(k, slot):
                    if not isinstance(k, int) or k >= SLOTS:
                        act.wait_ge(peaks_out, k - (SLOTS - 1))
                    act.wait_ge(turned, k + 1)
                    act.activation(hit_t[:, slot], ps_hit[:], ACT.Copy).then_inc(turned_copied, 1)

                def weigh(k, slot):
                    act.wait_ge(clipped, k + 1)
                    act.wait_ge(gather.freed, k + 1)
                    act.activation(weight[:, slot], below[:, slot], ACT.Exp, scale=HD ** -0.5).then_inc(weighed, 1)

                for k in range(AHEAD - 1):
                    gather.scalar(act, k, k)
                    copy(k, k)
                weigh(0, 0)

                def one_batch(k, slot, lap):
                    gather.scalar(act, k + 2, (slot + 2) % SLOTS)
                    weigh(k + 1, (slot + 1) % SLOTS)
                    copy(k + 2, (slot + 2) % SLOTS)

                batch_loop(act, batches, SLOTS, one_batch)


def message_phase(env):
    nc = env.nc
    ph = Phase(env)
    with ExitStack() as st:
        w_sb = sb(env, st, "w_sb", [128, K2, D])
        bias_bc = sb(env, st, "bias_bc", [P, D])
        rden = sb(env, st, "rden", [P, T, HEADS])
        alone = sb(env, st, "alone", [P, T])
        degree = sb(env, st, "degree", [P, 2, T])
        root = sb(env, st, "root", [P, 2, T])
        v_own = sb(env, st, "v_own", [P, T, D])
        msg = sb(env, st, "msg", [P, GT, D])
        msg_t = sb(env, st, "msg_t", [128, GT, K2 * P])
        turned_ps = ps(env, st, "turned_ps", [128, 2, 512])
        prod = ps(env, st, "prod", [128, 2, 512])
        w_landed, step, rooted, scaled, msg_ready = [ph.sem() for _ in range(5)]
        transposed, copied, multiplied, added, own = [ph.sem() for _ in range(5)]
        with nc.Block() as block:

            @block.sync
            def _(sp):
                ph.clear_other()
                sp.dma_start(w_sb[:], env.a["L0_gnn_Wo"].rearrange("(k p) n -> p k n", p=128)).then_inc(w_landed, 16)
                sp.dma_start(bias_bc[:], env.row("L0_gnn_bo").to_broadcast([P, D])).then_inc(w_landed, 16)
                sp.dma_start(v_own[:], env.v_table.rearrange("(t p) d -> p t d", p=P)).then_inc(w_landed, 16)

            @block.vector
            def _(v):
                deg = env.sums[:, :, D + HEADS:D + HEADS + 1].rearrange("p t o -> p (t o)")
                v.tensor_scalar(rden[:], env.sums[:, :, D:D + HEADS], 1e-30, None, ALU.max).then_inc(step, 1)
                v.tensor_scalar(alone[:], deg, 0.5, None, ALU.is_lt).then_inc(step, 1)
                v.tensor_scalar(degree[:, 0, :], deg, 1.0, None, ALU.max).then_inc(step, 1)
                v.tensor_scalar(degree[:, 1, :], deg, 1.0, None, ALU.add).then_inc(step, 1)
                v.wait_ge(step, 4)
                v.reciprocal(rden[:], rden[:]).then_inc(step, 1)
                v.wait_ge(rooted, 1)
                v.reciprocal(env.norm2[:], root[:, 0, :]).then_inc(step, 1)
                v.reciprocal(env.norm3[:], root[:, 1, :]).then_inc(step, 1)
                v.wait_ge(step, 7)
                v.wait_ge(w_landed, 48)
                v.sem_inc(added, 2)
                with v.Fori(0, G) as g:
                    for i in range(GT):
                        t = g * GT + i
                        v.wait_ge(transposed, t + 1)
                        v.tensor_tensor(msg[:, i, :].rearrange("p (h d) -> p h d", h=HEADS),
                                        env.sums[:, ds(t, 1), 0:D].rearrange("p o (h d) -> p (o h) d", h=HEADS),
                                        rden[:, ds(t, 1), :].rearrange("p o h -> p (o h)").unsqueeze(2).to_broadcast([P, HEADS, HD]),
                                        ALU.mult).then_inc(scaled, 1)
                        v.wait_ge(scaled, t + 1)
                        v.scalar_tensor_tensor(out=msg[:, i, :], in0=v_own[:, ds(t, 1), :].rearrange("p o d -> p (o d)"),
                                               scalar=alone[:, ds(t, 1)], in1=msg[:, i, :], op0=ALU.mult,
                                               op1=ALU.add).then_inc(msg_ready, 1)
                    for i in range(GT):
                        t = g * GT + i
                        here = env.sums[:, ds(t, 1), 0:D].rearrange("p o d -> p (o d)")
                        own_t = v_own[:, ds(t, 1), :].rearrange("p o d -> p (o d)")
                        v.tensor_scalar(own_t, env.x[:, ds(t, 1), :].rearrange("p o d -> p (o d)"),
                                        env.mean[:, ds(t, 1)], env.rstd[:, ds(t, 1)], ALU.subtract,
                                        ALU.mult).then_inc(own, 1)
                        v.wait_ge(own, 2 * t + 1)
                        v.tensor_tensor(own_t, own_t, bias_bc[:], ALU.add).then_inc(own, 1)
                        v.wait_ge(own, 2 * t + 2)
                        v.wait_ge(multiplied, t + 1 + GT)
                        v.tensor_tensor(here, prod[0:P, i % 2, 0:D], own_t, ALU.add).then_inc(added, 1)

            @block.tensor
            def _(pe):
                pe.sem_inc(transposed, GT)
                pe.sem_inc(multiplied, GT)
                pe.wait_ge(w_landed, 48)
                with pe.Fori(0, G) as g:
                    for i in range(GT):
                        t = g * GT + i
                        pe.wait_ge(msg_ready, t + 1)
                        pe.wait_ge(copied, t + (1 + (i == 0)))
                        for k in range(K2):
                            mm = pe.transpose(turned_ps[:, i % 2, k * P:(k + 1) * P],
                                              msg[:, i, k * 128:(k + 1) * 128], env.ident[0:P, 0:P])
                        mm.then_inc(transposed, 1)
                    for i in range(GT):
                        t = g * GT + i
                        pe.wait_ge(copied, t + 1 + 2)
                        pe.wait_ge(added, t + (1 + (i == 0)))
                        for k in range(K2):
                            mm = pe.matmul(prod[0:P, i % 2, 0:D], msg_t[:, i, k * P:(k + 1) * P], w_sb[:, k, :],
                                           start=k == 0, stop=k == K2 - 1)
                        mm.then_inc(multiplied, 1)

            @block.scalar
            def _(act):
                act.sem_inc(copied, 2)
                act.wait_ge(step, 4)
                act.activation(root[:], degree[:], ACT.Sqrt).then_inc(rooted, 1)
                with act.Fori(0, G) as g:
                    for i in range(GT):
                        t = g * GT + i
                        act.wait_ge(multiplied, t + 1)
                        act.wait_ge(transposed, t + 1 + GT)
                        act.activation(msg_t[:, i, :], turned_ps[:, i % 2, 0:K2 * P], ACT.Copy).then_inc(copied, 1)


def affine_phase(env):
    nc = env.nc
    ph = Phase(env)
    with ExitStack() as st:
        gamma = sb(env, st, "gamma", [P, D])
        beta = sb(env, st, "beta", [P, D])
        landed, step = ph.sem(), ph.sem()
        with nc.Block() as block:

            @block.sync
            def _(sp):
                ph.clear_other()
                sp.dma_start(gamma[:], env.row("L0_gnn_gamma").to_broadcast([P, D])).then_inc(landed, 16)
                sp.dma_start(beta[:], env.row("L0_gnn_beta").to_broadcast([P, D])).then_inc(landed, 16)

            @block.vector
            def _(v):
                v.wait_ge(landed, 32)
                y = env.sums[:, :, 0:D]

                def over(col):
                    return col[:].unsqueeze(2).to_broadcast([P, T, D])

                def along(row):
                    return row[:].unsqueeze(1).to_broadcast([P, T, D])

                v.tensor_tensor(y, y, over(env.mean), ALU.subtract).then_inc(step, 1)
                v.wait_ge(step, 1)
                v.tensor_tensor(y, y, over(env.rstd), ALU.mult).then_inc(step, 1)
                v.wait_ge(step, 2)
                v.tensor_tensor(y, y, along(gamma), ALU.mult).then_inc(step, 1)
                v.wait_ge(step, 3)
                v.tensor_tensor(y, y, along(beta), ALU.add).then_inc(step, 1)
                v.wait_ge(step, 4)
                v.tensor_tensor(env.x[:], env.x[:], y, ALU.add).then_inc(step, 1)


def store_phase(env):
    nc = env.nc
    ph = Phase(env)
    stored = ph.sem()
    with nc.Block() as block:

        @block.sync
        def _(sp):
            ph.clear_other()
            sp.dma_start(env.out.rearrange("(t p) d -> p t d", p=P), env.x[:]).then_inc(stored, 16)
            sp.wait_ge(stored, 16)


def router_phase(env, kind):
    nc = env.nc
    ph = Phase(env)
    ne = {"L0": 8, "L1": 8, "L2": 8, "L3": 4}[kind]
    twice = kind == "L1"
    w = env.a[{"L0": "L0_ffn_router_w", "L1": "L1_ffn_Wr", "L2": "L2_ffn_Wr", "L3": "L3_ffn_gW"}[kind]]
    b = {"L0": None, "L1": "L1_ffn_br", "L2": "L2_ffn_br", "L3": "L3_ffn_gb"}[kind]
    last_bias = env.a[{"L0": "L0_ffn_b2", "L1": "L1_ffn_b2", "L2": "L2_ffn_bo", "L3": "L3_ffn_eb3"}[kind]]
    shared_bias = "L3_ffn_sb3" if kind == "L3" else None
    with ExitStack() as st:
        w_sb = sb(env, st, "w_sb", [128, K2, ne])
        bias_bc = sb(env, st, "bias_bc", [P, ne])
        last_sb = sb(env, st, "last_sb", [ne, D])
        shared_bc = sb(env, st, "shared_bc", [P, D])
        normed = sb(env, st, "normed", [P, GT, D])
        again = sb(env, st, "again", [P, GT, D]) if twice else None
        a_t = sb(env, st, "a_t", [128, GT, K2 * P])
        logits = sb(env, st, "logits", [P, T, ne])
        probs = sb(env, st, "probs", [P, T, ne])
        one_a = sb(env, st, "one_a", [P, T, ne])
        one_b = sb(env, st, "one_b", [P, T, ne])
        rank = sb(env, st, "rank", [P, ne])
        top = sb(env, st, "top", [P, T])
        top2 = sb(env, st, "top2", [P, T])
        share = sb(env, st, "share", [P, T])
        pick = sb(env, st, "pick", [P, T])
        gate_s = sb(env, st, "gate_s", [P, GT, ne])
        gate_t = sb(env, st, "gate_t", [ne, GT, P])
        turned_ps = ps(env, st, "turned_ps", [128, 2, 512])
        again_ps = ps(env, st, "again_ps", [128, 2, 512])
        logit_ps = ps(env, st, "logit_ps", [128, 2, 512])
        landed, normed_ready, transposed, copied, kept, multiplied, added, own_added = [ph.sem() for _ in range(8)]
        step, exped, gated, gate_ready, gate_turned, gate_copied, biased, bias_added, hold = [ph.sem() for _ in range(9)]
        loads = 2 + (b is not None) + (shared_bias is not None)
        with nc.Block() as block:

            @block.sync
            def _(sp):
                ph.clear_other()
                sp.dma_start(w_sb[:], w.rearrange("(k p) e -> p k e", p=128)).then_inc(landed, 16)
                sp.dma_start(last_sb[:], last_bias).then_inc(landed, 16)
                if b is not None:
                    sp.dma_start(bias_bc[:], env.row(b).to_broadcast([P, ne])).then_inc(landed, 16)
                if shared_bias is not None:
                    sp.dma_start(shared_bc[:], env.row(shared_bias).to_broadcast([P, D])).then_inc(landed, 16)

            @block.vector
            def _(v):
                v.wait_ge(landed, 16 * loads)
                v.sem_inc(added, 2)
                with v.Fori(0, G) as g:
                    for i in range(GT):
                        t = g * GT + i
                        x_t = env.x[:, ds(t, 1), :].rearrange("p o d -> p (o d)")
                        v.wait_ge(transposed, t + 1)
                        v.tensor_scalar(normed[:, i, :], x_t, env.mean[:, ds(t, 1)], env.rstd[:, ds(t, 1)],
                                        ALU.subtract, ALU.mult).then_inc(normed_ready, 1)
                        if twice:
                            v.wait_ge(normed_ready, 2 * t + 1)
                            v.tensor_scalar(again[:, i, :], normed[:, i, :], env.mean2[:, ds(t, 1)],
                                            env.rstd2[:, ds(t, 1)], ALU.subtract, ALU.mult).then_inc(normed_ready, 1)
                        if kind == "L0":
                            v.wait_ge(normed_ready, t + 1)
                            v.tensor_tensor(x_t, x_t, normed[:, i, :], ALU.add).then_inc(own_added, 1)
                        if kind == "L3":
                            v.wait_ge(normed_ready, t + 1)
                            v.tensor_tensor(x_t, x_t, shared_bc[:], ALU.add).then_inc(own_added, 1)
                    for i in range(GT):
                        t = g * GT + i
                        v.wait_ge(multiplied, t + 1 + GT)
                        here = logits[:, ds(t, 1), :].rearrange("p o e -> p (o e)")
                        if b is None:
                            v.tensor_copy(here, logit_ps[0:P, i % 2, 0:ne]).then_inc(added, 1)
                        else:
                            v.tensor_tensor(here, logit_ps[0:P, i % 2, 0:ne], bias_bc[:], ALU.add).then_inc(added, 1)
                n = [0]

                def done(ins):
                    n[0] += 1
                    ins.then_inc(step, 1)
                    v.wait_ge(step, n[0])

                def wide(col):
                    return col[:].unsqueeze(2).to_broadcast([P, T, ne])

                v.wait_ge(added, 2 + T)
                done(v.tensor_reduce(top[:], logits[:], AX.X, ALU.max))
                done(v.tensor_tensor(logits[:], logits[:], wide(top), ALU.subtract))
                v.wait_ge(exped, 1)
                done(v.tensor_reduce(share[:], probs[:], AX.X, ALU.add))
                done(v.reciprocal(share[:], share[:]))
                if kind == "L2":
                    done(v.tensor_tensor(env.gates[:, :, 0:ne], probs[:], wide(share), ALU.mult))
                else:
                    done(v.tensor_tensor(probs[:], probs[:], wide(share), ALU.mult))
                    done(v.tensor_scalar(rank[:], env.iota[0:P, 0:ne], -1.0, float(ne), ALU.mult, ALU.add))

                    def first_largest(values, best, one):
                        done(v.tensor_reduce(best[:], values[:], AX.X, ALU.max))
                        done(v.tensor_tensor(one[:], values[:], wide(best), ALU.is_equal))
                        done(v.tensor_tensor(one[:], one[:], rank[:].unsqueeze(1).to_broadcast([P, T, ne]), ALU.mult))
                        done(v.tensor_reduce(pick[:], one[:], AX.X, ALU.max))
                        done(v.tensor_tensor(one[:], one[:], wide(pick), ALU.is_equal))

                    first_largest(probs, top, one_a)
                    done(v.scalar_tensor_tensor(out=probs[:], in0=one_a[:], scalar=-2.0, in1=probs[:], op0=ALU.mult,
                                                op1=ALU.add))
                    first_largest(probs, top2, one_b)
                    if kind == "L3":
                        done(v.tensor_tensor(top2[:], top2[:], top[:], ALU.subtract))
                        v.wait_ge(exped, 2)
                        done(v.memset(top[:], 1.0))
                    done(v.tensor_tensor(share[:], top[:], top2[:], ALU.add))
                    if kind == "L0":
                        done(v.tensor_scalar(share[:], share[:], 1e-12, None, ALU.max))
                    done(v.reciprocal(share[:], share[:]))
                    done(v.tensor_tensor(top[:], top[:], share[:], ALU.mult))
                    done(v.tensor_tensor(top2[:], top2[:], share[:], ALU.mult))
                    done(v.tensor_tensor(one_a[:], one_a[:], wide(top), ALU.mult))
                    done(v.tensor_tensor(one_b[:], one_b[:], wide(top2), ALU.mult))
                    done(v.tensor_tensor(env.gates[:, :, 0:ne], one_a[:], one_b[:], ALU.add))
                v.sem_inc(bias_added, 2)
                with v.Fori(0, G) as g:
                    for i in range(GT):
                        t = g * GT + i
                        v.wait_ge(gate_turned, t + 1)
                        v.tensor_copy(gate_s[:, i, :], env.gates[:, ds(t, 1), 0:ne].rearrange("p o e -> p (o e)")).then_inc(gate_ready, 1)
                    for i in range(GT):
                        t = g * GT + i
                        x_t = env.x[:, ds(t, 1), :].rearrange("p o d -> p (o d)")
                        v.wait_ge(biased, t + 1)
                        v.tensor_tensor(x_t, logit_ps[0:P, i % 2, 0:D], x_t, ALU.add).then_inc(bias_added, 1)

            @block.tensor
            def _(pe):
                pe.sem_inc(transposed, GT)
                pe.sem_inc(multiplied, GT)
                pe.sem_inc(gate_turned, GT)
                pe.wait_ge(landed, 16 * loads)
                with pe.Fori(0, G) as g:
                    for i in range(GT):
                        t = g * GT + i
                        pe.wait_ge(normed_ready, (2 * t + 2) if twice else t + 1)
                        pe.wait_ge(kept, t + (1 + (i == 0)))
                        for k in range(K2):
                            if twice:
                                pe.transpose(again_ps[:, i % 2, k * P:(k + 1) * P],
                                             again[:, i, k * 128:(k + 1) * 128], env.ident[0:P, 0:P])
                            mm = pe.transpose(turned_ps[:, i % 2, k * P:(k + 1) * P],
                                              normed[:, i, k * 128:(k + 1) * 128], env.ident[0:P, 0:P])
                        mm.then_inc(transposed, 1)
                    for i in range(GT):
                        t = g * GT + i
                        pe.wait_ge(copied, t + 1)
                        pe.wait_ge(added, t + (1 + (i == 0)))
                        for k in range(K2):
                            mm = pe.matmul(logit_ps[0:P, i % 2, 0:ne], a_t[:, i, k * P:(k + 1) * P], w_sb[:, k, :],
                                           start=k == 0, stop=k == K2 - 1)
                        mm.then_inc(multiplied, 1)
                pe.wait_ge(added, 2 + T)
                pe.wait_ge(kept, 2 + T)
                with pe.Fori(0, G) as g:
                    for i in range(GT):
                        t = g * GT + i
                        pe.wait_ge(gate_ready, t + 1)
                        pe.wait_ge(gate_copied, t + (1 + (i == 0)))
                        pe.transpose(turned_ps[0:ne, i % 2, 0:P], gate_s[:, i, :], env.ident[0:P, 0:P]).then_inc(gate_turned, 1)
                    for i in range(GT):
                        t = g * GT + i
                        pe.wait_ge(gate_copied, t + 1 + 2)
                        pe.wait_ge(bias_added, t + (1 + (i == 0)))
                        pe.matmul(logit_ps[0:P, i % 2, 0:D], gate_t[:, i, :], last_sb[:], start=True,
                                  stop=True).then_inc(biased, 1)

            @block.scalar
            def _(act):
                act.sem_inc(kept, 2)
                with act.Fori(0, G) as g:
                    for i in range(GT):
                        t = g * GT + i
                        act.wait_ge(multiplied, t + 1)
                        act.wait_ge(transposed, t + 1 + GT)
                        act.activation(a_t[:, i, :], turned_ps[:, i % 2, 0:K2 * P], ACT.Copy).then_inc(copied, 1)
                        src = again_ps if twice else turned_ps
                        act.activation(env.x_t[:, :, ds(t * P, P)], src[:, i % 2, 0:K2 * P].rearrange("p (k n) -> p k n", k=K2),
                                       ACT.Copy).then_inc(kept, 1)
                act.wait_ge(step, 2)
                act.activation(probs[:], logits[:], ACT.Exp).then_inc(exped, 1)
                if kind == "L3":
                    act.wait_ge(step, 18)
                    act.activation(top2[:], top2[:], ACT.Exp).then_inc(exped, 1)
                act.sem_inc(gate_copied, 2)
                with act.Fori(0, G) as g:
                    for i in range(GT):
                        t = g * GT + i
                        if i == 0:
                            act.wait_ge(bias_added, g * GT + 1)
                        act.wait_ge(gate_turned, t + 1 + GT)
                        act.activation(gate_t[:, i, :], turned_ps[0:ne, i % 2, 0:P], ACT.Copy).then_inc(gate_copied, 1)


PIECES = ((0, 320), (320, GN - 320))


def hidden_pieces(layers):
    return sum(-(-l["out"] // 128) for l in layers) * len(PIECES)


class Expert:

    def __init__(self, env, layers, w_last, k_last, ring, s):
        self.env, self.layers, self.w_last, self.k_last, self.ring, self.s = env, layers, w_last, k_last, ring, s
        self.pieces = hidden_pieces(layers)

    def tensor(self, pe, x_cols, first, tiles, hidden_ps, out_ps, offset=0):
        s, j, before = self.s, 0, 0
        for n, layer in enumerate(self.layers):
            for c, (lo, size) in enumerate(PIECES):
                for m in range(-(-layer["out"] // 128)):
                    rows = min(128, layer["out"] - m * 128)
                    pe.wait_ge(s.activated, first + (j + 1))
                    if n and m == 0:
                        pe.wait_ge(s.activated, first + (before + (c + 1) * (before_per) + self.ring))
                    kc = -(-layer["in"] // 128)
                    for k in range(kc):
                        kr = min(128, layer["in"] - k * 128)
                        rhs = x_cols(k, lo, size) if n == 0 else self.layers[n - 1]["h"][0:kr, k, lo:lo + size]
                        mm = pe.matmul(hidden_ps[0:rows, (offset + j) % self.ring, 0:size],
                                       layer["w"][0:kr, k, m * 128:m * 128 + rows], rhs, start=k == 0, stop=k == kc - 1)
                    mm.then_inc(s.multiplied, 1)
                    j += 1
            before_per = -(-layer["out"] // 128)
            before = j - before_per * len(PIECES)
        last = self.layers[-1]
        for i in range(GT):
            if i == 0:
                pe.wait_ge(s.activated, first + (before + before_per + self.ring))
            if i == 2:
                pe.wait_ge(s.activated, first + (before + 2 * before_per + self.ring))
            gap = {0: 1, 4: 4}.get(i, 5)
            pe.wait_ge(s.mixed, tiles + (i + 1 - gap + 5))
            kc = -(-last["out"] // 128)
            for k in range(kc):
                kr = min(128, last["out"] - k * 128)
                mm = pe.matmul(out_ps[0:P, i % 4, 0:D], last["h"][0:kr, k, i * P:(i + 1) * P],
                               self.w_last[0:kr, k, :], start=k == 0, stop=k == kc - 1)
            mm.then_inc(s.finished, 1)

    def scalar(self, act, column, first, hidden_ps, offset=0):
        s, j = self.s, 0
        for n, layer in enumerate(self.layers):
            for c, (lo, size) in enumerate(PIECES):
                for m in range(-(-layer["out"] // 128)):
                    rows = min(128, layer["out"] - m * 128)
                    act.wait_ge(s.multiplied, first + (j + 1))
                    act.sem_inc(s.hold, 1)
                    scale = layer["scale"](column, m, rows) if layer.get("scale") else 1.0
                    act.activation(layer["h"][0:rows, m, lo:lo + size], hidden_ps[0:rows, (offset + j) % self.ring, 0:size],
                                   layer["func"], bias=layer["bias"](column, m, rows), scale=scale).then_inc(s.activated, 1)
                    j += 1

    def vector(self, v, gate, tiles, g, out_ps):
        for i in range(GT):
            t = g * GT + i
            x_t = self.env.x[:, ds(t, 1), :].rearrange("p o d -> p (o d)")
            v.wait_ge(self.s.finished, tiles + (i + 1))
            v.scalar_tensor_tensor(out=x_t, in0=out_ps[0:P, i % 4, 0:D], scalar=gate(t), in1=x_t, op0=ALU.mult,
                                   op1=ALU.add).then_inc(self.s.mixed, 1)


def experts_phase(env, kind):
    nc = env.nc
    ph = Phase(env)
    a = env.a
    ne = 8
    hidden = 1024 if kind == "L1" else D
    hc = hidden // 128
    n_hidden = 2 if kind == "L2" else 1
    ring = 4
    with ExitStack() as st:
        names = {"L0": ["L0_ffn_w1", "L0_ffn_w2"], "L1": ["L1_ffn_W1", "L1_ffn_W2"],
                 "L2": ["L2_ffn_W1", "L2_ffn_W2", "L2_ffn_Wo"]}[kind]
        w_slots = []
        for s in range(2):
            ws = [sb(env, st, f"w{s}_0", [128, K2, hidden])]
            if n_hidden == 2:
                ws.append(sb(env, st, f"w{s}_1", [128, hc, hidden]))
            ws.append(sb(env, st, f"w{s}_last", [128, hc, D]))
            w_slots.append(ws)
        hs = [sb(env, st, f"h{n}", [128, hc, GN]) for n in range(n_hidden)]
        cols = ne * hc
        if kind == "L2":
            raw = {p: sb(env, st, f"raw_{p}", [128, cols]) for p in ("b1", "g1", "be1", "m1", "v1", "b2", "g2", "be2", "m2", "v2")}
            eps = sb(env, st, "eps", [128, 1])
        else:
            raw = {"b1": sb(env, st, "raw_b1", [128, cols])}
        if kind == "L1":
            raw["ln_g"] = sb(env, st, "raw_ln_g", [128, ne * K2])
            raw["ln_b"] = sb(env, st, "raw_ln_b", [128, ne * K2])
            x_e = sb(env, st, "x_e", [128, K2, GN])
        hidden_ps = ps(env, st, "hidden_ps", [128, ring, 512])
        out_ps = ps(env, st, "out_ps", [128, 4, 512])
        sems = ExpertSems(ph)
        w_landed = [ph.sem(), ph.sem()]
        params_landed, rooted, folded, shifted, pe_hold = [ph.sem() for _ in range(5)]
        func = ACT.Relu if kind == "L2" else ACT.Gelu

        def column(which):
            return lambda e, m, rows: raw[which][:, ds(e * hc + m, 1)]

        experts = []
        for s in range(2):
            layers = []
            for n in range(n_hidden):
                layers.append({"in": D, "out": hidden, "w": w_slots[s][n], "h": hs[n], "func": func,
                               "bias": column(f"b{n + 1}"), "scale": column(f"g{n + 1}") if kind == "L2" else None})
            experts.append(Expert(env, layers, w_slots[s][-1], hc, ring, sems))
        pieces = experts[0].pieces
        with nc.Block() as block:

            @block.sync
            def _(sp):
                ph.clear_other()
                for p, tile in raw.items():
                    sp.dma_start(tile[:], a[f"{kind}_ffn_{p}"]).then_inc(params_landed, 16)
                with sp.Fori(0, ne // 2) as pair:
                    for s in range(2):
                        e = pair * 2 + s
                        sp.wait_ge(sems.finished, (e + 1) * (G * GT))
                        for n, name in enumerate(names):
                            sp.dma_start(w_slots[s][n][:], a[name][ds(e, 1), :, :].rearrange("o (k p) n -> p (o k) n", p=128)).then_inc(w_landed[s], 16)
                sp.wait_ge(w_landed[0], 16 * len(names) * (ne // 2))
                sp.wait_ge(w_landed[1], 16 * len(names) * (ne // 2))

            @block.tensor
            def _(pe):
                pe.sem_inc(sems.finished, 2 * G * GT)
                with pe.Fori(0, ne // 2) as pair:
                    for s in range(2):
                        pe.wait_ge(w_landed[s], (pair + 1) * (16 * len(names)))
                        pe.sem_inc(pe_hold, 1)
                        with pe.Fori(0, G) as g:
                            unit = pair * (2 * G) + (s * G + g)
                            if kind == "L1":
                                pe.wait_ge(shifted, unit + 1)

                                def x_cols(k, lo, size):
                                    return x_e[:, k, lo:lo + size]
                            else:
                                def x_cols(k, lo, size):
                                    return env.x_t[:, k, ds(g * GN + lo, size)]
                            experts[s].tensor(pe, x_cols, unit * pieces, unit * GT, hidden_ps, out_ps)

            @block.scalar
            def _(act):
                act.wait_ge(params_landed, 16 * len(raw))
                act.sem_inc(sems.activated, ring)
                if kind == "L2":
                    act.wait_ge(folded, 1)
                    act.activation(raw["v1"][:], raw["v1"][:], ACT.Sqrt, bias=eps[:]).then_inc(rooted, 1)
                    act.activation(raw["v2"][:], raw["v2"][:], ACT.Sqrt, bias=eps[:]).then_inc(rooted, 1)
                    act.wait_ge(folded, 11)
                with act.Fori(0, ne // 2) as pair:
                    for s in range(2):
                        with act.Fori(0, G) as g:
                            unit = pair * (2 * G) + (s * G + g)
                            e = pair * 2 + s
                            if kind == "L1":
                                for k in range(K2):
                                    ins = act.activation(x_e[:, k, :], env.x_t[:, k, ds(g * GN, GN)], ACT.Identity,
                                                         bias=raw["ln_b"][:, ds(e * K2 + k, 1)],
                                                         scale=raw["ln_g"][:, ds(e * K2 + k, 1)])
                                ins.then_inc(shifted, 1)
                            experts[s].scalar(act, e, unit * pieces, hidden_ps)

            @block.vector
            def _(v):
                v.sem_inc(sems.mixed, 5)
                if kind == "L2":
                    v.memset(eps[:], 1e-3).then_inc(folded, 1)
                    v.wait_ge(rooted, 2)
                    n = 1
                    for j in "12":
                        for ins in (lambda: v.reciprocal(raw["v" + j][:], raw["v" + j][:]),
                                    lambda: v.tensor_tensor(raw["g" + j][:], raw["g" + j][:], raw["v" + j][:], ALU.mult),
                                    lambda: v.tensor_tensor(raw["b" + j][:], raw["b" + j][:], raw["m" + j][:], ALU.subtract),
                                    lambda: v.tensor_tensor(raw["b" + j][:], raw["b" + j][:], raw["g" + j][:], ALU.mult),
                                    lambda: v.tensor_tensor(raw["b" + j][:], raw["b" + j][:], raw["be" + j][:], ALU.add)):
                            ins().then_inc(folded, 1)
                            n += 1
                            v.wait_ge(folded, n)
                with v.Fori(0, ne // 2) as pair:
                    for s in range(2):
                        with v.Fori(0, G) as g:
                            unit = pair * (2 * G) + (s * G + g)
                            e = pair * 2 + s
                            experts[s].vector(v, lambda t: env.gates[:, ds(t, 1), ds(e, 1)].rearrange("p o e -> p (o e)"),
                                              unit * GT + 2 * G * GT, g, out_ps)


def gather_sum_phase(env, table, index_of_visit, key_of_edge, tile_of_visit, tiles, sums, rows, visits):
    nc = env.nc
    ph = Phase(env)
    batches = visits // VB
    with ExitStack() as st:
        gather = Gather(env, st, ph, table, index_of_visit, batches)
        hit = sb(env, st, "hit", [128, SLOTS, VB, rows])
        sum_ps = ps(env, st, "sum_ps", [128, SLOTS, VB, D])
        cleared, hits_made, summed = [ph.sem() for _ in range(3)]
        with nc.Block() as block:

            @block.sync
            def _(sp):
                ph.clear_other()

            @block.gpsimd
            def _(pool):
                pool.memset(sums[:], 0.0).then_inc(cleared, 1)
                gather.gpsimd(pool)

            @block.scalar
            def _(act):
                batch_loop(act, batches, 0, lambda k, slot, lap: gather.scalar(act, k, slot))

            @block.vector
            def _(v):
                v.wait_ge(cleared, 1)
                v.sem_inc(summed, SLOTS * VB)
                for k in range(2):
                    make_hits(v, env, hit[:, k], key_of_edge, rows, k).then_inc(hits_made, 1)

                def one_batch(k, slot, lap):
                    make_hits(v, env, hit[:, (slot + 2) % SLOTS], key_of_edge, rows, k + 2).then_inc(hits_made, 1)
                    v.wait_ge(gather.freed, k + (1 + SLOTS))
                    for i in range(VB):
                        tile = v.value_load(tile_of_visit[0:1, ds(k * VB + i, 1)], min_val=0, max_val=tiles - 1)
                        v.wait_ge(summed, k * VB + (i + SLOTS * VB))
                        here = sums[:, ds(tile, 1), :].rearrange("p o c -> p (o c)")
                        v.tensor_tensor(here, here, sum_ps[0:rows, slot, i, :], ALU.add).then_inc(summed, 1)

                batch_loop(v, batches, 0, one_batch)

            @block.tensor
            def _(pe):
                pe.sem_inc(gather.freed, SLOTS)

                def one_batch(k, slot, lap):
                    pe.wait_ge(hits_made, k + 1)
                    pe.wait_ge(summed, k * VB + VB)
                    gather.wait(pe, slot, lap)
                    for i in range(VB):
                        mm = pe.matmul(sum_ps[0:rows, slot, i, :], hit[:, slot, i, 0:rows], gather.rows[:, slot, i, :],
                                       start=True, stop=True)
                    mm.then_inc(gather.freed, 1)

                batch_loop(pe, batches, 0, one_batch)


def move_phase(env, to_dram):
    ph = Phase(env)
    moved = ph.sem()
    with env.nc.Block() as block:

        @block.sync
        def _(sp):
            ph.clear_other()
            rows = env.x_table.rearrange("(t p) d -> p t d", p=P)
            if to_dram:
                sp.dma_start(rows, env.x[:]).then_inc(moved, 16)
            else:
                sp.dma_start(env.x[:], rows).then_inc(moved, 16)
            sp.wait_ge(moved, 16)


WB = 2
NWP = round_up(NW, 2 * WB)


def relation_attention_phase(env):
    nc = env.nc
    ph = Phase(env)
    a = env.a
    M = WB * WR
    batches = NWP // WB
    with ExitStack() as st:
        w_sb = sb(env, st, "w_sb", [128, K2, 3 * D])
        bias_col = sb(env, st, "bias_col", [128, 3 * D // 128])
        v_bias = sb(env, st, "v_bias", [WR, D])
        other = sb(env, st, "other", [WR, WR])
        share = sb(env, st, "share", [WR, WN])
        s_rows = sb(env, st, "s_rows", [WR, WB, D])
        s_t = sb(env, st, "s_t", [128, K2, M])
        qk_t = sb(env, st, "qk_t", [128, 4, M])
        v_sb = sb(env, st, "v_sb", [WR, 2, WB, D])
        score = sb(env, st, "score", [WR, 2, WB * HEADS, WR])
        top = sb(env, st, "top", [WR, WB * HEADS])
        total = sb(env, st, "total", [WR, WB * HEADS])
        chooser = sb(env, st, "chooser", [WR, WB * HEADS, WN])
        weight = sb(env, st, "weight", [WR, WB * HEADS * WN])
        o_rows = sb(env, st, "o_rows", [WN, WB, D])
        turn_ps = ps(env, st, "turn_ps", [128, 512])
        qk_ps = ps(env, st, "qk_ps", [128, 2, 512])
        v_ps = ps(env, st, "v_ps", [128, 512])
        score_ps = ps(env, st, "score_ps", [128, WB, 512])
        weight_ps = ps(env, st, "weight_ps", [128, 512])
        o_ps = ps(env, st, "o_ps", [128, 512])
        landed, taken, turned, turned_copied, projected, qk_out, v_out = [ph.sem() for _ in range(7)]
        scored, masked, topped, lowered, exped, summed, inverted, chosen = [ph.sem() for _ in range(8)]
        weighed, weights_out, attended, o_out, stored, hold = [ph.sem() for _ in range(6)]
        with nc.Block() as block:

            @block.sync
            def _(sp):
                ph.clear_other()
                sp.dma_start(w_sb[:], a["L1_gnn_in_proj_w"].rearrange("(k p) n -> p k n", p=128)).then_inc(landed, 16)
                sp.dma_start(bias_col[:], a["L1_gnn_in_proj_b"]).then_inc(landed, 16)
                sp.dma_start(v_bias[:], env.row("in_proj_b_row")[:, 2 * D:3 * D].to_broadcast([WR, D])).then_inc(landed, 16)
                sp.dma_start(other[:], a["other_node"]).then_inc(landed, 16)
                sp.dma_start(share[:], a["node_share"]).then_inc(landed, 16)
                sp.sem_inc(stored, 1)
                with sp.Fori(0, batches) as k:
                    sp.wait_ge(o_out, k + 1 + 1)
                    sp.dma_start(env.o_table[ds(k * (WB * WN), WB * WN), :].rearrange("(j n) d -> n j d", n=WN),
                                 o_rows[:]).then_inc(stored, 16)
                sp.wait_ge(stored, 16 * batches + 1)

            @block.gpsimd
            def _(pool):
                def take(k):
                    pool.wait_ge(turned, k + 1)
                    pool.sem_inc(hold, 1)
                    pool.tensor_copy(s_rows[:], env.window_sums[:, ds(k * WB, WB), :]).then_inc(taken, 1)

                take(0)
                with pool.Fori(0, batches - 1) as k:
                    take(k + 1)
                pool.wait_ge(turned, batches + 1)
                pool.sem_inc(taken, 1)

            @block.tensor
            def _(pe):
                pe.sem_inc(turned, 1)
                pe.sem_inc(weighed, 2)
                pe.wait_ge(landed, 80)

                def turn(k):
                    pe.wait_ge(taken, k + 1)
                    pe.wait_ge(turned_copied, k + 1)
                    for c in range(K2):
                        for j in range(WB):
                            mm = pe.transpose(turn_ps[:, (c * WB + j) * WR:(c * WB + j + 1) * WR],
                                              s_rows[:, j, c * 128:(c + 1) * 128], env.ident[0:WR, 0:WR])
                    mm.then_inc(turned, 1)

                def project(k):
                    pe.wait_ge(turned_copied, k + 1 + 1)
                    pe.wait_ge(qk_out, k + 1)
                    pe.wait_ge(v_out, k + 1)
                    for m in range(4):
                        for c in range(K2):
                            pe.matmul(qk_ps[:, m // 2, (m % 2) * M:(m % 2 + 1) * M], w_sb[:, c, m * 128:(m + 1) * 128],
                                      s_t[:, c, :], start=c == 0, stop=c == K2 - 1)
                    for j in range(WB):
                        for c in range(K2):
                            mm = pe.matmul(v_ps[0:WR, j * D:(j + 1) * D], s_t[:, c, j * WR:(j + 1) * WR],
                                           w_sb[:, c, 2 * D:3 * D], start=c == 0, stop=c == K2 - 1)
                    mm.then_inc(projected, 1)

                turn(0)
                project(0)

                def attend(k, b):
                    pe.wait_ge(chosen, k + 1)
                    pe.wait_ge(weights_out, k + 1)
                    for n in range(WB * HEADS):
                        mm = pe.matmul(weight_ps[0:WR, n * WN:(n + 1) * WN], score[:, b, n, :], chooser[:, n, :],
                                       start=True, stop=True)
                    mm.then_inc(weighed, 1)

                def mean(k, b):
                    pe.wait_ge(weights_out, k + 1 + 1)
                    pe.wait_ge(o_out, k + 1)
                    for n in range(WB * HEADS):
                        j, h = n // 2 % WB, n % 2 * 2 + n // (2 * WB)
                        mm = pe.matmul(o_ps[0:WN, j * D + h * HD:j * D + (h + 1) * HD],
                                       weight[:, n * WN:(n + 1) * WN], v_sb[:, b, j, h * HD:(h + 1) * HD],
                                       start=True, stop=True)
                    mm.then_inc(attended, 1)

                def step(k, b, before):
                    pe.wait_ge(qk_out, k + 1 + 1)
                    pe.wait_ge(masked, k + 1)
                    for j in range(WB):
                        for h in range(HEADS):
                            f = slice((h % 2) * HD, (h % 2 + 1) * HD)
                            n = slice(j * WR, (j + 1) * WR)
                            at = (j * 2 + h // 2) * WR
                            mm = pe.matmul(score_ps[0:WR, h % 2, at:at + WR], qk_t[f, h // 2, n],
                                           qk_t[f, 2 + h // 2, n], start=True, stop=True)
                    mm.then_inc(scored, 1)
                    if before:
                        attend(k - 1, 1 - b)
                    turn(k + 1)
                    if before:
                        mean(k - 1, 1 - b)
                    project(k + 1)

                step(0, 0, False)
                step(1, 1, True)
                with pe.Fori(1, batches // 2) as it:
                    for b in range(2):
                        step(it * 2 + b, b, True)
                attend(batches - 1, 1)
                mean(batches - 1, 1)

            @block.scalar
            def _(act):
                act.wait_ge(landed, 80)
                act.sem_inc(turned_copied, 1)
                act.sem_inc(qk_out, 1)
                act.sem_inc(weights_out, 1)
                act.sem_inc(o_out, 1)

                def copy_turned(k):
                    act.wait_ge(projected, k) if not isinstance(k, int) else None
                    act.wait_ge(turned, k + 1 + 1)
                    act.activation(s_t[:].rearrange("p c n -> p (c n)"), turn_ps[:, 0:K2 * M], ACT.Copy).then_inc(turned_copied, 1)

                def qk(k):
                    act.wait_ge(scored, k) if not isinstance(k, int) else None
                    act.wait_ge(projected, k + 1)
                    for m in range(4):
                        ins = act.activation(qk_t[:, m, :], qk_ps[:, m // 2, (m % 2) * M:(m % 2 + 1) * M], ACT.Identity,
                                             bias=bias_col[:, m:m + 1])
                    ins.then_inc(qk_out, 1)

                copy_turned(0)
                qk(0)

                def weights(k):
                    act.wait_ge(weighed, k + 1 + 2)
                    act.activation(weight[:], weight_ps[0:WR, 0:WB * HEADS * WN], ACT.Copy).then_inc(weights_out, 1)

                def out(k):
                    act.wait_ge(attended, k + 1)
                    act.wait_ge(stored, k * 16 + 1)
                    act.activation(o_rows[:].rearrange("p j d -> p (j d)"), o_ps[0:WN, 0:WB * D], ACT.Copy).then_inc(o_out, 1)

                def step(k, b, before):
                    if before:
                        weights(k - 1)
                    copy_turned(k + 1)
                    if before:
                        out(k - 1)
                    act.wait_ge(lowered, k + 1)
                    act.activation(score[:, b], score[:, b], ACT.Exp, scale=HD ** -0.5).then_inc(exped, 1)
                    qk(k + 1)

                step(0, 0, False)
                step(1, 1, True)
                with act.Fori(1, batches // 2) as it:
                    for b in range(2):
                        step(it * 2 + b, b, True)
                weights(batches - 1)
                out(batches - 1)

            @block.vector
            def _(v):
                v.wait_ge(landed, 80)
                v.sem_inc(v_out, 1)
                v.sem_inc(masked, 1)

                def values(b, k):
                    v.wait_ge(projected, k + 1)
                    v.tensor_tensor(v_sb[:, b], v_ps[0:WR].rearrange("p (j d) -> p j d", j=WB),
                                    v_bias[:].unsqueeze(1).to_broadcast([WR, WB, D]), ALU.add).then_inc(v_out, 1)

                values(0, 0)
                with v.Fori(0, batches // 2) as it:
                    for b in range(2):
                        k = it * 2 + b
                        v.wait_ge(scored, k + 1)
                        v.wait_ge(weighed, k + 1)
                        v.tensor_tensor(score[:, b].rearrange("p (u j) n -> p u j n", u=2),
                                        score_ps[0:WR, :, 0:HEADS * WR].rearrange("p u (j n) -> p u j n", j=HEADS),
                                        other[:].unsqueeze(1).unsqueeze(1).to_broadcast([WR, 2, HEADS, WR]),
                                        ALU.add).then_inc(masked, 1)
                        v.wait_ge(masked, k + 1 + 1)
                        v.tensor_reduce(top[:], score[:, b], AX.X, ALU.max).then_inc(topped, 1)
                        v.wait_ge(topped, k + 1)
                        v.tensor_tensor(score[:, b], score[:, b], top[:].unsqueeze(2).to_broadcast([WR, WB * HEADS, WR]),
                                        ALU.subtract).then_inc(lowered, 1)
                        v.wait_ge(exped, k + 1)
                        v.tensor_reduce(total[:], score[:, b], AX.X, ALU.add).then_inc(summed, 1)
                        v.wait_ge(summed, k + 1)
                        v.reciprocal(total[:], total[:]).then_inc(inverted, 1)
                        v.wait_ge(inverted, k + 1)
                        v.wait_ge(weighed, k + 1 + 1)
                        v.tensor_tensor(chooser[:], share[:].unsqueeze(1).to_broadcast([WR, WB * HEADS, WN]),
                                        total[:].unsqueeze(2).to_broadcast([WR, WB * HEADS, WN]), ALU.mult).then_inc(chosen, 1)
                        values(1 - b, k + 1)


def relation_output_phase(env):
    nc = env.nc
    ph = Phase(env)
    a = env.a
    with ExitStack() as st:
        out_w = sb(env, st, "out_w", [128, K2, D])
        proj_w = sb(env, st, "proj_w", [128, K2, D])
        out_b = sb(env, st, "out_b", [128, K2])
        proj_bc = sb(env, st, "proj_bc", [P, D])
        normed = sb(env, st, "normed", [P, GT, D])
        o_rows = sb(env, st, "o_rows", [P, GT, D])
        o_t = sb(env, st, "o_t", [128, GT, K2 * P])
        h_t = sb(env, st, "h_t", [128, GT, K2 * P])
        turn_ps = ps(env, st, "turn_ps", [128, 2, 512])
        h_ps = ps(env, st, "h_ps", [128, 2, 512])
        y_ps = ps(env, st, "y_ps", [128, 2, 512])
        w_landed, turned, turned_copied, mixed, h_out, projected, added, biased, normed_made = [ph.sem() for _ in range(9)]
        o_landed = [ph.sem() for _ in range(GT)]
        with nc.Block() as block:

            @block.sync
            def _(sp):
                ph.clear_other()
                sp.dma_start(out_w[:], a["L1_gnn_attn_out_w"].rearrange("(k p) n -> p k n", p=128)).then_inc(w_landed, 16)
                sp.dma_start(proj_w[:], a["L1_gnn_proj_w"].rearrange("(k p) n -> p k n", p=128)).then_inc(w_landed, 16)
                sp.dma_start(out_b[:], a["L1_gnn_attn_out_b"]).then_inc(w_landed, 16)
                sp.dma_start(proj_bc[:], env.row("L1_gnn_proj_b").to_broadcast([P, D])).then_inc(w_landed, 16)
                with sp.Fori(0, G) as g:
                    for i in range(GT):
                        t = g * GT + i
                        sp.wait_ge(turned, t + 1)
                        sp.dma_start(o_rows[:, i, :], env.o_table[ds(t * P, P), :]).then_inc(o_landed[i], 16)
                for i in range(GT):
                    sp.wait_ge(o_landed[i], 16 * G)

            @block.vector
            def _(v):
                v.wait_ge(w_landed, 64)
                v.sem_inc(added, 2)
                with v.Fori(0, G) as g:
                    for i in range(GT):
                        t = g * GT + i
                        x_t = env.x[:, ds(t, 1), :].rearrange("p o d -> p (o d)")
                        v.wait_ge(mixed, t + 1)
                        v.tensor_scalar(normed[:, i, :], x_t, env.mean[:, ds(t, 1)], env.rstd[:, ds(t, 1)],
                                        ALU.subtract, ALU.mult).then_inc(normed_made, 1)
                    for i in range(GT):
                        t = g * GT + i
                        x_t = env.x[:, ds(t, 1), :].rearrange("p o d -> p (o d)")
                        v.tensor_tensor(x_t, x_t, proj_bc[:], ALU.add).then_inc(biased, 1)
                        v.wait_ge(biased, t + 1)
                        v.wait_ge(projected, t + 1 + GT)
                        v.tensor_tensor(x_t, y_ps[0:P, i % 2, 0:D], x_t, ALU.add).then_inc(added, 1)

            @block.tensor
            def _(pe):
                pe.sem_inc(turned, GT)
                pe.sem_inc(mixed, GT)
                pe.sem_inc(projected, GT)
                pe.wait_ge(w_landed, 64)
                with pe.Fori(0, G) as g:
                    for i in range(GT):
                        t = g * GT + i
                        pe.wait_ge(o_landed[i], (g + 1) * 16)
                        pe.wait_ge(turned_copied, t + (1 + (i == 0)))
                        for k in range(K2):
                            mm = pe.transpose(turn_ps[:, i % 2, k * P:(k + 1) * P], o_rows[:, i, k * 128:(k + 1) * 128],
                                              env.ident[0:P, 0:P])
                        mm.then_inc(turned, 1)
                    for i in range(GT):
                        t = g * GT + i
                        pe.wait_ge(turned_copied, t + 1 + 2)
                        pe.wait_ge(normed_made, t + 1)
                        pe.wait_ge(h_out, t + (1 + (i == 0)))
                        for m in range(K2):
                            out = h_ps[:, i % 2, m * P:(m + 1) * P]
                            for k in range(K2):
                                pe.matmul(out, out_w[:, k, m * 128:(m + 1) * 128], o_t[:, i, k * P:(k + 1) * P],
                                          start=k == 0, stop=False)
                            mm = pe.matmul(out, normed[:, i, m * 128:(m + 1) * 128], env.ident[0:P, 0:P],
                                           start=False, stop=True)
                        mm.then_inc(mixed, 1)
                    for i in range(GT):
                        t = g * GT + i
                        pe.wait_ge(h_out, t + 1 + 2)
                        pe.wait_ge(added, t + (1 + (i == 0)))
                        for k in range(K2):
                            mm = pe.matmul(y_ps[0:P, i % 2, 0:D], h_t[:, i, k * P:(k + 1) * P], proj_w[:, k, :],
                                           start=k == 0, stop=k == K2 - 1)
                        mm.then_inc(projected, 1)

            @block.scalar
            def _(act):
                act.wait_ge(w_landed, 64)
                act.sem_inc(turned_copied, 2)
                act.sem_inc(h_out, 2)
                with act.Fori(0, G) as g:
                    for i in range(GT):
                        t = g * GT + i
                        act.wait_ge(mixed, t + 1)
                        act.wait_ge(turned, t + 1 + GT)
                        act.activation(o_t[:, i, :], turn_ps[:, i % 2, 0:K2 * P], ACT.Copy).then_inc(turned_copied, 1)
                    for i in range(GT):
                        t = g * GT + i
                        act.wait_ge(projected, t + 1)
                        act.wait_ge(mixed, t + 1 + GT)
                        for m in range(K2):
                            ins = act.activation(h_t[:, i, m * P:(m + 1) * P], h_ps[:, i % 2, m * P:(m + 1) * P],
                                                 ACT.Identity, bias=out_b[:, m:m + 1])
                        ins.then_inc(h_out, 1)


def spread_phase(env, kind):
    nc = env.nc
    ph = Phase(env)
    with ExitStack() as st:
        own = sb(env, st, "own", [P, T, D]) if kind == "L3" else None
        bias_bc = sb(env, st, "bias_bc", [P, D])
        landed, step = ph.sem(), ph.sem()
        with nc.Block() as block:

            @block.sync
            def _(sp):
                ph.clear_other()
                if kind == "L3":
                    sp.dma_start(own[:], env.k_table.rearrange("(t p) d -> p t d", p=P)).then_inc(landed, 16)
                    sp.dma_start(bias_bc[:], env.row("L3_gnn_b").to_broadcast([P, D])).then_inc(landed, 16)

            @block.vector
            def _(v):
                n = [0]

                def done(ins):
                    n[0] += 1
                    ins.then_inc(step, 1)
                    v.wait_ge(step, n[0])

                y, x = env.node_sums[:], env.x[:]
                scale = (env.norm2 if kind == "L2" else env.norm3)[:].unsqueeze(2).to_broadcast([P, T, D])
                if kind == "L3":
                    v.wait_ge(landed, 32)
                    done(v.tensor_tensor(y, y, own[:], ALU.add))
                done(v.tensor_tensor(y, y, scale, ALU.mult))
                if kind == "L3":
                    done(v.tensor_tensor(y, y, bias_bc[:].unsqueeze(1).to_broadcast([P, T, D]), ALU.add))
                    done(v.scalar_tensor_tensor(out=y, in0=y, scalar=0.2, in1=y, op0=ALU.mult, op1=ALU.max))
                done(v.tensor_tensor(x, x, y, ALU.add))


def small_experts_phase(env):
    nc = env.nc
    ph = Phase(env)
    a = env.a
    ring = 2
    with ExitStack() as st:
        sizes = [("s", None, 256, 128)] + [("e", e, 128, 64) for e in range(4)]
        sems = ExpertSems(ph)
        landed = ph.sem()
        hidden_ps = ps(env, st, "hidden_ps", [128, ring, 512])
        out_ps = ps(env, st, "out_ps", [128, 4, 512])
        h1 = sb(env, st, "h1", [128, 2, GN])
        h2 = sb(env, st, "h2", [128, 1, GN])
        bias = {"sb1": sb(env, st, "sb1", [128, 2]), "sb2": sb(env, st, "sb2", [128, 1]),
                "eb1": sb(env, st, "eb1", [128, 4]), "eb2": sb(env, st, "eb2", [64, 4])}
        loads, experts = [(tile, a[f"L3_ffn_{p}"]) for p, tile in bias.items()], []
        for which, e, d1, d2 in sizes:
            w1 = sb(env, st, f"w1_{which}{e}", [128, K2, d1])
            w2 = sb(env, st, f"w2_{which}{e}", [128, d1 // 128, d2])
            w3 = sb(env, st, f"w3_{which}{e}", [d2, 1, D])
            for j, tile in enumerate((w1, w2, w3)):
                src = a[f"L3_ffn_{which}W{j + 1}"]
                src = src if e is None else src[e]
                loads.append((tile, src.rearrange("(k p) n -> p k n", p=min(128, src.shape[0]))))
            def cols(b, first):
                return lambda g, m, rows: bias[b][0:rows, first + m:first + m + 1]
            experts.append(Expert(env, [
                {"in": D, "out": d1, "w": w1, "h": h1, "func": ACT.Relu, "bias": cols(which + "b1", e or 0)},
                {"in": d1, "out": d2, "w": w2, "h": h2, "func": ACT.Relu, "bias": cols(which + "b2", e or 0)},
            ], w3, 1, ring, sems))
        total = sum(x.pieces for x in experts)
        firsts = [sum(x.pieces for x in experts[:n]) for n in range(len(experts))]
        with nc.Block() as block:

            @block.sync
            def _(sp):
                ph.clear_other()
                for tile, src in loads:
                    sp.dma_start(tile[:], src).then_inc(landed, 16)

            @block.tensor
            def _(pe):
                pe.wait_ge(landed, 16 * len(loads))
                with pe.Fori(0, G) as g:
                    for n, x in enumerate(experts):
                        x.tensor(pe, lambda k, lo, size: env.x_t[:, k, ds(g * GN + lo, size)], g * total + firsts[n],
                                 g * (5 * GT) + n * GT, hidden_ps, out_ps, firsts[n])

            @block.scalar
            def _(act):
                act.wait_ge(landed, 16 * len(loads))
                act.sem_inc(sems.activated, ring)
                with act.Fori(0, G) as g:
                    for n, x in enumerate(experts):
                        x.scalar(act, g, g * total + firsts[n], hidden_ps, firsts[n])

            @block.vector
            def _(v):
                v.sem_inc(sems.mixed, 5)
                with v.Fori(0, G) as g:
                    for n, x in enumerate(experts):
                        x.vector(v, lambda t: env.ones[0:P, 0:1] if n == 0 else
                                 env.gates[:, ds(t, 1), n - 1:n].rearrange("p o e -> p (o e)"),
                                 g * (5 * GT) + n * GT, g, out_ps)


def build(nc, a, out, stop=99):
    env = Env(nc, a, out)
    with ExitStack() as st:
        env.sem_sets = [[st.enter_context(nc.semaphore(f"set{s}_{i}")) for i in range(24)] for s in range(2)]
        env.gathered = [st.enter_context(nc.semaphore(f"gathered_{s}")) for s in range(SLOTS)]
        env.gathered_base = [0] * SLOTS
        env.mean = sb(env, st, "mean", [P, T])
        env.rstd = sb(env, st, "rstd", [P, T])
        env.mean2 = sb(env, st, "mean2", [P, T])
        env.rstd2 = sb(env, st, "rstd2", [P, T])
        env.norm2 = sb(env, st, "norm2", [P, T])
        env.norm3 = sb(env, st, "norm3", [P, T])
        env.ident = sb(env, st, "ident", [128, 128])
        env.ones = sb(env, st, "ones", [128, 128])
        env.iota = sb(env, st, "iota", [128, VW_PAD])
        env.part = sb(env, st, "part", [128, 1])
        env.tile_of_visit = sb(env, st, "tile_of_visit", [1, VT_PAD], I32)
        env.window_of_visit = sb(env, st, "window_of_visit", [1, VW_PAD], I32)
        env.src_of_visit = sb(env, st, "src_of_visit", [128, VT_PAD], I32)
        env.message_of_visit = sb(env, st, "message_of_visit", [128, VW_PAD], I32)
        env.rel_dst = sb(env, st, "rel_dst", [128, VT_PAD])
        env.type64 = sb(env, st, "type64", [128, VT_PAD])
        env.row_of_edge = sb(env, st, "row_of_edge", [128, VW_PAD])
        env.k_table = nc.dram_tensor("k_table", (N, D), F32).ap()
        env.v_table = nc.dram_tensor("v_table", (N, D), F32).ap()
        env.x_table = nc.dram_tensor("x_table", (N, D), F32).ap()
        env.o_table = nc.dram_tensor("o_table", (NWP * WN, D), F32).ap()
        env.messages = nc.dram_tensor("messages", (N * R6, D), F32).ap()

        x_stack = ExitStack()
        env.x = sb(env, x_stack, "x", [P, T, D])
        setup_phase(env, a)
        stats_phase(env, env.x)
        with ExitStack() as l0:
            env.sums = sb(env, l0, "sums", [P, T, VC])
            env.peaks = sb(env, l0, "peaks", [P, T, HEADS])
            env.scores = sb(env, l0, "scores", [128, VT_PAD, HEADS])
            with ExitStack() as sq:
                env.q = sb(env, sq, "q", [P, T, D])
                project_phase(env, a["qkv_w"].rearrange("(k p) n -> p k n", p=128),
                              env.row("qkv_b").to_broadcast([P, 3 * D]), 3 * D, "qkv")
                score_phase(env)
            peak_phase(env)
            attend_phase(env)
            message_phase(env)
            stats_phase(env, env.sums[:, :, 0:D])
            affine_phase(env)
        if stop == 0:
            store_phase(env)
            x_stack.close()
            return
        stats_phase(env, env.x)
        with ExitStack() as f0:
            env.gates = sb(env, f0, "gates", [P, T, 8])
            env.x_t = sb(env, f0, "x_t", [128, K2, N])
            router_phase(env, "L0")
            experts_phase(env, "L0")
        if stop == 1:
            store_phase(env)
            x_stack.close()
            return
        stats_phase(env, env.x)
        project_phase(env, a["L1_gnn_W"].rearrange("(k p) n -> p k n", p=128),
                      env.row("L1_gnn_b").to_broadcast([P, R6 * D]), R6 * D, "plain",
                      env.messages.rearrange("(n r) d -> n (r d)", r=R6))
        move_phase(env, True)
        x_stack.close()
        with ExitStack() as l1:
            env.window_sums = sb(env, l1, "window_sums", [WR, NWP, D])
            gather_sum_phase(env, env.messages, env.message_of_visit, env.row_of_edge, env.window_of_visit, NW,
                             env.window_sums, WR, VW)
            relation_attention_phase(env)
        env.x = sb(env, x_stack, "x", [P, T, D])
        move_phase(env, False)
        relation_output_phase(env)
        if stop == 2:
            store_phase(env)
            x_stack.close()
            return
        stats_phase(env, env.x)
        with ExitStack() as f1:
            env.gates = sb(env, f1, "gates", [P, T, 8])
            env.x_t = sb(env, f1, "x_t", [128, K2, N])
            with ExitStack() as sn:
                env.normed = sb(env, sn, "normed_all", [P, T, D])
                norm_phase(env)
                stats_phase(env, env.normed, env.mean2, env.rstd2)
            router_phase(env, "L1")
            experts_phase(env, "L1")
        if stop == 3:
            store_phase(env)
            x_stack.close()
            return
        stats_phase(env, env.x)
        for kind in ("L2", "L3"):
            with ExitStack() as l2:
                env.node_sums = sb(env, l2, "node_sums", [P, T, D])
                env.scale = env.norm2 if kind == "L2" else env.norm3
                w = a[f"{kind}_gnn_W"].rearrange("(k p) n -> p k n", p=128)
                bias = env.row("L2_gnn_b").to_broadcast([P, D]) if kind == "L2" else None
                project_phase(env, w, bias, D, "scaled", env.k_table)
                gather_sum_phase(env, env.k_table, env.src_of_visit, env.rel_dst, env.tile_of_visit, T,
                                 env.node_sums, P, VT)
                spread_phase(env, kind)
            stats_phase(env, env.x)
            with ExitStack() as f2:
                env.gates = sb(env, f2, "gates", [P, T, 8])
                env.x_t = sb(env, f2, "x_t", [128, K2, N])
                router_phase(env, kind)
                if kind == "L2":
                    experts_phase(env, "L2")
                    stats_phase(env, env.x)
                else:
                    small_experts_phase(env)
        store_phase(env)
        x_stack.close()


def kernel(**inputs):
    import numpy as _np
    import concourse.bacc as _bacc
    from concourse import mybir as _mybir
    from concourse.bass_utils import run_bass_kernel_spmd as _run

    given = {n: _np.ascontiguousarray(v) for n, v in inputs.items()}
    given["qkv_w"] = _np.concatenate([given.pop(f"L0_gnn_W{c}") for c in "qkv"], axis=1)
    given["qkv_b"] = _np.concatenate([given.pop(f"L0_gnn_b{c}") for c in "qkv"])
    for n in ("L1_gnn_in_proj_w", "L1_gnn_attn_out_w", "L1_gnn_proj_w", "L2_gnn_W", "L0_ffn_router_w"):
        given[n] = _np.ascontiguousarray(given[n].T)
    given["L1_gnn_W"] = _np.ascontiguousarray(given["L1_gnn_W"].transpose(1, 0, 2).reshape(D, R6 * D))
    given["L1_gnn_b"] = given["L1_gnn_b"].reshape(-1)
    given["in_proj_b_row"] = given["L1_gnn_in_proj_b"]
    node = _np.arange(WR) % WN
    given["other_node"] = _np.where(node[:, None] == node[None, :], 0.0, -1e30).astype(_np.float32)
    given["node_share"] = _np.where(node[:, None] == _np.arange(WN)[None, :], 1.0 / R6, 0.0).astype(_np.float32)
    given["L0_gnn_query_emb"] = _np.ascontiguousarray(given["L0_gnn_query_emb"].reshape(-1, 128).T)
    for n in ["L1_gnn_in_proj_b", "L1_gnn_attn_out_b", "L0_ffn_b1", "L1_ffn_b1", "L1_ffn_ln_g", "L1_ffn_ln_b", "L3_ffn_sb1", "L3_ffn_sb2", "L3_ffn_eb1"] + [
            f"L2_ffn_{p}{j}" for p in ("b", "g", "be", "m", "v") for j in "12"]:
        given[n] = _np.ascontiguousarray(given[n].reshape(-1, 128).T)
    given["L3_ffn_eb2"] = _np.ascontiguousarray(given["L3_ffn_eb2"].T)
    nc = _bacc.Bacc("TRN2", target_bir_lowering=False, num_devices=1)
    arrays, args = {}, {}
    for n, v in given.items():
        arrays[f"in_{n}"] = v
        args[n] = nc.dram_tensor(f"in_{n}", v.shape, _mybir.dt.from_np(v.dtype), kind="ExternalInput").ap()
    out = nc.dram_tensor("out_0_dram", given["x"].shape, F32, kind="ExternalOutput").ap()
    build(nc, args, out)
    r = _run(nc, [arrays], core_ids=[0])
    return r.results[0]["out_0_dram"]
```

```python
from contextlib import ExitStack

import numpy as np
import concourse.bass as bass
from concourse import mybir

F32 = mybir.dt.float32
I32 = mybir.dt.int32
U32 = mybir.dt.uint32
ALU = mybir.AluOpType
ACT = mybir.ActivationFunctionType
AX = mybir.AxisListType
ds = bass.ds

N = 3125
D = 256
K2 = D // 128
P = 125
T = N // P
G = 5
GT = T // G
GN = GT * P
E = 50000
CH = 128
NQ = 4
CQ = 98
C = NQ * CQ
REAL = -(-E // CH)
HEADS = 4
HD = D // HEADS
R6 = 6
R64 = 64
WN = 20
NW = -(-N // WN)
WR = R6 * WN
VB = 4
FAR = 1000000


class Env:

    def __init__(self, nc, a, out):
        self.nc, self.a, self.out, self.phase = nc, a, out, 0

    def row(self, name):
        return self.a[name].rearrange("(o d) -> o d", o=1)


class ExpertSems:

    def __init__(self, ph):
        self.activated = ph.sem()
        self.multiplied = ph.sem()
        self.finished = ph.sem()
        self.mixed = ph.sem()
        self.hold = ph.sem()


def round_up(a, b):
    return -(-a // b) * b


VT = round_up(REAL + T - 1, VB)
VW = round_up(REAL + NW - 1, VB)
AHEAD = 3
VT_PAD = round_up(VT + AHEAD * VB, 2)
VW_PAD = round_up(VW + AHEAD * VB, 2)
SLOTS = 4


def batch_loop(engine, total, head, block):
    for k in range(head):
        block(k, k % SLOTS, k // SLOTS)
    laps = (total - head) // SLOTS
    with engine.Fori(0, laps) as it:
        for b in range(head, head + SLOTS):
            block(it * SLOTS + b, b % SLOTS, it + b // SLOTS)
    for k in range(head + laps * SLOTS, total):
        block(k, k % SLOTS, k // SLOTS)


def tiles_of_batch(engine, tile_of_visit, k, tiles):
    return [engine.value_load(tile_of_visit[0:1, ds(k * VB + i, 1)], min_val=0, max_val=tiles - 1) for i in range(VB)]


class Gather:

    def __init__(self, env, st, ph, table, index_of_visit, batches):
        self.env, self.table, self.index_of_visit, self.batches = env, table, index_of_visit, batches
        self.index = sb(env, st, "index", [128, SLOTS, VB], I32)
        self.rows = sb(env, st, "gathered_rows", [128, SLOTS, VB, D])
        self.indexed = ph.sem()
        self.freed = ph.sem()
        self.hold = ph.sem()
        self.passed = ph.sem()
        self.base = list(env.gathered_base)
        for s in range(SLOTS):
            env.gathered_base[s] += 16 * VB * len(range(s, batches, SLOTS))

    def scalar(self, act, k, slot):
        act.wait_ge(self.freed, k + 1)
        act.sem_inc(self.hold, 1)
        act.activation(self.index[:, slot, :], self.index_of_visit[:, ds(k * VB, VB)], ACT.Copy).then_inc(self.indexed, 1)

    def gpsimd(self, pool):
        def start(k, slot, lap):
            pool.wait_ge(self.freed, k + 1)
            pool.wait_ge(self.indexed, k + 1)
            pool.sem_inc(self.passed, 1)
            for i in range(VB):
                pool.indirect_dma_start(self.rows[:, slot, i, :], None, self.table, bass.IndirectOffsetOnAxis(
                    self.index[:, slot, i:i + 1], 0)).then_inc(self.env.gathered[slot], 16)

        batch_loop(pool, self.batches, 0, start)

    def wait(self, engine, slot, lap):
        engine.wait_ge(self.env.gathered[slot], lap * (16 * VB) + (self.base[slot] + 16 * VB))


class Phase:

    def __init__(self, env):
        self.env = env
        self.nc = env.nc
        self.set = env.sem_sets[env.phase % 2]
        self.other = env.sem_sets[(env.phase + 1) % 2]
        self.first = env.phase == 0
        self.used = 0
        env.phase += 1

    def sem(self):
        s = self.set[self.used]
        self.used += 1
        return s

    def clear_other(self):
        if not self.first:
            lo = min(s.num for s in self.other)
            hi = max(s.num for s in self.other)
            self.nc.sync.sem_clear(range(lo, hi + 1))


def sb(env, stack, name, shape, dt=F32):
    return stack.enter_context(env.nc.sbuf_tensor(f"{name}_{env.phase}", shape, dt))


def ps(env, stack, name, shape, dt=F32):
    return stack.enter_context(env.nc.psum_tensor(f"{name}_{env.phase}", shape, dt))


def setup_phase(env, a):
    nc = env.nc
    ph = Phase(env)
    with ExitStack() as st:
        rows_i = sb(env, st, "rows_i", [CQ, 4, NQ, CH], I32)
        rows_f = sb(env, st, "rows_f", [CQ, 4, NQ, CH])
        chunk_max = sb(env, st, "chunk_max", [CQ, NQ])
        edges_t = sb(env, st, "edges_t", [CQ, 256])
        before = sb(env, st, "before", [CQ, NQ, 256])
        key = sb(env, st, "key", [128, 2])
        cmp_a = sb(env, st, "cmp_a", [128, 2, VW_PAD])
        tile_bc = sb(env, st, "tile_bc", [128, VW_PAD])
        chunk_bc = sb(env, st, "chunk_bc", [128, VW_PAD])
        chunk_id = sb(env, st, "chunk_id", [CQ, NQ])
        sel = sb(env, st, "sel", [CQ, NQ, VW_PAD])
        rel_w = sb(env, st, "rel_w", [128, VW_PAD])
        in_a = sb(env, st, "in_a", [128, VW_PAD])
        in_b = sb(env, st, "in_b", [128, VW_PAD])
        kk = sb(env, st, "kk", [128, VW_PAD])
        src_f = sb(env, st, "src_f", [128, VW_PAD])
        iota_i = sb(env, st, "iota_i", [128, VW_PAD], I32)
        part_i = sb(env, st, "part_i", [128, 1], I32)
        pc = ps(env, st, "pc", [128, 512])
        pb = ps(env, st, "pb", [128, 2, 512])
        pv = ps(env, st, "pv", [128, 2, 2, 512])
        rows_cleared, rows_landed, x_landed = ph.sem(), ph.sem(), ph.sem()
        made, step, on_pe, loaded = ph.sem(), ph.sem(), ph.sem(), ph.sem()
        names = ["dst", "src", "edge_type_6", "edge_type_64"]

        with nc.Block() as block:

            @block.sync
            def _(sp):
                sp.dma_start(env.x[:], a["x"].rearrange("(t p) d -> p t d", p=P)).then_inc(x_landed, 16)
                sp.wait_ge(rows_cleared, 2)
                for j, name in enumerate(names):
                    for q in range(NQ):
                        lo = q * CQ * CH
                        n = min(CQ, (E - lo) // CH)
                        sp.dma_start(rows_i[0:n, j, q, :], a[name][lo:lo + n * CH].rearrange(
                            "(c e) -> c e", e=CH)).then_inc(rows_landed, 16)
                    tail = E - (REAL - 1) * CH
                    r = REAL - 1 - (NQ - 1) * CQ
                    sp.dma_start(rows_i[r:r + 1, j, NQ - 1, 0:tail], a[name][E - tail:E].rearrange(
                        "(c e) -> c e", c=1)).then_inc(rows_landed, 16)
                sp.wait_ge(x_landed, 16)

            @block.gpsimd
            def _(pool):
                pool.memset(rows_i[:, 0, NQ - 1, :], FAR).then_inc(rows_cleared, 1)
                pool.memset(rows_i[:, 1:4, NQ - 1, :], 0).then_inc(rows_cleared, 1)
                pool.iota(iota_i[:], [[1, VW_PAD]], base=0, channel_multiplier=0).then_inc(made, 1)
                pool.iota(part_i[:], [[0, 1]], base=0, channel_multiplier=1).then_inc(made, 1)
                pool.memset(env.ones[:], 1.0).then_inc(made, 1)
                pool.memset(env.ident[:], 0.0).then_inc(made, 1)
                pool.wait_ge(made, 4)
                pool.affine_select(out=env.ident[:], in_=env.ident[:], compare_op=ALU.not_equal, fill=1.0,
                                   base=0, pattern=[[-1, 128]], channel_multiplier=1).then_inc(made, 1)

            @block.vector
            def _(v):
                n = [0]

                def done(ins):
                    n[0] += 1
                    ins.then_inc(step, 1)
                    v.wait_ge(step, n[0])

                v.wait_ge(made, 5)
                done(v.tensor_copy(env.iota[:], iota_i[:]))
                done(v.tensor_copy(env.part[:], part_i[:]))
                for q in range(NQ):
                    done(v.tensor_scalar(chunk_id[:, q:q + 1], env.part[0:CQ, :], float(q * CQ), None, ALU.add))
                v.wait_ge(rows_landed, 16 * 4 * (NQ + 1))
                done(v.tensor_copy(rows_f[:], rows_i[:]))
                done(v.tensor_reduce(chunk_max[:], rows_f[:, 0], AX.X, ALU.max))
                pe = [0]

                def after_pe():
                    pe[0] += 1
                    v.wait_ge(on_pe, pe[0])

                for width, count, visits in ((P, T, VT_PAD), (WN, NW, VW_PAD)):
                    half = visits // 2
                    done(v.tensor_scalar(edges_t[:, 0:count], env.iota[0:CQ, 0:count], float(width), None, ALU.mult))
                    for q in range(NQ):
                        done(v.tensor_scalar(before[:, q, 0:count], edges_t[:, 0:count],
                                             chunk_max[:, q:q + 1], None, ALU.is_gt))
                    sets = [(w0, min(128, count - w0)) for w0 in range(0, count, 128)]
                    after_pe()
                    for j, (w0, m) in enumerate(sets):
                        done(v.tensor_scalar(key[0:m, j:j + 1], pc[0:m, j:j + 1], env.part[0:m, :], float(w0),
                                             ALU.add, ALU.add))
                        done(v.tensor_scalar(cmp_a[0:m, j, 0:visits], env.iota[0:m, 0:visits],
                                             key[0:m, j:j + 1], None, ALU.is_ge))
                    after_pe()
                    for h in range(2):
                        done(v.tensor_scalar(tile_bc[:, h * half:(h + 1) * half], pb[:, h, 0:half], -1.0, None, ALU.add))
                    done(v.tensor_tensor(chunk_bc[:, 0:visits], env.iota[:, 0:visits], tile_bc[:, 0:visits], ALU.subtract))
                    for q in range(NQ):
                        done(v.tensor_scalar(sel[:, q, 0:visits], chunk_bc[0:CQ, 0:visits],
                                             chunk_id[:, q:q + 1], None, ALU.is_equal))
                    tiles = env.tile_of_visit if width == P else env.window_of_visit
                    done(v.tensor_copy(tiles[0:1, 0:visits], tile_bc[0:1, 0:visits]))
                    after_pe()
                    for h in range(2):
                        s = slice(h * half, (h + 1) * half)
                        rel = env.rel_dst if width == P else rel_w
                        done(v.scalar_tensor_tensor(out=rel[:, s], in0=tile_bc[:, s], scalar=float(-width),
                                                    in1=pv[:, 0, h, 0:half], op0=ALU.mult, op1=ALU.add))
                        if width == P:
                            done(v.tensor_copy(env.src_of_visit[:, s], pv[:, 1, h, 0:half]))
                        else:
                            done(v.tensor_copy(src_f[:, s], pv[:, 1, h, 0:half]))
                    after_pe()
                    for h in range(2):
                        s = slice(h * half, (h + 1) * half)
                        if width == P:
                            done(v.tensor_copy(env.type64[:, s], pv[:, 0, h, 0:half]))
                        else:
                            done(v.tensor_scalar(in_a[:, s], rel_w[:, s], 0.0, None, ALU.is_ge))
                            done(v.scalar_tensor_tensor(out=in_b[:, s], in0=rel_w[:, s], scalar=float(WN),
                                                        in1=in_a[:, s], op0=ALU.is_lt, op1=ALU.mult))
                            done(v.scalar_tensor_tensor(out=kk[:, s], in0=pv[:, 0, h, 0:half], scalar=float(WN),
                                                        in1=rel_w[:, s], op0=ALU.mult, op1=ALU.add))
                            done(v.scalar_tensor_tensor(out=in_a[:, s], in0=kk[:, s], scalar=1.0,
                                                        in1=in_b[:, s], op0=ALU.add, op1=ALU.mult))
                            done(v.tensor_scalar(env.row_of_edge[:, s], in_a[:, s], -1.0, None, ALU.add))
                            done(v.scalar_tensor_tensor(out=kk[:, s], in0=src_f[:, s], scalar=float(R6),
                                                        in1=pv[:, 0, h, 0:half], op0=ALU.mult, op1=ALU.add))
                            done(v.tensor_copy(env.message_of_visit[:, s], kk[:, s]))

            @block.tensor
            def _(pe):
                n = 2 + NQ + 2
                for width, count, visits in ((P, T, VT_PAD), (WN, NW, VW_PAD)):
                    half = visits // 2
                    sets = [(w0, min(128, count - w0)) for w0 in range(0, count, 128)]
                    n += 1 + NQ
                    pe.wait_ge(step, n)
                    for j, (w0, m) in enumerate(sets):
                        for q in range(NQ):
                            mm = pe.matmul(pc[0:m, j:j + 1], before[:, q, w0:w0 + m], env.ones[0:CQ, 0:1],
                                           start=q == 0, stop=q == NQ - 1)
                    mm.then_inc(on_pe, 1)
                    n += 2 * len(sets)
                    pe.wait_ge(step, n)
                    for h in range(2):
                        for j, (w0, m) in enumerate(sets):
                            mm = pe.matmul(pb[:, h, 0:half], env.ones[0:m, :], cmp_a[0:m, j, h * half:(h + 1) * half],
                                           start=j == 0, stop=j == len(sets) - 1)
                    mm.then_inc(on_pe, 1)
                    n += 2 + 1 + NQ
                    pe.wait_ge(step, n)
                    for k, j in enumerate((0, 1)):
                        for h in range(2):
                            for q in range(NQ):
                                mm = pe.matmul(pv[:, k, h, 0:half], rows_f[:, j, q, :], sel[:, q, h * half:(h + 1) * half],
                                               start=q == 0, stop=q == NQ - 1)
                    mm.then_inc(on_pe, 1)
                    n += 1 + 4
                    pe.wait_ge(step, n)
                    j = 3 if width == P else 2
                    for h in range(2):
                        for q in range(NQ):
                            mm = pe.matmul(pv[:, 0, h, 0:half], rows_f[:, j, q, :], sel[:, q, h * half:(h + 1) * half],
                                           start=q == 0, stop=q == NQ - 1)
                    mm.then_inc(on_pe, 1)
                    n += 2 if width == P else 14


def stats_phase(env, x, mean=None, rstd=None):
    nc = env.nc
    mean, rstd = mean or env.mean, rstd or env.rstd
    ph = Phase(env)
    with ExitStack() as st:
        moments = sb(env, st, "moments", [P, T, 6])
        mv = sb(env, st, "mv", [P, T, 2])
        std = sb(env, st, "std", [P, T])
        eps = sb(env, st, "eps", [P, 1])
        summed, whole, rooted, step = ph.sem(), ph.sem(), ph.sem(), ph.sem()
        with nc.Block() as block:

            @block.sync
            def _(sp):
                ph.clear_other()

            @block.gpsimd
            def _(pool):
                pool.memset(eps[:], 1e-5).then_inc(whole, 1)

            @block.vector
            def _(v):
                with v.Fori(0, T) as t:
                    v.bn_stats(moments[:, ds(t, 1), :], x[:, ds(t, 1), :]).then_inc(summed, 1)
                v.wait_ge(summed, T)
                for t in range(T):
                    v.bn_aggr(mv[:, t, :], moments[:, t, :]).then_inc(step, 1)
                v.wait_ge(step, T)
                v.tensor_copy(mean[:], mv[:, :, 0:1].rearrange("p t o -> p (t o)")).then_inc(whole, 1)
                v.wait_ge(rooted, 1)
                v.reciprocal(rstd[:], std[:]).then_inc(step, 1)

            @block.scalar
            def _(act):
                act.wait_ge(whole, 2)
                act.activation(std[:], mv[:, :, 1:2].rearrange("p t o -> p (t o)"), ACT.Sqrt,
                               bias=eps[:]).then_inc(rooted, 1)


def norm_phase(env):
    ph = Phase(env)
    step = ph.sem()
    with env.nc.Block() as block:

        @block.sync
        def _(sp):
            ph.clear_other()

        @block.vector
        def _(v):
            v.tensor_tensor(env.normed[:], env.x[:], env.mean[:].unsqueeze(2).to_broadcast([P, T, D]),
                            ALU.subtract).then_inc(step, 1)
            v.wait_ge(step, 1)
            v.tensor_tensor(env.normed[:], env.normed[:], env.rstd[:].unsqueeze(2).to_broadcast([P, T, D]),
                            ALU.mult).then_inc(step, 1)


def project_phase(env, w, bias, cols, kind, out_table=None):
    nc = env.nc
    ph = Phase(env)
    banks = -(-cols // 512)
    with ExitStack() as st:
        w_sb = sb(env, st, "w_sb", [128, K2, cols])
        bias_bc = sb(env, st, "bias_bc", [P, cols])
        normed = sb(env, st, "normed", [P, GT, D])
        x_t = sb(env, st, "x_t", [128, GT, K2, P])
        rows = sb(env, st, "rows", [P, GT, cols])
        query = sb(env, st, "query", [128, K2])
        query_s = sb(env, st, "query_s", [128, K2])
        turned = ps(env, st, "turned", [128, 2, K2 * 256])
        prod = ps(env, st, "prod", [128, 2, banks, 512])
        w_landed, query_scaled = ph.sem(), ph.sem()
        normed_ready, transposed, x_t_ready, multiplied = ph.sem(), ph.sem(), ph.sem(), ph.sem()
        added, rows_ready, stored = ph.sem(), ph.sem(), ph.sem()
        loads = 1 + (bias is not None) + (kind == "qkv")
        stores = 2 if kind == "qkv" else 1
        with nc.Block() as block:

            @block.sync
            def _(sp):
                ph.clear_other()
                sp.dma_start(w_sb[:], w).then_inc(w_landed, 16)
                if bias is not None:
                    sp.dma_start(bias_bc[:], bias).then_inc(w_landed, 16)
                if kind == "qkv":
                    sp.dma_start(query[:], env.a["L0_gnn_query_emb"]).then_inc(w_landed, 16)
                sp.sem_inc(stored, 1)
                with sp.Fori(0, G) as g:
                    for i in range(GT):
                        sp.wait_ge(rows_ready, g * GT + i + 1)
                        r = ds((g * GT + i) * P, P)
                        if kind == "qkv":
                            sp.dma_start(env.k_table[r, :], rows[:, i, D:2 * D]).then_inc(stored, 16)
                            sp.dma_start(env.v_table[r, :], rows[:, i, 2 * D:3 * D]).then_inc(stored, 16)
                        else:
                            sp.dma_start(out_table[r, :], rows[:, i, :]).then_inc(stored, 16)
                sp.wait_ge(stored, 16 * stores * T + 1)

            @block.vector
            def _(v):
                v.wait_ge(w_landed, 16 * loads)
                if kind == "qkv":
                    v.tensor_scalar(query_s[:], query[:], 0.1, None, ALU.mult).then_inc(query_scaled, 1)
                v.sem_inc(added, 2)
                with v.Fori(0, G) as g:
                    for i in range(GT):
                        t = g * GT + i
                        v.wait_ge(transposed, t + 1)
                        v.tensor_scalar(normed[:, i, :], env.x[:, ds(t, 1), :].rearrange("p o d -> p (o d)"),
                                        env.mean[:, ds(t, 1)], env.rstd[:, ds(t, 1)], ALU.subtract,
                                        ALU.mult).then_inc(normed_ready, 1)
                    v.wait_ge(stored, g * (16 * stores * GT) + 1)
                    for i in range(GT):
                        t = g * GT + i
                        v.wait_ge(multiplied, t + 1 + GT)
                        for b in range(banks):
                            s = slice(b * 512, min(cols, b * 512 + 512))
                            here = prod[0:P, i % 2, b, 0:s.stop - s.start]
                            if bias is None:
                                ins = v.tensor_copy(rows[:, i, s], here)
                            else:
                                ins = v.tensor_tensor(rows[:, i, s], here, bias_bc[:, s], ALU.add)
                        ins.then_inc(added, 1)
                        v.wait_ge(added, t + 1 + 2)
                        if kind == "qkv":
                            v.tensor_copy(env.q[:, ds(t, 1), :].rearrange("p o d -> p (o d)"),
                                          rows[:, i, 0:D]).then_inc(rows_ready, 1)
                        elif kind == "scaled":
                            v.tensor_scalar(rows[:, i, :], rows[:, i, :], env.scale[:, ds(t, 1)], None,
                                            ALU.mult).then_inc(rows_ready, 1)
                        else:
                            v.sem_inc(rows_ready, 1)

            @block.tensor
            def _(pe):
                pe.sem_inc(transposed, GT)
                pe.sem_inc(multiplied, GT)
                pe.wait_ge(w_landed, 16 * loads)
                with pe.Fori(0, G) as g:
                    for i in range(GT):
                        t = g * GT + i
                        pe.wait_ge(normed_ready, t + 1)
                        pe.wait_ge(x_t_ready, t + (1 + (i == 0)))
                        for k in range(K2):
                            mm = pe.transpose(turned[:, i % 2, k * P:(k + 1) * P],
                                              normed[:, i, k * 128:(k + 1) * 128], env.ident[0:P, 0:P])
                        mm.then_inc(transposed, 1)
                    for i in range(GT):
                        t = g * GT + i
                        pe.wait_ge(x_t_ready, t + 1 + 2)
                        pe.wait_ge(added, t + (1 + (i == 0)))
                        for b in range(banks):
                            s = slice(b * 512, min(cols, b * 512 + 512))
                            for k in range(K2):
                                mm = pe.matmul(prod[0:P, i % 2, b, 0:s.stop - s.start], x_t[:, i, k, :],
                                               w_sb[:, k, s], start=k == 0, stop=k == K2 - 1)
                        mm.then_inc(multiplied, 1)

            @block.scalar
            def _(act):
                act.sem_inc(x_t_ready, 2)
                if kind == "qkv":
                    act.wait_ge(query_scaled, 1)
                with act.Fori(0, G) as g:
                    for i in range(GT):
                        t = g * GT + i
                        act.wait_ge(multiplied, t + 1)
                        act.wait_ge(transposed, t + 1 + GT)
                        if kind == "qkv":
                            for k in range(K2):
                                ins = act.activation(x_t[:, i, k, :], turned[:, i % 2, k * P:(k + 1) * P],
                                                     ACT.Identity, bias=query_s[:, k:k + 1])
                            ins.then_inc(x_t_ready, 1)
                        else:
                            act.activation(x_t[:, i].rearrange("p k n -> p (k n)"), turned[:, i % 2, 0:K2 * P],
                                           ACT.Copy).then_inc(x_t_ready, 1)


def make_hits(v, env, out, key_of_edge, width, k):
    return v.tensor_tensor(out, env.iota[:, 0:width].unsqueeze(1).to_broadcast([128, VB, width]),
                           key_of_edge[:, ds(k * VB, VB)].unsqueeze(2).to_broadcast([128, VB, width]), ALU.is_equal)


def score_phase(env):
    nc = env.nc
    ph = Phase(env)
    batches = VT // VB
    with ExitStack() as st:
        rel_raw = sb(env, st, "rel_raw", [R64, HD])
        rel_w = sb(env, st, "rel_w", [R64, HD])
        gather = Gather(env, st, ph, env.k_table, env.src_of_visit, batches)
        hit = sb(env, st, "hit", [128, SLOTS, VB, 128])
        hit_type = sb(env, st, "hit_type", [128, SLOTS, VB, R64])
        hit_t = sb(env, st, "hit_t", [128, SLOTS, VB * 128])
        type_t = sb(env, st, "type_t", [R64, SLOTS, VB * 128])
        q_rows = sb(env, st, "q_rows", [128, SLOTS, VB, D])
        terms = sb(env, st, "terms", [128, VB, D])
        ps_hit = ps(env, st, "ps_hit", [128, VB * 128])
        ps_type = ps(env, st, "ps_type", [128, VB * 128])
        ps_q = ps(env, st, "ps_q", [128, 2, VB, D])
        ps_rel = ps(env, st, "ps_rel", [128, 2, 512])
        rel_landed, rel_scaled = ph.sem(), ph.sem()
        hits_made, turned, turned_copied, multiplied, q_copied, summed, scored = [ph.sem() for _ in range(7)]
        with nc.Block() as block:

            @block.sync
            def _(sp):
                ph.clear_other()
                sp.dma_start(rel_raw[:], env.a["L0_gnn_rel_w"]).then_inc(rel_landed, 16)

            @block.gpsimd
            def _(pool):
                gather.gpsimd(pool)

            @block.vector
            def _(v):
                v.wait_ge(rel_landed, 16)
                v.tensor_scalar(rel_w[:], rel_raw[:], 0.2, None, ALU.mult).then_inc(rel_scaled, 1)
                v.sem_inc(gather.freed, SLOTS)
                v.sem_inc(scored, 2)
                v.memset(env.scores[:, VT:VT_PAD, :], 0.0)

                def hits(k, slot):
                    make_hits(v, env, hit[:, slot], env.rel_dst, 128, k)
                    make_hits(v, env, hit_type[:, slot], env.type64, R64, k).then_inc(hits_made, 1)

                hits(0, 0)
                hits(1, 1)

                def one_batch(k, slot, lap):
                    v.wait_ge(turned, k + 1)
                    hits(k + 2, (slot + 2) % SLOTS)
                    gather.wait(v, slot, lap)
                    v.wait_ge(multiplied, k + 1)
                    k_rows = gather.rows[:, slot].rearrange("p v (h d) -> p v h d", h=HEADS)
                    rel = ps_rel[:, slot % 2, 0:VB * HD].rearrange("p (v d) -> p v d", v=VB)
                    v.tensor_tensor(terms[:].rearrange("p v (h d) -> p v h d", h=HEADS), k_rows,
                                    rel.unsqueeze(2).to_broadcast([128, VB, HEADS, HD]), ALU.add).then_inc(gather.freed, 1)
                    v.wait_ge(gather.freed, k + (1 + SLOTS))
                    v.wait_ge(q_copied, k + (1 + SLOTS))
                    v.tensor_tensor(terms[:], terms[:], q_rows[:, slot], ALU.mult).then_inc(summed, 1)
                    v.wait_ge(summed, k + 1)
                    v.tensor_reduce(env.scores[:, ds(k * VB, VB), :], terms[:].rearrange("p v (h d) -> p v h d", h=HEADS),
                                    AX.X, ALU.add).then_inc(scored, 1)
                    v.wait_ge(scored, k + (1 + 2))

                batch_loop(v, batches, 0, one_batch)

            @block.tensor
            def _(pe):
                pe.wait_ge(rel_scaled, 1)

                def turn(k, slot):
                    pe.wait_ge(hits_made, k + 1)
                    pe.wait_ge(turned_copied, k + 1)
                    for i in range(VB):
                        pe.transpose(ps_hit[:, i * 128:(i + 1) * 128], hit[:, slot, i, :], env.ident[:])
                        mm = pe.transpose(ps_type[0:R64, i * 128:(i + 1) * 128], hit_type[:, slot, i, :], env.ident[:])
                    mm.then_inc(turned, 1)

                turn(0, 0)

                def one_batch(k, slot, lap):
                    turn(k + 1, (slot + 1) % SLOTS)
                    pe.wait_ge(turned_copied, k + 1 + 1)
                    pe.wait_ge(q_copied, k + (1 + SLOTS - 2))
                    pe.wait_ge(scored, k + 1)
                    for i in range(VB):
                        tile = pe.value_load(env.tile_of_visit[0:1, ds(k * VB + i, 1)], min_val=0, max_val=T - 1)
                        pe.matmul(ps_q[:, slot % 2, i, :], hit_t[0:P, slot, i * 128:(i + 1) * 128],
                                  env.q[:, ds(tile, 1), :].rearrange("p o d -> p (o d)"), start=True, stop=True)
                        mm = pe.matmul(ps_rel[:, slot % 2, i * HD:(i + 1) * HD], type_t[:, slot, i * 128:(i + 1) * 128],
                                       rel_w[:], start=True, stop=True)
                    mm.then_inc(multiplied, 1)

                batch_loop(pe, batches, 0, one_batch)

            @block.scalar
            def _(act):
                act.sem_inc(turned_copied, 1)
                act.sem_inc(q_copied, SLOTS)

                def copy(k, slot):
                    if not isinstance(k, int) or k >= SLOTS:
                        act.wait_ge(multiplied, k - (SLOTS - 1))
                    act.wait_ge(turned, k + 1)
                    act.activation(hit_t[:, slot], ps_hit[:], ACT.Copy)
                    act.activation(type_t[:, slot], ps_type[0:R64, :], ACT.Copy).then_inc(turned_copied, 1)

                for k in range(2):
                    gather.scalar(act, k, k)
                copy(0, 0)

                def one_batch(k, slot, lap):
                    gather.scalar(act, k + 2, (slot + 2) % SLOTS)
                    copy(k + 1, (slot + 1) % SLOTS)
                    act.wait_ge(multiplied, k + 1)
                    if not isinstance(k, int) or k >= SLOTS:
                        act.wait_ge(scored, k + (1 + 2 - SLOTS))
                    act.activation(q_rows[:, slot], ps_q[:, slot % 2], ACT.Copy).then_inc(q_copied, 1)

                batch_loop(act, batches, SLOTS, one_batch)


def peak_phase(env):
    nc = env.nc
    ph = Phase(env)
    with ExitStack() as st:
        low = sb(env, st, "low", [128, HEADS])
        low_h = sb(env, st, "low_h", [HEADS, 1])
        low_diag = sb(env, st, "low_diag", [HEADS, HEADS])
        low_bc = sb(env, st, "low_bc", [128, HEADS])
        hit = sb(env, st, "hit", [128, SLOTS, VB, 128])
        masked = sb(env, st, "masked", [128, SLOTS, VB * HEADS, 128])
        peak = sb(env, st, "peak", [P, VB * HEADS])
        ps_masked = ps(env, st, "ps_masked", [128, 2, VB, 512])
        ps_low = ps_masked[:, 0, 0, :]
        step, low_turned, hits_made, masked_made, turned, reduced, merged, zeroed, hold = [ph.sem() for _ in range(9)]
        batches = VT // VB
        with nc.Block() as block:

            @block.sync
            def _(sp):
                ph.clear_other()

            @block.gpsimd
            def _(pool):
                pool.memset(env.peaks[:], 0.0).then_inc(zeroed, 1)
                pool.wait_ge(step, 5)

                def one_batch(k, slot, lap):
                    pool.wait_ge(hits_made, k + 1)
                    pool.wait_ge(turned, k + 1)
                    pool.sem_inc(hold, 1)
                    pool.tensor_tensor(masked[:, slot].rearrange("p (v h) n -> p v h n", v=VB),
                                       hit[:, slot].unsqueeze(2).to_broadcast([128, VB, HEADS, 128]),
                                       env.scores[:, ds(k * VB, VB), :].unsqueeze(3).to_broadcast([128, VB, HEADS, 128]),
                                       ALU.mult).then_inc(masked_made, 1)

                batch_loop(pool, batches, 0, one_batch)

            @block.vector
            def _(v):
                v.tensor_reduce(low[:], env.scores[:, 0:VT, :].rearrange("p v h -> p h v"), AX.X,
                                ALU.min).then_inc(step, 1)
                v.wait_ge(low_turned, 1)
                v.tensor_reduce(low_h[:], ps_low[0:HEADS, 0:128], AX.X, ALU.min).then_inc(step, 1)
                v.wait_ge(step, 2)
                v.tensor_scalar(low_diag[:], env.ident[0:HEADS, 0:HEADS], low_h[:], None, ALU.mult).then_inc(step, 1)
                v.wait_ge(low_turned, 2)
                v.tensor_copy(low_bc[:], ps_low[:, 128:128 + HEADS]).then_inc(step, 1)
                v.wait_ge(step, 4)
                v.tensor_tensor(env.scores[:, 0:VT, :], env.scores[:, 0:VT, :],
                                low_bc[:].unsqueeze(1).to_broadcast([128, VT, HEADS]), ALU.subtract).then_inc(step, 1)

                for k in range(AHEAD):
                    make_hits(v, env, hit[:, k], env.rel_dst, 128, k).then_inc(hits_made, 1)
                v.wait_ge(zeroed, 1)
                v.sem_inc(reduced, 2)
                v.sem_inc(merged, 1)

                def one_batch(k, slot, lap):
                    v.wait_ge(turned, k + (1 + SLOTS))
                    v.wait_ge(merged, k * VB + 1)
                    v.tensor_reduce(peak[:], ps_masked[0:P, slot % 2].rearrange("p v (h e) -> p (v h) e", h=HEADS),
                                    AX.X, ALU.max).then_inc(reduced, 1)
                    make_hits(v, env, hit[:, (slot + AHEAD) % SLOTS], env.rel_dst, 128, k + AHEAD).then_inc(hits_made, 1)
                    tiles = tiles_of_batch(v, env.tile_of_visit, k, T)
                    v.wait_ge(reduced, k + (1 + 2))
                    for i in range(VB):
                        here = env.peaks[:, ds(tiles[i], 1), :].rearrange("p o h -> p (o h)")
                        v.tensor_tensor(here, here, peak[:, i * HEADS:(i + 1) * HEADS], ALU.max).then_inc(merged, 1)
                        if i < VB - 1:
                            v.wait_ge(merged, k * VB + (i + 1 + 1))

                batch_loop(v, batches, 0, one_batch)

            @block.tensor
            def _(pe):
                pe.sem_inc(turned, SLOTS)
                pe.wait_ge(step, 1)
                pe.transpose(ps_low[0:HEADS, 0:128], low[:], env.ident[:]).then_inc(low_turned, 1)
                pe.wait_ge(step, 3)
                pe.matmul(ps_low[:, 128:128 + HEADS], env.ones[0:HEADS, :], low_diag[:], start=True,
                          stop=True).then_inc(low_turned, 1)

                def one_batch(k, slot, lap):
                    pe.wait_ge(masked_made, k + 1)
                    pe.wait_ge(reduced, k + 1)
                    for i in range(VB * HEADS):
                        mm = pe.transpose(ps_masked[:, slot % 2, i // HEADS, (i % HEADS) * 128:(i % HEADS + 1) * 128],
                                          masked[:, slot, i, :], env.ident[:])
                    mm.then_inc(turned, 1)

                batch_loop(pe, batches, 0, one_batch)


VC = D + HEADS + 1


def attend_phase(env):
    nc = env.nc
    ph = Phase(env)
    batches = VT // VB
    with ExitStack() as st:
        gather = Gather(env, st, ph, env.v_table, env.src_of_visit, batches)
        hit = sb(env, st, "hit", [128, SLOTS, VB, 128])
        hit_t = sb(env, st, "hit_t", [128, SLOTS, VB * 128])
        below = sb(env, st, "below", [128, SLOTS, VB, HEADS])
        weight = sb(env, st, "weight", [128, SLOTS, VB, HEADS])
        summand = sb(env, st, "summand", [128, SLOTS, VB, VC])
        ps_hit = ps(env, st, "ps_hit", [128, VB * 128])
        ps_peak = ps(env, st, "ps_peak", [128, VB, HEADS])
        ps_sum = ps(env, st, "ps_sum", [128, VB, 512])
        cleared, hits_made, turned, turned_copied, peaks_out, lowered, clipped, weighed = [ph.sem() for _ in range(8)]
        multiplied, summed = ph.sem(), ph.sem()
        with nc.Block() as block:

            @block.sync
            def _(sp):
                ph.clear_other()

            @block.gpsimd
            def _(pool):
                pool.memset(env.sums[:], 0.0).then_inc(cleared, 1)
                pool.memset(summand[:], 1.0).then_inc(cleared, 1)
                gather.gpsimd(pool)

            @block.vector
            def _(v):
                def lower(k, slot):
                    v.wait_ge(peaks_out, k + 1)
                    v.tensor_tensor(below[:, slot], env.scores[:, ds(k * VB, VB), :], ps_peak[:],
                                    ALU.subtract).then_inc(lowered, 1)
                    v.wait_ge(lowered, k + 1)
                    v.tensor_scalar(below[:, slot], below[:, slot], 0.0, None, ALU.min).then_inc(clipped, 1)

                def add(k, tiles):
                    for i in range(VB):
                        v.wait_ge(summed, k * VB + (i + VB))
                        here = env.sums[:, ds(tiles[i], 1), :].rearrange("p o c -> p (o c)")
                        v.tensor_tensor(here, here, ps_sum[0:P, i, 0:VC], ALU.add).then_inc(summed, 1)

                v.wait_ge(cleared, 2)
                v.sem_inc(gather.freed, SLOTS)
                v.sem_inc(summed, VB)
                for k in range(AHEAD):
                    make_hits(v, env, hit[:, k], env.rel_dst, 128, k).then_inc(hits_made, 1)
                lower(0, 0)

                def one_batch(k, slot, lap):
                    lower(k + 1, (slot + 1) % SLOTS)
                    gather.wait(v, slot, lap)
                    v.wait_ge(weighed, k + 1)
                    v.tensor_tensor(summand[:, slot, :, 0:D].rearrange("p v (h d) -> p v h d", h=HEADS),
                                    gather.rows[:, slot].rearrange("p v (h d) -> p v h d", h=HEADS),
                                    weight[:, slot].unsqueeze(3).to_broadcast([128, VB, HEADS, HD]), ALU.mult)
                    v.tensor_copy(summand[:, slot, :, D:D + HEADS], weight[:, slot]).then_inc(gather.freed, 1)
                    before = not isinstance(k, int) or k > 0
                    if before:
                        tiles = tiles_of_batch(v, env.tile_of_visit, k - 1, T)
                        v.wait_ge(multiplied, k * VB)
                    make_hits(v, env, hit[:, (slot + AHEAD) % SLOTS], env.rel_dst, 128, k + AHEAD).then_inc(hits_made, 1)
                    if before:
                        add(k - 1, tiles)

                batch_loop(v, batches, 1, one_batch)
                v.wait_ge(multiplied, batches * VB)
                add(batches - 1, tiles_of_batch(v, env.tile_of_visit, batches - 1, T))

            @block.tensor
            def _(pe):
                def turn(k, slot):
                    pe.wait_ge(hits_made, k + 1)
                    pe.wait_ge(turned_copied, k + 1)
                    for i in range(VB):
                        mm = pe.transpose(ps_hit[:, i * 128:(i + 1) * 128], hit[:, slot, i, :], env.ident[:])
                    mm.then_inc(turned, 1)

                def peaks(k, slot):
                    tiles = tiles_of_batch(pe, env.tile_of_visit, k, T)
                    pe.wait_ge(turned_copied, k + 1 + 1)
                    if not isinstance(k, int) or k > 0:
                        pe.wait_ge(lowered, k)
                    for i in range(VB):
                        mm = pe.matmul(ps_peak[:, i, :], hit_t[0:P, slot, i * 128:(i + 1) * 128],
                                       env.peaks[:, ds(tiles[i], 1), :].rearrange("p o h -> p (o h)"), start=True, stop=True)
                    mm.then_inc(peaks_out, 1)

                turn(0, 0)
                peaks(0, 0)
                turn(1, 1)
                peaks(1, 1)
                turn(2, 2)

                def one_batch(k, slot, lap):
                    peaks(k + 2, (slot + 2) % SLOTS)
                    pe.wait_ge(gather.freed, k + (1 + SLOTS))
                    for i in range(VB):
                        pe.wait_ge(summed, k * VB + (i + 1))
                        pe.matmul(ps_sum[0:P, i, 0:VC], hit[:, slot, i, 0:P], summand[:, slot, i, :], start=True,
                                  stop=True).then_inc(multiplied, 1)
                    turn(k + 3, (slot + 3) % SLOTS)

                batch_loop(pe, batches, 1, one_batch)

            @block.scalar
            def _(act):
                act.sem_inc(turned_copied, 1)

                def copy(k, slot):
                    if not isinstance(k, int) or k >= SLOTS:
                        act.wait_ge(peaks_out, k - (SLOTS - 1))
                    act.wait_ge(turned, k + 1)
                    act.activation(hit_t[:, slot], ps_hit[:], ACT.Copy).then_inc(turned_copied, 1)

                def weigh(k, slot):
                    act.wait_ge(clipped, k + 1)
                    act.wait_ge(gather.freed, k + 1)
                    act.activation(weight[:, slot], below[:, slot], ACT.Exp, scale=HD ** -0.5).then_inc(weighed, 1)

                for k in range(3):
                    gather.scalar(act, k, k)
                    copy(k, k)
                weigh(0, 0)

                def one_batch(k, slot, lap):
                    weigh(k + 1, (slot + 1) % SLOTS)
                    gather.scalar(act, k + 3, (slot + 3) % SLOTS)
                    copy(k + 3, (slot + 3) % SLOTS)

                batch_loop(act, batches, SLOTS, one_batch)


def message_phase(env):
    nc = env.nc
    ph = Phase(env)
    with ExitStack() as st:
        w_sb = sb(env, st, "w_sb", [128, K2, D])
        bias_bc = sb(env, st, "bias_bc", [P, D])
        rden = sb(env, st, "rden", [P, T, HEADS])
        alone = sb(env, st, "alone", [P, T])
        degree = sb(env, st, "degree", [P, 2, T])
        root = sb(env, st, "root", [P, 2, T])
        v_own = sb(env, st, "v_own", [P, T, D])
        msg = sb(env, st, "msg", [P, GT, D])
        msg_t = sb(env, st, "msg_t", [128, GT, K2 * P])
        turned_ps = ps(env, st, "turned_ps", [128, 2, 512])
        prod = ps(env, st, "prod", [128, 2, 512])
        w_landed, step, rooted, scaled, msg_ready = [ph.sem() for _ in range(5)]
        transposed, copied, multiplied, added, own = [ph.sem() for _ in range(5)]
        with nc.Block() as block:

            @block.sync
            def _(sp):
                ph.clear_other()
                sp.dma_start(w_sb[:], env.a["L0_gnn_Wo"].rearrange("(k p) n -> p k n", p=128)).then_inc(w_landed, 16)
                sp.dma_start(bias_bc[:], env.row("L0_gnn_bo").to_broadcast([P, D])).then_inc(w_landed, 16)
                sp.dma_start(v_own[:], env.v_table.rearrange("(t p) d -> p t d", p=P)).then_inc(w_landed, 16)

            @block.vector
            def _(v):
                deg = env.sums[:, :, D + HEADS:D + HEADS + 1].rearrange("p t o -> p (t o)")
                v.tensor_scalar(rden[:], env.sums[:, :, D:D + HEADS], 1e-30, None, ALU.max).then_inc(step, 1)
                v.tensor_scalar(alone[:], deg, 0.5, None, ALU.is_lt).then_inc(step, 1)
                v.tensor_scalar(degree[:, 0, :], deg, 1.0, None, ALU.max).then_inc(step, 1)
                v.tensor_scalar(degree[:, 1, :], deg, 1.0, None, ALU.add).then_inc(step, 1)
                v.wait_ge(step, 4)
                v.reciprocal(rden[:], rden[:]).then_inc(step, 1)
                v.wait_ge(rooted, 1)
                v.reciprocal(env.norm2[:], root[:, 0, :]).then_inc(step, 1)
                v.reciprocal(env.norm3[:], root[:, 1, :]).then_inc(step, 1)
                v.wait_ge(step, 7)
                v.wait_ge(w_landed, 48)
                v.sem_inc(added, 2)
                with v.Fori(0, G) as g:
                    for i in range(GT):
                        t = g * GT + i
                        v.wait_ge(transposed, t + 1)
                        v.tensor_tensor(msg[:, i, :].rearrange("p (h d) -> p h d", h=HEADS),
                                        env.sums[:, ds(t, 1), 0:D].rearrange("p o (h d) -> p (o h) d", h=HEADS),
                                        rden[:, ds(t, 1), :].rearrange("p o h -> p (o h)").unsqueeze(2).to_broadcast([P, HEADS, HD]),
                                        ALU.mult).then_inc(scaled, 1)
                        v.wait_ge(scaled, t + 1)
                        v.scalar_tensor_tensor(out=msg[:, i, :], in0=v_own[:, ds(t, 1), :].rearrange("p o d -> p (o d)"),
                                               scalar=alone[:, ds(t, 1)], in1=msg[:, i, :], op0=ALU.mult,
                                               op1=ALU.add).then_inc(msg_ready, 1)
                    for i in range(GT):
                        t = g * GT + i
                        here = env.sums[:, ds(t, 1), 0:D].rearrange("p o d -> p (o d)")
                        own_t = v_own[:, ds(t, 1), :].rearrange("p o d -> p (o d)")
                        v.tensor_scalar(own_t, env.x[:, ds(t, 1), :].rearrange("p o d -> p (o d)"),
                                        env.mean[:, ds(t, 1)], env.rstd[:, ds(t, 1)], ALU.subtract,
                                        ALU.mult).then_inc(own, 1)
                        v.wait_ge(own, 2 * t + 1)
                        v.tensor_tensor(own_t, own_t, bias_bc[:], ALU.add).then_inc(own, 1)
                        v.wait_ge(own, 2 * t + 2)
                        v.wait_ge(multiplied, t + 1 + GT)
                        v.tensor_tensor(here, prod[0:P, i % 2, 0:D], own_t, ALU.add).then_inc(added, 1)

            @block.tensor
            def _(pe):
                pe.sem_inc(transposed, GT)
                pe.sem_inc(multiplied, GT)
                pe.wait_ge(w_landed, 48)
                with pe.Fori(0, G) as g:
                    for i in range(GT):
                        t = g * GT + i
                        pe.wait_ge(msg_ready, t + 1)
                        pe.wait_ge(copied, t + (1 + (i == 0)))
                        for k in range(K2):
                            mm = pe.transpose(turned_ps[:, i % 2, k * P:(k + 1) * P],
                                              msg[:, i, k * 128:(k + 1) * 128], env.ident[0:P, 0:P])
                        mm.then_inc(transposed, 1)
                    for i in range(GT):
                        t = g * GT + i
                        pe.wait_ge(copied, t + 1 + 2)
                        pe.wait_ge(added, t + (1 + (i == 0)))
                        for k in range(K2):
                            mm = pe.matmul(prod[0:P, i % 2, 0:D], msg_t[:, i, k * P:(k + 1) * P], w_sb[:, k, :],
                                           start=k == 0, stop=k == K2 - 1)
                        mm.then_inc(multiplied, 1)

            @block.scalar
            def _(act):
                act.sem_inc(copied, 2)
                act.wait_ge(step, 4)
                act.activation(root[:], degree[:], ACT.Sqrt).then_inc(rooted, 1)
                with act.Fori(0, G) as g:
                    for i in range(GT):
                        t = g * GT + i
                        act.wait_ge(multiplied, t + 1)
                        act.wait_ge(transposed, t + 1 + GT)
                        act.activation(msg_t[:, i, :], turned_ps[:, i % 2, 0:K2 * P], ACT.Copy).then_inc(copied, 1)


def affine_phase(env):
    nc = env.nc
    ph = Phase(env)
    with ExitStack() as st:
        gamma = sb(env, st, "gamma", [P, D])
        beta = sb(env, st, "beta", [P, D])
        landed, step = ph.sem(), ph.sem()
        with nc.Block() as block:

            @block.sync
            def _(sp):
                ph.clear_other()
                sp.dma_start(gamma[:], env.row("L0_gnn_gamma").to_broadcast([P, D])).then_inc(landed, 16)
                sp.dma_start(beta[:], env.row("L0_gnn_beta").to_broadcast([P, D])).then_inc(landed, 16)

            @block.vector
            def _(v):
                v.wait_ge(landed, 32)
                y = env.sums[:, :, 0:D]

                def over(col):
                    return col[:].unsqueeze(2).to_broadcast([P, T, D])

                def along(row):
                    return row[:].unsqueeze(1).to_broadcast([P, T, D])

                v.tensor_tensor(y, y, over(env.mean), ALU.subtract).then_inc(step, 1)
                v.wait_ge(step, 1)
                v.tensor_tensor(y, y, over(env.rstd), ALU.mult).then_inc(step, 1)
                v.wait_ge(step, 2)
                v.tensor_tensor(y, y, along(gamma), ALU.mult).then_inc(step, 1)
                v.wait_ge(step, 3)
                v.tensor_tensor(y, y, along(beta), ALU.add).then_inc(step, 1)
                v.wait_ge(step, 4)
                v.tensor_tensor(env.x[:], env.x[:], y, ALU.add).then_inc(step, 1)


def store_phase(env):
    nc = env.nc
    ph = Phase(env)
    stored = ph.sem()
    with nc.Block() as block:

        @block.sync
        def _(sp):
            ph.clear_other()
            sp.dma_start(env.out.rearrange("(t p) d -> p t d", p=P), env.x[:]).then_inc(stored, 16)
            sp.wait_ge(stored, 16)


def router_phase(env, kind):
    nc = env.nc
    ph = Phase(env)
    ne = {"L0": 8, "L1": 8, "L2": 8, "L3": 4}[kind]
    twice = kind == "L1"
    routed = kind in ("L0", "L1")
    w = env.a[{"L0": "L0_ffn_router_w", "L1": "L1_ffn_Wr", "L2": "L2_ffn_Wr", "L3": "L3_ffn_gW"}[kind]]
    b = {"L0": None, "L1": "L1_ffn_br", "L2": "L2_ffn_br", "L3": "L3_ffn_gb"}[kind]
    last_bias = env.a[{"L0": "L0_ffn_b2", "L1": "L1_ffn_b2", "L2": "L2_ffn_bo", "L3": "L3_ffn_eb3"}[kind]]
    shared_bias = "L3_ffn_sb3" if kind == "L3" else None
    with ExitStack() as st:
        w_sb = sb(env, st, "w_sb", [128, K2, ne])
        bias_bc = sb(env, st, "bias_bc", [P, ne])
        last_sb = sb(env, st, "last_sb", [ne, D])
        shared_bc = sb(env, st, "shared_bc", [P, D])
        normed = sb(env, st, "normed", [P, GT, D])
        a_t = sb(env, st, "a_t", [128, GT, K2 * P])
        logits = sb(env, st, "logits", [P, T, ne])
        probs = sb(env, st, "probs", [P, T, ne])
        one_a = sb(env, st, "one_a", [P, T, ne])
        one_b = sb(env, st, "one_b", [P, T, ne])
        rank = sb(env, st, "rank", [P, ne])
        top = sb(env, st, "top", [P, T])
        top2 = sb(env, st, "top2", [P, T])
        share = sb(env, st, "share", [P, T])
        pick = sb(env, st, "pick", [P, T])
        gate_s = sb(env, st, "gate_s", [P, GT, ne])
        gate_t = sb(env, st, "gate_t", [ne, GT, P])
        turned_ps = ps(env, st, "turned_ps", [128, 2, 512])
        count_ps = ps(env, st, "count_ps", [128, 2, 512]) if routed else None
        if routed:
            route = Route(env, st, ph, count_ps)
            zeros = sb(env, st, "zeros", [128, D]) if kind == "L0" else None
        logit_ps = ps(env, st, "logit_ps", [128, 2, 512])
        landed, normed_ready, transposed, copied, kept, multiplied, added, own_added = [ph.sem() for _ in range(8)]
        step, exped, gated, gate_ready, gate_turned, gate_copied, biased, bias_added, hold = [ph.sem() for _ in range(9)]
        zeroed, zeros_stored = ph.sem(), ph.sem()
        loads = 2 + (b is not None) + (shared_bias is not None)
        with nc.Block() as block:

            @block.sync
            def _(sp):
                ph.clear_other()
                sp.dma_start(w_sb[:], w.rearrange("(k p) e -> p k e", p=128)).then_inc(landed, 16)
                sp.dma_start(last_sb[:], last_bias).then_inc(landed, 16)
                if kind == "L0":
                    sp.wait_ge(zeroed, 1)
                    sp.dma_start(env.x_slots.rearrange("(t p) d -> p t d", p=128),
                                 zeros[:].unsqueeze(1).to_broadcast([128, SLOT_ROWS // 128, D])).then_inc(zeros_stored, 16)
                if b is not None:
                    sp.dma_start(bias_bc[:], env.row(b).to_broadcast([P, ne])).then_inc(landed, 16)
                if shared_bias is not None:
                    sp.dma_start(shared_bc[:], env.row(shared_bias).to_broadcast([P, D])).then_inc(landed, 16)
                if kind == "L0":
                    sp.wait_ge(zeros_stored, 16)

            @block.gpsimd
            def _(pool):
                if kind == "L0":
                    pool.memset(zeros[:], 0.0).then_inc(zeroed, 1)

            @block.vector
            def _(v):
                v.wait_ge(landed, 16 * loads)
                v.sem_inc(added, 2)
                with v.Fori(0, G) as g:
                    for i in range(GT):
                        t = g * GT + i
                        x_t = env.x[:, ds(t, 1), :].rearrange("p o d -> p (o d)")
                        v.wait_ge(transposed, t + 1)
                        if kind == "L0":
                            v.wait_ge(kept, t + 1)
                        v.tensor_scalar(normed[:, i, :], x_t, env.mean[:, ds(t, 1)], env.rstd[:, ds(t, 1)],
                                        ALU.subtract, ALU.mult).then_inc(normed_ready, 1)
                        if twice:
                            v.wait_ge(normed_ready, 2 * t + 1)
                            v.tensor_scalar(env.rows[:, ds(t, 1), :].rearrange("p o d -> p (o d)"), normed[:, i, :], env.mean2[:, ds(t, 1)],
                                            env.rstd2[:, ds(t, 1)], ALU.subtract, ALU.mult).then_inc(normed_ready, 1)
                        if kind == "L0":
                            v.wait_ge(normed_ready, t + 1)
                            v.tensor_tensor(x_t, x_t, normed[:, i, :], ALU.add).then_inc(own_added, 1)
                        if kind == "L3":
                            v.wait_ge(normed_ready, t + 1)
                            v.tensor_tensor(x_t, x_t, shared_bc[:], ALU.add).then_inc(own_added, 1)
                    for i in range(GT):
                        t = g * GT + i
                        v.wait_ge(multiplied, t + 1 + GT)
                        here = logits[:, ds(t, 1), :].rearrange("p o e -> p (o e)")
                        if b is None:
                            v.tensor_copy(here, logit_ps[0:P, i % 2, 0:ne]).then_inc(added, 1)
                        else:
                            v.tensor_tensor(here, logit_ps[0:P, i % 2, 0:ne], bias_bc[:], ALU.add).then_inc(added, 1)
                n = [0]

                def done(ins):
                    n[0] += 1
                    ins.then_inc(step, 1)
                    v.wait_ge(step, n[0])

                def wide(col):
                    return col[:].unsqueeze(2).to_broadcast([P, T, ne])

                v.wait_ge(added, 2 + T)
                done(v.tensor_reduce(top[:], logits[:], AX.X, ALU.max))
                done(v.tensor_tensor(logits[:], logits[:], wide(top), ALU.subtract))
                v.wait_ge(exped, 1)
                done(v.tensor_reduce(share[:], probs[:], AX.X, ALU.add))
                done(v.reciprocal(share[:], share[:]))
                if kind == "L2":
                    done(v.tensor_tensor(env.gates[:, :, 0:ne], probs[:], wide(share), ALU.mult))
                else:
                    done(v.tensor_tensor(probs[:], probs[:], wide(share), ALU.mult))
                    done(v.tensor_scalar(rank[:], env.iota[0:P, 0:ne], -1.0, float(ne), ALU.mult, ALU.add))

                    def first_largest(values, best, one):
                        done(v.tensor_reduce(best[:], values[:], AX.X, ALU.max))
                        done(v.tensor_tensor(one[:], values[:], wide(best), ALU.is_equal))
                        done(v.tensor_tensor(one[:], one[:], rank[:].unsqueeze(1).to_broadcast([P, T, ne]), ALU.mult))
                        done(v.tensor_reduce(pick[:], one[:], AX.X, ALU.max))
                        done(v.tensor_tensor(one[:], one[:], wide(pick), ALU.is_equal))

                    first_largest(probs, top, one_a)
                    done(v.scalar_tensor_tensor(out=probs[:], in0=one_a[:], scalar=-2.0, in1=probs[:], op0=ALU.mult,
                                                op1=ALU.add))
                    first_largest(probs, top2, one_b)
                    if kind == "L3":
                        done(v.tensor_tensor(top2[:], top2[:], top[:], ALU.subtract))
                        v.wait_ge(exped, 2)
                        done(v.memset(top[:], 1.0))
                    done(v.tensor_tensor(share[:], top[:], top2[:], ALU.add))
                    if kind == "L0":
                        done(v.tensor_scalar(share[:], share[:], 1e-12, None, ALU.max))
                    done(v.reciprocal(share[:], share[:]))
                    done(v.tensor_tensor(top[:], top[:], share[:], ALU.mult))
                    done(v.tensor_tensor(top2[:], top2[:], share[:], ALU.mult))
                    if routed:
                        route.vector(v, done, one_a, one_b, top, top2)
                    done(v.tensor_tensor(one_a[:], one_a[:], wide(top), ALU.mult))
                    done(v.tensor_tensor(one_b[:], one_b[:], wide(top2), ALU.mult))
                    done(v.tensor_tensor(env.gates[:, :, 0:ne], one_a[:], one_b[:], ALU.add))
                v.sem_inc(bias_added, 2)
                with v.Fori(0, G) as g:
                    for i in range(GT):
                        t = g * GT + i
                        v.wait_ge(gate_turned, t + 1)
                        v.tensor_copy(gate_s[:, i, :], env.gates[:, ds(t, 1), 0:ne].rearrange("p o e -> p (o e)")).then_inc(gate_ready, 1)
                    for i in range(GT):
                        t = g * GT + i
                        x_t = env.x[:, ds(t, 1), :].rearrange("p o d -> p (o d)")
                        v.wait_ge(biased, t + 1)
                        v.tensor_tensor(x_t, logit_ps[0:P, i % 2, 0:D], x_t, ALU.add).then_inc(bias_added, 1)

            @block.tensor
            def _(pe):
                pe.sem_inc(transposed, GT)
                pe.sem_inc(multiplied, GT)
                pe.sem_inc(gate_turned, GT)
                pe.wait_ge(landed, 16 * loads)
                with pe.Fori(0, G) as g:
                    for i in range(GT):
                        t = g * GT + i
                        pe.wait_ge(normed_ready, (2 * t + 2) if twice else t + 1)
                        pe.wait_ge(copied if routed else kept, t + (1 + (i == 0)))
                        for k in range(K2):
                            mm = pe.transpose(turned_ps[:, i % 2, k * P:(k + 1) * P],
                                              normed[:, i, k * 128:(k + 1) * 128], env.ident[0:P, 0:P])
                        mm.then_inc(transposed, 1)
                    for i in range(GT):
                        t = g * GT + i
                        pe.wait_ge(copied, t + 1 + 2)
                        pe.wait_ge(added, t + (1 + (i == 0)))
                        for k in range(K2):
                            mm = pe.matmul(logit_ps[0:P, i % 2, 0:ne], a_t[:, i, k * P:(k + 1) * P], w_sb[:, k, :],
                                           start=k == 0, stop=k == K2 - 1)
                        mm.then_inc(multiplied, 1)
                pe.wait_ge(added, 2 + T)
                pe.wait_ge(copied if routed else kept, 2 + T)
                if routed:
                    route.tensor(pe)
                with pe.Fori(0, G) as g:
                    for i in range(GT):
                        t = g * GT + i
                        pe.wait_ge(gate_ready, t + 1)
                        pe.wait_ge(gate_copied, t + (1 + (i == 0)))
                        pe.transpose(turned_ps[0:ne, i % 2, 0:P], gate_s[:, i, :], env.ident[0:P, 0:P]).then_inc(gate_turned, 1)
                    for i in range(GT):
                        t = g * GT + i
                        pe.wait_ge(gate_copied, t + 1 + 2)
                        pe.wait_ge(bias_added, t + (1 + (i == 0)))
                        pe.matmul(logit_ps[0:P, i % 2, 0:D], gate_t[:, i, :], last_sb[:], start=True,
                                  stop=True).then_inc(biased, 1)

            @block.scalar
            def _(act):
                act.sem_inc(copied, 2)
                act.sem_inc(kept, GT if routed else 2)
                with act.Fori(0, G) as g:
                    for i in range(GT):
                        t = g * GT + i
                        act.wait_ge(multiplied, t + 1)
                        act.wait_ge(transposed, t + 1 + GT)
                        act.activation(a_t[:, i, :], turned_ps[:, i % 2, 0:K2 * P], ACT.Copy).then_inc(copied, 1)
                        if kind == "L0":
                            act.activation(env.rows[:, ds(t, 1), :].rearrange("p o d -> p (o d)"), normed[:, i, :],
                                           ACT.Copy).then_inc(kept, 1)
                        if routed:
                            continue
                        act.activation(env.x_t[:, :, ds(t * P, P)], turned_ps[:, i % 2, 0:K2 * P].rearrange("p (k n) -> p k n", k=K2),
                                       ACT.Copy).then_inc(kept, 1)
                act.wait_ge(step, 2)
                act.activation(probs[:], logits[:], ACT.Exp).then_inc(exped, 1)
                if kind == "L3":
                    act.wait_ge(step, 18)
                    act.activation(top2[:], top2[:], ACT.Exp).then_inc(exped, 1)
                act.sem_inc(gate_copied, 2)
                with act.Fori(0, G) as g:
                    for i in range(GT):
                        t = g * GT + i
                        if i == 0:
                            act.wait_ge(bias_added, g * GT + 1)
                        act.wait_ge(gate_turned, t + 1 + GT)
                        act.activation(gate_t[:, i, :], turned_ps[0:ne, i % 2, 0:P], ACT.Copy).then_inc(gate_copied, 1)


UNIT = 256
UT = UNIT // 128
UNITS = round_up((2 * N + 8 * (UNIT - 1)) // UNIT, 4)
MAX_UNITS = -(-N // UNIT)
SLOT_ROWS = UNITS * UNIT


class Route:

    def __init__(self, env, st, ph, count_ps):
        self.env, self.count_ps, ne = env, count_ps, 8
        self.ne = ne
        self.both = sb(env, st, "both", [P, T, ne])
        self.earlier = sb(env, st, "earlier", [P, P])
        self.inside = sb(env, st, "inside", [P, T, ne])
        self.in_tile = sb(env, st, "in_tile", [P, T, ne])
        self.sum = [sb(env, st, f"sum{j}", [P, T, ne]) for j in range(2)]
        self.limit = sb(env, st, "limit", [P, MAX_UNITS])
        self.over = sb(env, st, "over", [P, ne, MAX_UNITS])
        self.units = sb(env, st, "units", [P, ne])
        self.end = [sb(env, st, f"end{j}", [P, ne]) for j in range(2)]
        self.slot = sb(env, st, "slot", [P, 2, T])
        self.ended = sb(env, st, "ended", [1, UNITS, ne])
        self.expert = sb(env, st, "expert", [1, UNITS])
        self.chosen, self.counted = ph.sem(), ph.sem()

    def tensor(self, pe):
        env, cols = self.env, T * self.ne
        count_ps = self.count_ps
        pe.wait_ge(self.chosen, 1)
        pe.matmul(count_ps[0:P, 0, 0:cols], self.earlier[:], self.both[:].rearrange("p t e -> p (t e)"), start=True, stop=True)
        pe.matmul(count_ps[0:P, 1, 0:cols], env.ones[0:P, 0:P], self.both[:].rearrange("p t e -> p (t e)"), start=True,
                  stop=True).then_inc(self.counted, 1)

    def vector(self, v, done, one_a, one_b, top, top2):
        env, ne = self.env, self.ne
        v.tensor_copy(env.gate_of_choice[:, 0, :], top[:])
        v.tensor_copy(env.gate_of_choice[:, 1, :], top2[:])
        done(v.tensor_scalar(self.earlier[:], env.iota[0:P, 0:P], env.part[0:P, :], None, ALU.is_gt))
        done(v.tensor_tensor(self.both[:], one_a[:], one_b[:], ALU.add))
        v.sem_inc(self.chosen, 1)
        v.wait_ge(self.counted, 1)

        def counts(j):
            return self.count_ps[0:P, j, 0:T * ne].rearrange("p (t e) -> p t e", t=T)

        done(v.tensor_copy(self.inside[:], counts(0)))
        done(v.tensor_copy(self.in_tile[:], counts(1)))
        done(v.tensor_copy(self.sum[0][:], counts(1)))
        now, step = 0, 1
        while step < T:
            a, b = self.sum[now], self.sum[1 - now]
            done(v.tensor_copy(b[:, 0:step, :], a[:, 0:step, :]))
            done(v.tensor_tensor(b[:, step:T, :], a[:, step:T, :], a[:, 0:T - step, :], ALU.add))
            now, step = 1 - now, 2 * step
        upto = self.sum[now]
        total = upto[:, T - 1:T, :].rearrange("p o e -> p (o e)")
        done(v.tensor_scalar(self.limit[:], env.iota[0:P, 0:MAX_UNITS], float(UNIT), None, ALU.mult))
        done(v.tensor_tensor(self.over[:], self.limit[:].unsqueeze(1).to_broadcast([P, ne, MAX_UNITS]),
                             total.unsqueeze(2).to_broadcast([P, ne, MAX_UNITS]), ALU.is_lt))
        done(v.tensor_reduce(self.units[:], self.over[:], AX.X, ALU.add))
        done(v.tensor_copy(self.end[0][:], self.units[:]))
        at, step = 0, 1
        while step < ne:
            a, b = self.end[at], self.end[1 - at]
            done(v.tensor_copy(b[:, 0:step], a[:, 0:step]))
            done(v.tensor_tensor(b[:, step:ne], a[:, step:ne], a[:, 0:ne - step], ALU.add))
            at, step = 1 - at, 2 * step
        end = self.end[at]
        done(v.tensor_tensor(self.ended[:], end[0:1, :].unsqueeze(1).to_broadcast([1, UNITS, ne]),
                             env.iota[0:1, 0:UNITS].unsqueeze(2).to_broadcast([1, UNITS, ne]), ALU.is_le))
        done(v.tensor_reduce(self.expert[:], self.ended[:], AX.X, ALU.add))
        done(v.tensor_scalar(self.expert[:], self.expert[:], float(ne - 1), None, ALU.min))
        done(v.tensor_copy(env.expert_of_unit[:], self.expert[:]))
        done(v.tensor_tensor(self.units[:], end[:], self.units[:], ALU.subtract))
        done(v.tensor_scalar(self.units[:], self.units[:], float(UNIT), None, ALU.mult))
        done(v.tensor_tensor(self.in_tile[:], upto[:], self.in_tile[:], ALU.subtract))
        done(v.tensor_tensor(self.inside[:], self.inside[:], self.in_tile[:], ALU.add))
        done(v.tensor_tensor(self.inside[:], self.inside[:], self.units[:].unsqueeze(1).to_broadcast([P, T, ne]), ALU.add))
        for c, one in enumerate((one_a, one_b)):
            done(v.tensor_tensor(self.both[:], self.inside[:], one[:], ALU.mult))
            done(v.tensor_reduce(self.slot[:, c, :], self.both[:], AX.X, ALU.add))
        done(v.tensor_copy(env.slots[:], self.slot[:]))


def routed_experts_phase(env, kind):
    nc = env.nc
    ph = Phase(env)
    a = env.a
    hidden = 1024 if kind == "L1" else D
    hc = hidden // 128
    n_slots = 4
    with ExitStack() as st:
        w1 = sb(env, st, "w1", [128, n_slots, K2, hidden])
        w2 = sb(env, st, "w2", [128, n_slots, hc, D])
        b1 = sb(env, st, "b1", [128, n_slots, hc])
        ln = sb(env, st, "ln", [128, n_slots, 2, K2]) if kind == "L1" else None
        rows = sb(env, st, "rows", [128, n_slots, UT, D])
        x_e = sb(env, st, "x_e", [128, 2, K2, UNIT])
        h = sb(env, st, "h", [128, 2, hc, UNIT])
        y = sb(env, st, "y", [128, n_slots, UT, D])
        choice = sb(env, st, "choice", [P, n_slots, 2, D])
        turn_ps = ps(env, st, "turn_ps", [128, K2 * UNIT])
        hidden_ps = ps(env, st, "hidden_ps", [128, 4, 512])
        out_ps = ps(env, st, "out_ps", [128, UT, 512])
        landed = [ph.sem() for _ in range(n_slots)]
        stored = [ph.sem() for _ in range(n_slots)]
        turned, x_ready, multiplied, activated, finished, copied, used = [ph.sem() for _ in range(7)]
        first_scatter = env.scatter_base
        env.scatter_base += 16 * 2 * T
        first_gather = list(env.gathered_base)
        for s in range(SLOTS):
            env.gathered_base[s] += 16 * 2 * len(range(s, T, SLOTS))
        parts = [(w1, f"{kind}_ffn_{'w' if kind == 'L0' else 'W'}1"), (w2, f"{kind}_ffn_{'w' if kind == 'L0' else 'W'}2")]
        loads = len(parts) + 2 + (2 if kind == "L1" else 0)
        with nc.Block() as block:

            @block.sync
            def _(sp):
                ph.clear_other()

                def load(j, s):
                    e = sp.value_load(env.expert_of_unit[0:1, ds(j, 1)], min_val=0, max_val=7)
                    for tile, name in parts:
                        sp.dma_start(tile[:, s], a[name][ds(e, 1), :, :].rearrange("o (k p) n -> p (o k) n", p=128)).then_inc(landed[s], 16)
                    sp.dma_start(b1[:, s], a[f"{kind}_ffn_b1"][:, ds(e * hc, hc)]).then_inc(landed[s], 16)
                    if kind == "L1":
                        sp.dma_start(ln[:, s, 0], a["L1_ffn_ln_g"][:, ds(e * K2, K2)]).then_inc(landed[s], 16)
                        sp.dma_start(ln[:, s, 1], a["L1_ffn_ln_b"][:, ds(e * K2, K2)]).then_inc(landed[s], 16)
                    sp.dma_start(rows[:, s], env.x_slots[ds(j * UNIT, UNIT), :].rearrange("(c p) d -> p c d", p=128)).then_inc(landed[s], 16)

                def store(j, s):
                    sp.wait_ge(copied, j * UT + (UT + UT))
                    sp.dma_start(env.y_slots[ds(j * UNIT, UNIT), :].rearrange("(c p) d -> p c d", p=128), y[:, s]).then_inc(stored[s], 16)

                for s in range(n_slots):
                    sp.sem_inc(stored[s], 1)
                sp.wait_ge(env.scattered, first_scatter + 16 * 2 * T)
                for s in range(n_slots):
                    load(s, s)
                with sp.Fori(0, UNITS // n_slots - 1) as it:
                    for s in range(n_slots):
                        j = it * n_slots + s
                        sp.wait_ge(finished, j * UT + (UT + n_slots))
                        load(j + n_slots, s)
                        store(j, s)
                for s in range(n_slots):
                    store(UNITS - n_slots + s, s)

            @block.gpsimd
            def _(pool):
                for t in range(T):
                    for c in range(2):
                        pool.indirect_dma_start(env.x_slots, bass.IndirectOffsetOnAxis(env.slots[:, c, t:t + 1], 0),
                                                env.rows[:, t, :], None).then_inc(env.scattered, 16)
                for s in range(n_slots):
                    pool.wait_ge(stored[s], 16 * (UNITS // n_slots) + 1)
                for t in range(T):
                    if t >= n_slots:
                        pool.wait_ge(used, 2 * (t - n_slots + 1))
                    for c in range(2):
                        pool.indirect_dma_start(choice[:, t % n_slots, c, :], None, env.y_slots, bass.IndirectOffsetOnAxis(
                            env.slots[:, c, t:t + 1], 0)).then_inc(env.gathered[t % n_slots], 16)

            @block.tensor
            def _(pe):
                pe.sem_inc(finished, n_slots)
                pe.sem_inc(copied, UT)

                def turn(j, s, lap):
                    pe.wait_ge(landed[s], lap * (16 * loads) + 16 * loads)
                    for c in range(UT):
                        for k in range(K2):
                            mm = pe.transpose(turn_ps[:, k * UNIT + c * 128:k * UNIT + (c + 1) * 128],
                                              rows[:, s, c, k * 128:(k + 1) * 128], env.ident[:])
                    mm.then_inc(turned, 1)

                def hidden_layer(j, s):
                    pe.wait_ge(x_ready, j + 1)
                    for m in range(hc):
                        pe.wait_ge(activated, j * hc + (m + 1))
                        for k in range(K2):
                            mm = pe.matmul(hidden_ps[:, (s * hc + m) % 4, 0:UNIT], w1[:, s, k, m * 128:(m + 1) * 128],
                                           x_e[:, s % 2, k, :], start=k == 0, stop=k == K2 - 1)
                        mm.then_inc(multiplied, 1)

                def output(j, s):
                    pe.wait_ge(activated, j * hc + (hc + 4))
                    for c in range(UT):
                        pe.wait_ge(copied, j * UT + (c + 1))
                        for k in range(hc):
                            mm = pe.matmul(out_ps[:, c, 0:D], h[:, s % 2, k, c * 128:(c + 1) * 128], w2[:, s, k, :],
                                           start=k == 0, stop=k == hc - 1)
                        mm.then_inc(finished, 1)

                def unit(j, s, lap):
                    hidden_layer(j, s)
                    turn(j + 1, (s + 1) % n_slots, lap + (s + 1) // n_slots)
                    output(j, s)

                turn(0, 0, 0)
                batch_loop(pe, UNITS - 1, 0, unit)
                hidden_layer(UNITS - 1, n_slots - 1)
                output(UNITS - 1, n_slots - 1)

            @block.scalar
            def _(act):
                act.sem_inc(activated, 4)

                def expert_input(j, s, lap):
                    act.wait_ge(landed[s], lap * (16 * loads) + 16 * loads)
                    act.wait_ge(turned, j + 1)
                    if kind == "L1":
                        for k in range(K2):
                            ins = act.activation(x_e[:, s % 2, k, :], turn_ps[:, k * UNIT:(k + 1) * UNIT], ACT.Identity,
                                                 bias=ln[:, s, 1, k:k + 1], scale=ln[:, s, 0, k:k + 1])
                    else:
                        ins = act.activation(x_e[:, s % 2].rearrange("p k n -> p (k n)"), turn_ps[:], ACT.Copy)
                    ins.then_inc(x_ready, 1)

                def hidden_values(j, s):
                    act.wait_ge(finished, j * UT + (n_slots - UT))
                    for m in range(hc):
                        act.wait_ge(multiplied, j * hc + (m + 1))
                        act.activation(h[:, s % 2, m, :], hidden_ps[:, (s * hc + m) % 4, 0:UNIT], ACT.Gelu,
                                       bias=b1[:, s, m:m + 1]).then_inc(activated, 1)

                def unit(j, s, lap):
                    hidden_values(j, s)
                    expert_input(j + 1, (s + 1) % n_slots, lap + (s + 1) // n_slots)

                expert_input(0, 0, 0)
                batch_loop(act, UNITS - 1, 0, unit)
                hidden_values(UNITS - 1, n_slots - 1)

            @block.vector
            def _(v):
                def copy_out(j, s, lap):
                    v.wait_ge(stored[s], lap * 16 + 1)
                    for c in range(UT):
                        v.wait_ge(finished, j * UT + (c + 1 + n_slots))
                        v.tensor_copy(y[:, s, c, :], out_ps[:, c, 0:D]).then_inc(copied, 1)

                batch_loop(v, UNITS, 0, copy_out)
                for t in range(T):
                    s = t % n_slots
                    v.wait_ge(env.gathered[s], first_gather[s] + 32 * (t // n_slots + 1))
                    for c in range(2):
                        v.scalar_tensor_tensor(out=env.x[:, t, :], in0=choice[:, s, c, :], scalar=env.gate_of_choice[:, c, t:t + 1],
                                               in1=env.x[:, t, :], op0=ALU.mult, op1=ALU.add).then_inc(used, 1)
                        v.wait_ge(used, 2 * t + c + 1)


PIECES = ((0, 320), (320, GN - 320))


def hidden_pieces(layers):
    return sum(-(-l["out"] // 128) for l in layers) * len(PIECES)


class Expert:

    def __init__(self, env, layers, w_last, k_last, ring, s):
        self.env, self.layers, self.w_last, self.k_last, self.ring, self.s = env, layers, w_last, k_last, ring, s
        self.pieces = hidden_pieces(layers)

    def tensor(self, pe, x_cols, first, tiles, hidden_ps, out_ps, offset=0):
        s, j, before = self.s, 0, 0
        for n, layer in enumerate(self.layers):
            for c, (lo, size) in enumerate(PIECES):
                for m in range(-(-layer["out"] // 128)):
                    rows = min(128, layer["out"] - m * 128)
                    pe.wait_ge(s.activated, first + (j + 1))
                    if n and m == 0:
                        pe.wait_ge(s.activated, first + (before + (c + 1) * (before_per) + self.ring))
                    kc = -(-layer["in"] // 128)
                    for k in range(kc):
                        kr = min(128, layer["in"] - k * 128)
                        rhs = x_cols(k, lo, size) if n == 0 else self.layers[n - 1]["h"][0:kr, k, lo:lo + size]
                        mm = pe.matmul(hidden_ps[0:rows, (offset + j) % self.ring, 0:size],
                                       layer["w"][0:kr, k, m * 128:m * 128 + rows], rhs, start=k == 0, stop=k == kc - 1)
                    mm.then_inc(s.multiplied, 1)
                    j += 1
            before_per = -(-layer["out"] // 128)
            before = j - before_per * len(PIECES)
        last = self.layers[-1]
        for i in range(GT):
            if i == 0:
                pe.wait_ge(s.activated, first + (before + before_per + self.ring))
            if i == 2:
                pe.wait_ge(s.activated, first + (before + 2 * before_per + self.ring))
            gap = {0: 1, 4: 4}.get(i, 5)
            pe.wait_ge(s.mixed, tiles + (i + 1 - gap + 5))
            kc = -(-last["out"] // 128)
            for k in range(kc):
                kr = min(128, last["out"] - k * 128)
                mm = pe.matmul(out_ps[0:P, i % 4, 0:D], last["h"][0:kr, k, i * P:(i + 1) * P],
                               self.w_last[0:kr, k, :], start=k == 0, stop=k == kc - 1)
            mm.then_inc(s.finished, 1)

    def scalar(self, act, column, first, hidden_ps, offset=0):
        s, j = self.s, 0
        for n, layer in enumerate(self.layers):
            for c, (lo, size) in enumerate(PIECES):
                for m in range(-(-layer["out"] // 128)):
                    rows = min(128, layer["out"] - m * 128)
                    act.wait_ge(s.multiplied, first + (j + 1))
                    act.sem_inc(s.hold, 1)
                    scale = layer["scale"](column, m, rows) if layer.get("scale") else 1.0
                    act.activation(layer["h"][0:rows, m, lo:lo + size], hidden_ps[0:rows, (offset + j) % self.ring, 0:size],
                                   layer["func"], bias=layer["bias"](column, m, rows), scale=scale).then_inc(s.activated, 1)
                    j += 1

    def vector(self, v, gate, tiles, g, out_ps):
        for i in range(GT):
            t = g * GT + i
            x_t = self.env.x[:, ds(t, 1), :].rearrange("p o d -> p (o d)")
            v.wait_ge(self.s.finished, tiles + (i + 1))
            v.scalar_tensor_tensor(out=x_t, in0=out_ps[0:P, i % 4, 0:D], scalar=gate(t), in1=x_t, op0=ALU.mult,
                                   op1=ALU.add).then_inc(self.s.mixed, 1)


def experts_phase(env):
    nc = env.nc
    ph = Phase(env)
    a = env.a
    ne = 8
    hidden = D
    hc = hidden // 128
    n_hidden = 2
    ring = 4
    with ExitStack() as st:
        names = ["L2_ffn_W1", "L2_ffn_W2", "L2_ffn_Wo"]
        w_slots = []
        for s in range(2):
            w_slots.append([sb(env, st, f"w{s}_0", [128, K2, hidden]), sb(env, st, f"w{s}_1", [128, hc, hidden]),
                            sb(env, st, f"w{s}_last", [128, hc, D])])
        hs = [sb(env, st, f"h{n}", [128, hc, GN]) for n in range(n_hidden)]
        cols = ne * hc
        raw = {p: sb(env, st, f"raw_{p}", [128, cols]) for p in ("b1", "g1", "be1", "m1", "v1", "b2", "g2", "be2", "m2", "v2")}
        eps = sb(env, st, "eps", [128, 1])
        hidden_ps = ps(env, st, "hidden_ps", [128, ring, 512])
        out_ps = ps(env, st, "out_ps", [128, 4, 512])
        sems = ExpertSems(ph)
        w_landed = [ph.sem(), ph.sem()]
        params_landed, rooted, folded, pe_hold = [ph.sem() for _ in range(4)]

        def column(which):
            return lambda e, m, rows: raw[which][:, ds(e * hc + m, 1)]

        experts = []
        for s in range(2):
            layers = []
            for n in range(n_hidden):
                layers.append({"in": D, "out": hidden, "w": w_slots[s][n], "h": hs[n], "func": ACT.Relu,
                               "bias": column(f"b{n + 1}"), "scale": column(f"g{n + 1}")})
            experts.append(Expert(env, layers, w_slots[s][-1], hc, ring, sems))
        pieces = experts[0].pieces
        with nc.Block() as block:

            @block.sync
            def _(sp):
                ph.clear_other()
                for p, tile in raw.items():
                    sp.dma_start(tile[:], a[f"L2_ffn_{p}"]).then_inc(params_landed, 16)
                with sp.Fori(0, ne // 2) as pair:
                    for s in range(2):
                        e = pair * 2 + s
                        sp.wait_ge(sems.finished, (e + 1) * (G * GT))
                        for n, name in enumerate(names):
                            sp.dma_start(w_slots[s][n][:], a[name][ds(e, 1), :, :].rearrange("o (k p) n -> p (o k) n", p=128)).then_inc(w_landed[s], 16)
                sp.wait_ge(w_landed[0], 16 * len(names) * (ne // 2))
                sp.wait_ge(w_landed[1], 16 * len(names) * (ne // 2))

            @block.tensor
            def _(pe):
                pe.sem_inc(sems.finished, 2 * G * GT)
                with pe.Fori(0, ne // 2) as pair:
                    for s in range(2):
                        pe.wait_ge(w_landed[s], (pair + 1) * (16 * len(names)))
                        pe.sem_inc(pe_hold, 1)
                        with pe.Fori(0, G) as g:
                            unit = pair * (2 * G) + (s * G + g)

                            def x_cols(k, lo, size):
                                return env.x_t[:, k, ds(g * GN + lo, size)]

                            experts[s].tensor(pe, x_cols, unit * pieces, unit * GT, hidden_ps, out_ps)

            @block.scalar
            def _(act):
                act.wait_ge(params_landed, 16 * len(raw))
                act.sem_inc(sems.activated, ring)
                act.wait_ge(folded, 1)
                act.activation(raw["v1"][:], raw["v1"][:], ACT.Sqrt, bias=eps[:]).then_inc(rooted, 1)
                act.activation(raw["v2"][:], raw["v2"][:], ACT.Sqrt, bias=eps[:]).then_inc(rooted, 1)
                act.wait_ge(folded, 11)
                with act.Fori(0, ne // 2) as pair:
                    for s in range(2):
                        with act.Fori(0, G) as g:
                            unit = pair * (2 * G) + (s * G + g)
                            e = pair * 2 + s
                            experts[s].scalar(act, e, unit * pieces, hidden_ps)

            @block.vector
            def _(v):
                v.sem_inc(sems.mixed, 5)
                v.memset(eps[:], 1e-3).then_inc(folded, 1)
                v.wait_ge(rooted, 2)
                n = [1]

                def done(ins):
                    n[0] += 1
                    ins.then_inc(folded, 1)
                    v.wait_ge(folded, n[0])

                for j in "12":
                    gain, shift = raw["g" + j][:], raw["b" + j][:]
                    done(v.reciprocal(raw["v" + j][:], raw["v" + j][:]))
                    done(v.tensor_tensor(gain, gain, raw["v" + j][:], ALU.mult))
                    done(v.tensor_tensor(shift, shift, raw["m" + j][:], ALU.subtract))
                    done(v.tensor_tensor(shift, shift, gain, ALU.mult))
                    done(v.tensor_tensor(shift, shift, raw["be" + j][:], ALU.add))
                with v.Fori(0, ne // 2) as pair:
                    for s in range(2):
                        with v.Fori(0, G) as g:
                            unit = pair * (2 * G) + (s * G + g)
                            e = pair * 2 + s
                            experts[s].vector(v, lambda t: env.gates[:, ds(t, 1), ds(e, 1)].rearrange("p o e -> p (o e)"),
                                              unit * GT + 2 * G * GT, g, out_ps)


def gather_sum_phase(env, table, index_of_visit, key_of_edge, tile_of_visit, tiles, sums, rows, visits):
    nc = env.nc
    ph = Phase(env)
    batches = visits // VB
    with ExitStack() as st:
        gather = Gather(env, st, ph, table, index_of_visit, batches)
        hit = sb(env, st, "hit", [128, SLOTS, VB, rows])
        sum_ps = ps(env, st, "sum_ps", [128, SLOTS, VB, D])
        cleared, hits_made, summed = [ph.sem() for _ in range(3)]
        with nc.Block() as block:

            @block.sync
            def _(sp):
                ph.clear_other()

            @block.gpsimd
            def _(pool):
                pool.memset(sums[:], 0.0).then_inc(cleared, 1)
                gather.gpsimd(pool)

            @block.scalar
            def _(act):
                batch_loop(act, batches, 0, lambda k, slot, lap: gather.scalar(act, k, slot))

            @block.vector
            def _(v):
                v.wait_ge(cleared, 1)
                v.sem_inc(summed, SLOTS * VB)
                for k in range(2):
                    make_hits(v, env, hit[:, k], key_of_edge, rows, k).then_inc(hits_made, 1)

                def one_batch(k, slot, lap):
                    make_hits(v, env, hit[:, (slot + 2) % SLOTS], key_of_edge, rows, k + 2).then_inc(hits_made, 1)
                    v.wait_ge(gather.freed, k + (1 + SLOTS))
                    for i in range(VB):
                        tile = v.value_load(tile_of_visit[0:1, ds(k * VB + i, 1)], min_val=0, max_val=tiles - 1)
                        v.wait_ge(summed, k * VB + (i + SLOTS * VB))
                        here = sums[:, ds(tile, 1), :].rearrange("p o c -> p (o c)")
                        v.tensor_tensor(here, here, sum_ps[0:rows, slot, i, :], ALU.add).then_inc(summed, 1)

                batch_loop(v, batches, 0, one_batch)

            @block.tensor
            def _(pe):
                pe.sem_inc(gather.freed, SLOTS)

                def one_batch(k, slot, lap):
                    pe.wait_ge(hits_made, k + 1)
                    pe.wait_ge(summed, k * VB + VB)
                    gather.wait(pe, slot, lap)
                    for i in range(VB):
                        mm = pe.matmul(sum_ps[0:rows, slot, i, :], hit[:, slot, i, 0:rows], gather.rows[:, slot, i, :],
                                       start=True, stop=True)
                    mm.then_inc(gather.freed, 1)

                batch_loop(pe, batches, 0, one_batch)


def move_phase(env, to_dram):
    ph = Phase(env)
    moved = ph.sem()
    with env.nc.Block() as block:

        @block.sync
        def _(sp):
            ph.clear_other()
            rows = env.x_table.rearrange("(t p) d -> p t d", p=P)
            if to_dram:
                sp.dma_start(rows, env.x[:]).then_inc(moved, 16)
            else:
                sp.dma_start(env.x[:], rows).then_inc(moved, 16)
            sp.wait_ge(moved, 16)


WB = 2
NWP = round_up(NW, 2 * WB)


def relation_attention_phase(env):
    nc = env.nc
    ph = Phase(env)
    a = env.a
    M = WB * WR
    batches = NWP // WB
    with ExitStack() as st:
        w_sb = sb(env, st, "w_sb", [128, K2, 3 * D])
        bias_col = sb(env, st, "bias_col", [128, 3 * D // 128])
        v_bias = sb(env, st, "v_bias", [WR, D])
        other = sb(env, st, "other", [WR, WR])
        share = sb(env, st, "share", [WR, WN])
        s_rows = sb(env, st, "s_rows", [WR, WB, D])
        s_t = sb(env, st, "s_t", [128, K2, M])
        qk_t = sb(env, st, "qk_t", [128, 4, M])
        v_sb = sb(env, st, "v_sb", [WR, 2, WB, D])
        score = sb(env, st, "score", [WR, 2, WB * HEADS, WR])
        top = sb(env, st, "top", [WR, WB * HEADS])
        total = sb(env, st, "total", [WR, WB * HEADS])
        chooser = sb(env, st, "chooser", [WR, WB * HEADS, WN])
        weight = sb(env, st, "weight", [WR, WB * HEADS * WN])
        o_rows = sb(env, st, "o_rows", [WN, WB, D])
        turn_ps = ps(env, st, "turn_ps", [128, 512])
        qk_ps = ps(env, st, "qk_ps", [128, 2, 512])
        v_ps = ps(env, st, "v_ps", [128, 512])
        score_ps = ps(env, st, "score_ps", [128, WB, 512])
        weight_ps = ps(env, st, "weight_ps", [128, 512])
        o_ps = ps(env, st, "o_ps", [128, 512])
        landed, taken, turned, turned_copied, projected, qk_out, v_out = [ph.sem() for _ in range(7)]
        scored, masked, topped, lowered, exped, summed, inverted, chosen = [ph.sem() for _ in range(8)]
        weighed, weights_out, attended, o_out, stored, hold = [ph.sem() for _ in range(6)]
        with nc.Block() as block:

            @block.sync
            def _(sp):
                ph.clear_other()
                sp.dma_start(w_sb[:], a["L1_gnn_in_proj_w"].rearrange("(k p) n -> p k n", p=128)).then_inc(landed, 16)
                sp.dma_start(bias_col[:], a["L1_gnn_in_proj_b"]).then_inc(landed, 16)
                sp.dma_start(v_bias[:], env.row("in_proj_b_row")[:, 2 * D:3 * D].to_broadcast([WR, D])).then_inc(landed, 16)
                sp.dma_start(other[:], a["other_node"]).then_inc(landed, 16)
                sp.dma_start(share[:], a["node_share"]).then_inc(landed, 16)
                sp.sem_inc(stored, 1)
                with sp.Fori(0, batches) as k:
                    sp.wait_ge(o_out, k + 1 + 1)
                    sp.dma_start(env.o_table[ds(k * (WB * WN), WB * WN), :].rearrange("(j n) d -> n j d", n=WN),
                                 o_rows[:]).then_inc(stored, 16)
                sp.wait_ge(stored, 16 * batches + 1)

            @block.gpsimd
            def _(pool):
                def take(k):
                    pool.wait_ge(turned, k + 1)
                    pool.sem_inc(hold, 1)
                    pool.tensor_copy(s_rows[:], env.window_sums[:, ds(k * WB, WB), :]).then_inc(taken, 1)

                take(0)
                with pool.Fori(0, batches - 1) as k:
                    take(k + 1)
                for ahead in (1, 2):
                    pool.wait_ge(turned, batches + ahead)
                    pool.sem_inc(taken, 1)

            @block.tensor
            def _(pe):
                pe.sem_inc(turned, 1)
                pe.sem_inc(attended, 1)
                pe.sem_inc(weighed, 2)
                pe.wait_ge(landed, 80)

                def turn(k):
                    pe.wait_ge(taken, k + 1)
                    pe.wait_ge(turned_copied, k + 1)
                    for c in range(K2):
                        for j in range(WB):
                            mm = pe.transpose(turn_ps[:, (c * WB + j) * WR:(c * WB + j + 1) * WR],
                                              s_rows[:, j, c * 128:(c + 1) * 128], env.ident[0:WR, 0:WR])
                    mm.then_inc(turned, 1)

                def project(k):
                    pe.wait_ge(turned_copied, k + 1 + 1)
                    pe.wait_ge(qk_out, k + 1)
                    pe.wait_ge(v_out, k + 1)
                    for m in range(4):
                        for c in range(K2):
                            pe.matmul(qk_ps[:, m // 2, (m % 2) * M:(m % 2 + 1) * M], w_sb[:, c, m * 128:(m + 1) * 128],
                                      s_t[:, c, :], start=c == 0, stop=c == K2 - 1)
                    for j in range(WB):
                        for c in range(K2):
                            mm = pe.matmul(v_ps[0:WR, j * D:(j + 1) * D], s_t[:, c, j * WR:(j + 1) * WR],
                                           w_sb[:, c, 2 * D:3 * D], start=c == 0, stop=c == K2 - 1)
                    mm.then_inc(projected, 1)

                turn(0)
                project(0)
                turn(1)

                def attend(k, b):
                    pe.wait_ge(chosen, k + 1)
                    pe.wait_ge(weights_out, k + 1)
                    for n in range(WB * HEADS):
                        mm = pe.matmul(weight_ps[0:WR, n * WN:(n + 1) * WN], score[:, b, n, :], chooser[:, n, :],
                                       start=True, stop=True)
                    mm.then_inc(weighed, 1)

                def mean(k, b):
                    pe.wait_ge(weights_out, k + 1 + 1)
                    pe.wait_ge(o_out, k + 1)
                    for n in range(WB * HEADS):
                        j, h = n // 2 % WB, n % 2 * 2 + n // (2 * WB)
                        mm = pe.matmul(o_ps[0:WN, j * D + h * HD:j * D + (h + 1) * HD],
                                       weight[:, n * WN:(n + 1) * WN], v_sb[:, b, j, h * HD:(h + 1) * HD],
                                       start=True, stop=True)
                    mm.then_inc(attended, 1)

                def step(k, b, before):
                    pe.wait_ge(qk_out, k + 1 + 1)
                    pe.wait_ge(masked, k + 1)
                    for j in range(WB):
                        for h in range(HEADS):
                            f = slice((h % 2) * HD, (h % 2 + 1) * HD)
                            n = slice(j * WR, (j + 1) * WR)
                            at = (j * 2 + h // 2) * WR
                            mm = pe.matmul(score_ps[0:WR, h % 2, at:at + WR], qk_t[f, h // 2, n],
                                           qk_t[f, 2 + h // 2, n], start=True, stop=True)
                    mm.then_inc(scored, 1)
                    project(k + 1)
                    if before:
                        attend(k - 1, 1 - b)
                    turn(k + 2)
                    if before:
                        mean(k - 1, 1 - b)

                step(0, 0, False)
                step(1, 1, True)
                with pe.Fori(1, batches // 2) as it:
                    for b in range(2):
                        step(it * 2 + b, b, True)
                attend(batches - 1, 1)
                mean(batches - 1, 1)

            @block.scalar
            def _(act):
                act.wait_ge(landed, 80)
                act.sem_inc(turned_copied, 1)
                act.sem_inc(qk_out, 1)
                act.sem_inc(weights_out, 1)
                act.sem_inc(o_out, 1)

                def copy_turned(k):
                    if not isinstance(k, int) or k > 0:
                        act.wait_ge(projected, k)
                    act.wait_ge(turned, k + 1 + 1)
                    act.activation(s_t[:].rearrange("p c n -> p (c n)"), turn_ps[:, 0:K2 * M], ACT.Copy).then_inc(turned_copied, 1)

                def qk(k):
                    if not isinstance(k, int) or k > 0:
                        act.wait_ge(scored, k)
                    act.wait_ge(projected, k + 1)
                    for m in range(4):
                        ins = act.activation(qk_t[:, m, :], qk_ps[:, m // 2, (m % 2) * M:(m % 2 + 1) * M], ACT.Identity,
                                             bias=bias_col[:, m:m + 1])
                    ins.then_inc(qk_out, 1)

                copy_turned(0)
                qk(0)
                copy_turned(1)

                def weights(k):
                    act.wait_ge(weighed, k + 1 + 2)
                    act.activation(weight[:], weight_ps[0:WR, 0:WB * HEADS * WN], ACT.Copy).then_inc(weights_out, 1)

                def out(k):
                    act.wait_ge(attended, k + 1 + 1)
                    act.wait_ge(stored, k * 16 + 1)
                    act.activation(o_rows[:].rearrange("p j d -> p (j d)"), o_ps[0:WN, 0:WB * D], ACT.Copy).then_inc(o_out, 1)

                def step(k, b, before):
                    act.wait_ge(lowered, k + 1)
                    act.activation(score[:, b], score[:, b], ACT.Exp, scale=HD ** -0.5).then_inc(exped, 1)
                    qk(k + 1)
                    if before:
                        weights(k - 1)
                    copy_turned(k + 2)
                    if before:
                        out(k - 1)

                step(0, 0, False)
                step(1, 1, True)
                with act.Fori(1, batches // 2) as it:
                    for b in range(2):
                        step(it * 2 + b, b, True)
                weights(batches - 1)
                out(batches - 1)

            @block.vector
            def _(v):
                v.wait_ge(landed, 80)
                v.sem_inc(v_out, 1)
                v.sem_inc(masked, 1)

                def values(b, k):
                    if not isinstance(k, int) or k > 0:
                        v.wait_ge(attended, k)
                    v.wait_ge(projected, k + 1)
                    v.tensor_tensor(v_sb[:, b], v_ps[0:WR].rearrange("p (j d) -> p j d", j=WB),
                                    v_bias[:].unsqueeze(1).to_broadcast([WR, WB, D]), ALU.add).then_inc(v_out, 1)

                values(0, 0)
                with v.Fori(0, batches // 2) as it:
                    for b in range(2):
                        k = it * 2 + b
                        v.wait_ge(scored, k + 1)
                        v.wait_ge(weighed, k + 1)
                        v.tensor_tensor(score[:, b].rearrange("p (u j) n -> p u j n", u=2),
                                        score_ps[0:WR, :, 0:HEADS * WR].rearrange("p u (j n) -> p u j n", j=HEADS),
                                        other[:].unsqueeze(1).unsqueeze(1).to_broadcast([WR, 2, HEADS, WR]),
                                        ALU.add).then_inc(masked, 1)
                        v.wait_ge(masked, k + 1 + 1)
                        v.tensor_reduce(top[:], score[:, b], AX.X, ALU.max).then_inc(topped, 1)
                        v.wait_ge(topped, k + 1)
                        v.tensor_tensor(score[:, b], score[:, b], top[:].unsqueeze(2).to_broadcast([WR, WB * HEADS, WR]),
                                        ALU.subtract).then_inc(lowered, 1)
                        v.wait_ge(exped, k + 1)
                        v.tensor_reduce(total[:], score[:, b], AX.X, ALU.add).then_inc(summed, 1)
                        v.wait_ge(summed, k + 1)
                        v.reciprocal(total[:], total[:]).then_inc(inverted, 1)
                        v.wait_ge(inverted, k + 1)
                        v.wait_ge(weighed, k + 1 + 1)
                        v.tensor_tensor(chooser[:], share[:].unsqueeze(1).to_broadcast([WR, WB * HEADS, WN]),
                                        total[:].unsqueeze(2).to_broadcast([WR, WB * HEADS, WN]), ALU.mult).then_inc(chosen, 1)
                        values(1 - b, k + 1)


def relation_output_phase(env):
    nc = env.nc
    ph = Phase(env)
    a = env.a
    with ExitStack() as st:
        out_w = sb(env, st, "out_w", [128, K2, D])
        proj_w = sb(env, st, "proj_w", [128, K2, D])
        out_b = sb(env, st, "out_b", [128, K2])
        proj_bc = sb(env, st, "proj_bc", [P, D])
        normed = sb(env, st, "normed", [P, GT, D])
        o_rows = sb(env, st, "o_rows", [P, GT, D])
        o_t = sb(env, st, "o_t", [128, GT, K2 * P])
        h_t = sb(env, st, "h_t", [128, GT, K2 * P])
        turn_ps = ps(env, st, "turn_ps", [128, 2, 512])
        h_ps = ps(env, st, "h_ps", [128, 2, 512])
        y_ps = ps(env, st, "y_ps", [128, 2, 512])
        w_landed, turned, turned_copied, mixed, h_out, projected, added, biased, normed_made = [ph.sem() for _ in range(9)]
        o_landed = [ph.sem() for _ in range(GT)]
        with nc.Block() as block:

            @block.sync
            def _(sp):
                ph.clear_other()
                sp.dma_start(out_w[:], a["L1_gnn_attn_out_w"].rearrange("(k p) n -> p k n", p=128)).then_inc(w_landed, 16)
                sp.dma_start(proj_w[:], a["L1_gnn_proj_w"].rearrange("(k p) n -> p k n", p=128)).then_inc(w_landed, 16)
                sp.dma_start(out_b[:], a["L1_gnn_attn_out_b"]).then_inc(w_landed, 16)
                sp.dma_start(proj_bc[:], env.row("L1_gnn_proj_b").to_broadcast([P, D])).then_inc(w_landed, 16)
                with sp.Fori(0, G) as g:
                    for i in range(GT):
                        t = g * GT + i
                        sp.wait_ge(turned, t + 1)
                        sp.dma_start(o_rows[:, i, :], env.o_table[ds(t * P, P), :]).then_inc(o_landed[i], 16)
                for i in range(GT):
                    sp.wait_ge(o_landed[i], 16 * G)

            @block.vector
            def _(v):
                v.wait_ge(w_landed, 64)
                v.sem_inc(added, 2)
                with v.Fori(0, G) as g:
                    for i in range(GT):
                        t = g * GT + i
                        x_t = env.x[:, ds(t, 1), :].rearrange("p o d -> p (o d)")
                        v.wait_ge(mixed, t + 1)
                        v.tensor_scalar(normed[:, i, :], x_t, env.mean[:, ds(t, 1)], env.rstd[:, ds(t, 1)],
                                        ALU.subtract, ALU.mult).then_inc(normed_made, 1)
                    for i in range(GT):
                        t = g * GT + i
                        x_t = env.x[:, ds(t, 1), :].rearrange("p o d -> p (o d)")
                        v.tensor_tensor(x_t, x_t, proj_bc[:], ALU.add).then_inc(biased, 1)
                        v.wait_ge(biased, t + 1)
                        v.wait_ge(projected, t + 1 + GT)
                        v.tensor_tensor(x_t, y_ps[0:P, i % 2, 0:D], x_t, ALU.add).then_inc(added, 1)

            @block.tensor
            def _(pe):
                pe.sem_inc(turned, GT)
                pe.sem_inc(mixed, GT)
                pe.sem_inc(projected, GT)
                pe.wait_ge(w_landed, 64)
                with pe.Fori(0, G) as g:
                    for i in range(GT):
                        t = g * GT + i
                        pe.wait_ge(o_landed[i], (g + 1) * 16)
                        pe.wait_ge(turned_copied, t + (1 + (i == 0)))
                        for k in range(K2):
                            mm = pe.transpose(turn_ps[:, i % 2, k * P:(k + 1) * P], o_rows[:, i, k * 128:(k + 1) * 128],
                                              env.ident[0:P, 0:P])
                        mm.then_inc(turned, 1)
                    for i in range(GT):
                        t = g * GT + i
                        pe.wait_ge(turned_copied, t + 1 + 2)
                        pe.wait_ge(normed_made, t + 1)
                        pe.wait_ge(h_out, t + (1 + (i == 0)))
                        for m in range(K2):
                            out = h_ps[:, i % 2, m * P:(m + 1) * P]
                            for k in range(K2):
                                pe.matmul(out, out_w[:, k, m * 128:(m + 1) * 128], o_t[:, i, k * P:(k + 1) * P],
                                          start=k == 0, stop=False)
                            mm = pe.matmul(out, normed[:, i, m * 128:(m + 1) * 128], env.ident[0:P, 0:P],
                                           start=False, stop=True)
                        mm.then_inc(mixed, 1)
                    for i in range(GT):
                        t = g * GT + i
                        pe.wait_ge(h_out, t + 1 + 2)
                        pe.wait_ge(added, t + (1 + (i == 0)))
                        for k in range(K2):
                            mm = pe.matmul(y_ps[0:P, i % 2, 0:D], h_t[:, i, k * P:(k + 1) * P], proj_w[:, k, :],
                                           start=k == 0, stop=k == K2 - 1)
                        mm.then_inc(projected, 1)

            @block.scalar
            def _(act):
                act.wait_ge(w_landed, 64)
                act.sem_inc(turned_copied, 2)
                act.sem_inc(h_out, 2)
                with act.Fori(0, G) as g:
                    for i in range(GT):
                        t = g * GT + i
                        act.wait_ge(mixed, t + 1)
                        act.wait_ge(turned, t + 1 + GT)
                        act.activation(o_t[:, i, :], turn_ps[:, i % 2, 0:K2 * P], ACT.Copy).then_inc(turned_copied, 1)
                    for i in range(GT):
                        t = g * GT + i
                        act.wait_ge(projected, t + 1)
                        act.wait_ge(mixed, t + 1 + GT)
                        for m in range(K2):
                            ins = act.activation(h_t[:, i, m * P:(m + 1) * P], h_ps[:, i % 2, m * P:(m + 1) * P],
                                                 ACT.Identity, bias=out_b[:, m:m + 1])
                        ins.then_inc(h_out, 1)


def spread_phase(env, kind):
    nc = env.nc
    ph = Phase(env)
    with ExitStack() as st:
        own = sb(env, st, "own", [P, T, D]) if kind == "L3" else None
        bias_bc = sb(env, st, "bias_bc", [P, D])
        landed, step = ph.sem(), ph.sem()
        with nc.Block() as block:

            @block.sync
            def _(sp):
                ph.clear_other()
                if kind == "L3":
                    sp.dma_start(own[:], env.k_table.rearrange("(t p) d -> p t d", p=P)).then_inc(landed, 16)
                    sp.dma_start(bias_bc[:], env.row("L3_gnn_b").to_broadcast([P, D])).then_inc(landed, 16)

            @block.vector
            def _(v):
                n = [0]

                def done(ins):
                    n[0] += 1
                    ins.then_inc(step, 1)
                    v.wait_ge(step, n[0])

                y, x = env.node_sums[:], env.x[:]
                scale = (env.norm2 if kind == "L2" else env.norm3)[:].unsqueeze(2).to_broadcast([P, T, D])
                if kind == "L3":
                    v.wait_ge(landed, 32)
                    done(v.tensor_tensor(y, y, own[:], ALU.add))
                done(v.tensor_tensor(y, y, scale, ALU.mult))
                if kind == "L3":
                    done(v.tensor_tensor(y, y, bias_bc[:].unsqueeze(1).to_broadcast([P, T, D]), ALU.add))
                    done(v.scalar_tensor_tensor(out=y, in0=y, scalar=0.2, in1=y, op0=ALU.mult, op1=ALU.max))
                done(v.tensor_tensor(x, x, y, ALU.add))


def small_experts_phase(env):
    nc = env.nc
    ph = Phase(env)
    a = env.a
    ring = 2
    with ExitStack() as st:
        sizes = [("s", None, 256, 128)] + [("e", e, 128, 64) for e in range(4)]
        sems = ExpertSems(ph)
        landed = ph.sem()
        hidden_ps = ps(env, st, "hidden_ps", [128, ring, 512])
        out_ps = ps(env, st, "out_ps", [128, 4, 512])
        h1 = sb(env, st, "h1", [128, 2, GN])
        h2 = sb(env, st, "h2", [128, 1, GN])
        bias = {"sb1": sb(env, st, "sb1", [128, 2]), "sb2": sb(env, st, "sb2", [128, 1]),
                "eb1": sb(env, st, "eb1", [128, 4]), "eb2": sb(env, st, "eb2", [64, 4])}
        loads, experts = [(tile, a[f"L3_ffn_{p}"]) for p, tile in bias.items()], []
        for which, e, d1, d2 in sizes:
            w1 = sb(env, st, f"w1_{which}{e}", [128, K2, d1])
            w2 = sb(env, st, f"w2_{which}{e}", [128, d1 // 128, d2])
            w3 = sb(env, st, f"w3_{which}{e}", [d2, 1, D])
            for j, tile in enumerate((w1, w2, w3)):
                src = a[f"L3_ffn_{which}W{j + 1}"]
                src = src if e is None else src[e]
                loads.append((tile, src.rearrange("(k p) n -> p k n", p=min(128, src.shape[0]))))
            def cols(b, first):
                return lambda g, m, rows: bias[b][0:rows, first + m:first + m + 1]
            experts.append(Expert(env, [
                {"in": D, "out": d1, "w": w1, "h": h1, "func": ACT.Relu, "bias": cols(which + "b1", e or 0)},
                {"in": d1, "out": d2, "w": w2, "h": h2, "func": ACT.Relu, "bias": cols(which + "b2", e or 0)},
            ], w3, 1, ring, sems))
        total = sum(x.pieces for x in experts)
        firsts = [sum(x.pieces for x in experts[:n]) for n in range(len(experts))]
        with nc.Block() as block:

            @block.sync
            def _(sp):
                ph.clear_other()
                for tile, src in loads:
                    sp.dma_start(tile[:], src).then_inc(landed, 16)

            @block.tensor
            def _(pe):
                pe.wait_ge(landed, 16 * len(loads))
                with pe.Fori(0, G) as g:
                    for n, x in enumerate(experts):
                        x.tensor(pe, lambda k, lo, size: env.x_t[:, k, ds(g * GN + lo, size)], g * total + firsts[n],
                                 g * (5 * GT) + n * GT, hidden_ps, out_ps, firsts[n])

            @block.scalar
            def _(act):
                act.wait_ge(landed, 16 * len(loads))
                act.sem_inc(sems.activated, ring)
                with act.Fori(0, G) as g:
                    for n, x in enumerate(experts):
                        x.scalar(act, g, g * total + firsts[n], hidden_ps, firsts[n])

            @block.vector
            def _(v):
                v.sem_inc(sems.mixed, 5)
                with v.Fori(0, G) as g:
                    for n, x in enumerate(experts):
                        x.vector(v, lambda t: env.ones[0:P, 0:1] if n == 0 else
                                 env.gates[:, ds(t, 1), n - 1:n].rearrange("p o e -> p (o e)"),
                                 g * (5 * GT) + n * GT, g, out_ps)


def routing_buffers(env, st):
    env.gates = sb(env, st, "gates", [P, T, 8])
    env.rows = sb(env, st, "rows_all", [P, T, D])
    env.gate_of_choice = sb(env, st, "gate_of_choice", [P, 2, T])
    env.slots = sb(env, st, "slots", [P, 2, T], I32)
    env.expert_of_unit = sb(env, st, "expert_of_unit", [1, UNITS], I32)


def build(nc, a, out, stop=99):
    env = Env(nc, a, out)
    with ExitStack() as st:
        env.sem_sets = [[st.enter_context(nc.semaphore(f"set{s}_{i}")) for i in range(24)] for s in range(2)]
        env.gathered = [st.enter_context(nc.semaphore(f"gathered_{s}")) for s in range(SLOTS)]
        env.gathered_base = [0] * SLOTS
        env.scattered = st.enter_context(nc.semaphore("scattered"))
        env.scatter_base = 0
        env.mean = sb(env, st, "mean", [P, T])
        env.rstd = sb(env, st, "rstd", [P, T])
        env.mean2 = sb(env, st, "mean2", [P, T])
        env.rstd2 = sb(env, st, "rstd2", [P, T])
        env.norm2 = sb(env, st, "norm2", [P, T])
        env.norm3 = sb(env, st, "norm3", [P, T])
        env.ident = sb(env, st, "ident", [128, 128])
        env.ones = sb(env, st, "ones", [128, 128])
        env.iota = sb(env, st, "iota", [128, VW_PAD])
        env.part = sb(env, st, "part", [128, 1])
        env.tile_of_visit = sb(env, st, "tile_of_visit", [1, VT_PAD], I32)
        env.window_of_visit = sb(env, st, "window_of_visit", [1, VW_PAD], I32)
        env.src_of_visit = sb(env, st, "src_of_visit", [128, VT_PAD], I32)
        env.message_of_visit = sb(env, st, "message_of_visit", [128, VW_PAD], I32)
        env.rel_dst = sb(env, st, "rel_dst", [128, VT_PAD])
        env.type64 = sb(env, st, "type64", [128, VT_PAD])
        env.row_of_edge = sb(env, st, "row_of_edge", [128, VW_PAD])
        env.k_table = nc.dram_tensor("k_table", (N, D), F32).ap()
        env.v_table = nc.dram_tensor("v_table", (N, D), F32).ap()
        env.x_table = nc.dram_tensor("x_table", (N, D), F32).ap()
        env.o_table = nc.dram_tensor("o_table", (NWP * WN, D), F32).ap()
        env.x_slots = nc.dram_tensor("x_slots", (SLOT_ROWS, D), F32).ap()
        env.y_slots = nc.dram_tensor("y_slots", (SLOT_ROWS, D), F32).ap()
        env.messages = nc.dram_tensor("messages", (N * R6, D), F32).ap()

        x_stack = ExitStack()
        env.x = sb(env, x_stack, "x", [P, T, D])
        setup_phase(env, a)
        stats_phase(env, env.x)
        with ExitStack() as l0:
            env.sums = sb(env, l0, "sums", [P, T, VC])
            env.peaks = sb(env, l0, "peaks", [P, T, HEADS])
            env.scores = sb(env, l0, "scores", [128, VT_PAD, HEADS])
            with ExitStack() as sq:
                env.q = sb(env, sq, "q", [P, T, D])
                project_phase(env, a["qkv_w"].rearrange("(k p) n -> p k n", p=128),
                              env.row("qkv_b").to_broadcast([P, 3 * D]), 3 * D, "qkv")
                score_phase(env)
            peak_phase(env)
            attend_phase(env)
            message_phase(env)
            stats_phase(env, env.sums[:, :, 0:D])
            affine_phase(env)
        if stop == 0:
            store_phase(env)
            x_stack.close()
            return
        stats_phase(env, env.x)
        with ExitStack() as f0:
            routing_buffers(env, f0)
            router_phase(env, "L0")
            routed_experts_phase(env, "L0")
        if stop == 1:
            store_phase(env)
            x_stack.close()
            return
        stats_phase(env, env.x)
        project_phase(env, a["L1_gnn_W"].rearrange("(k p) n -> p k n", p=128),
                      env.row("L1_gnn_b").to_broadcast([P, R6 * D]), R6 * D, "plain",
                      env.messages.rearrange("(n r) d -> n (r d)", r=R6))
        move_phase(env, True)
        x_stack.close()
        with ExitStack() as l1:
            env.window_sums = sb(env, l1, "window_sums", [WR, NWP, D])
            gather_sum_phase(env, env.messages, env.message_of_visit, env.row_of_edge, env.window_of_visit, NW,
                             env.window_sums, WR, VW)
            relation_attention_phase(env)
        env.x = sb(env, x_stack, "x", [P, T, D])
        move_phase(env, False)
        relation_output_phase(env)
        if stop == 2:
            store_phase(env)
            x_stack.close()
            return
        stats_phase(env, env.x)
        with ExitStack() as f1:
            routing_buffers(env, f1)
            with ExitStack() as sn:
                env.normed = sb(env, sn, "normed_all", [P, T, D])
                norm_phase(env)
                stats_phase(env, env.normed, env.mean2, env.rstd2)
            router_phase(env, "L1")
            routed_experts_phase(env, "L1")
        if stop == 3:
            store_phase(env)
            x_stack.close()
            return
        stats_phase(env, env.x)
        for kind in ("L2", "L3"):
            with ExitStack() as l2:
                env.node_sums = sb(env, l2, "node_sums", [P, T, D])
                env.scale = env.norm2 if kind == "L2" else env.norm3
                w = a[f"{kind}_gnn_W"].rearrange("(k p) n -> p k n", p=128)
                bias = env.row("L2_gnn_b").to_broadcast([P, D]) if kind == "L2" else None
                project_phase(env, w, bias, D, "scaled", env.k_table)
                gather_sum_phase(env, env.k_table, env.src_of_visit, env.rel_dst, env.tile_of_visit, T,
                                 env.node_sums, P, VT)
                spread_phase(env, kind)
            stats_phase(env, env.x)
            with ExitStack() as f2:
                env.gates = sb(env, f2, "gates", [P, T, 8])
                env.x_t = sb(env, f2, "x_t", [128, K2, N])
                router_phase(env, kind)
                if kind == "L2":
                    experts_phase(env)
                    stats_phase(env, env.x)
                else:
                    small_experts_phase(env)
        store_phase(env)
        x_stack.close()


def kernel(**inputs):
    import numpy as _np
    import concourse.bacc as _bacc
    from concourse import mybir as _mybir
    from concourse.bass_utils import run_bass_kernel_spmd as _run

    given = {n: _np.ascontiguousarray(v) for n, v in inputs.items()}
    given["qkv_w"] = _np.concatenate([given.pop(f"L0_gnn_W{c}") for c in "qkv"], axis=1)
    given["qkv_b"] = _np.concatenate([given.pop(f"L0_gnn_b{c}") for c in "qkv"])
    for n in ("L1_gnn_in_proj_w", "L1_gnn_attn_out_w", "L1_gnn_proj_w", "L2_gnn_W", "L0_ffn_router_w"):
        given[n] = _np.ascontiguousarray(given[n].T)
    given["L1_gnn_W"] = _np.ascontiguousarray(given["L1_gnn_W"].transpose(1, 0, 2).reshape(D, R6 * D))
    given["L1_gnn_b"] = given["L1_gnn_b"].reshape(-1)
    given["in_proj_b_row"] = given["L1_gnn_in_proj_b"]
    node = _np.arange(WR) % WN
    given["other_node"] = _np.where(node[:, None] == node[None, :], 0.0, -1e30).astype(_np.float32)
    given["node_share"] = _np.where(node[:, None] == _np.arange(WN)[None, :], 1.0 / R6, 0.0).astype(_np.float32)
    given["L0_gnn_query_emb"] = _np.ascontiguousarray(given["L0_gnn_query_emb"].reshape(-1, 128).T)
    for n in ["L1_gnn_in_proj_b", "L1_gnn_attn_out_b", "L0_ffn_b1", "L1_ffn_b1", "L1_ffn_ln_g", "L1_ffn_ln_b", "L3_ffn_sb1", "L3_ffn_sb2", "L3_ffn_eb1"] + [
            f"L2_ffn_{p}{j}" for p in ("b", "g", "be", "m", "v") for j in "12"]:
        given[n] = _np.ascontiguousarray(given[n].reshape(-1, 128).T)
    given["L3_ffn_eb2"] = _np.ascontiguousarray(given["L3_ffn_eb2"].T)
    nc = _bacc.Bacc("TRN2", target_bir_lowering=False, num_devices=1)
    arrays, args = {}, {}
    for n, v in given.items():
        arrays[f"in_{n}"] = v
        args[n] = nc.dram_tensor(f"in_{n}", v.shape, _mybir.dt.from_np(v.dtype), kind="ExternalInput").ap()
    out = nc.dram_tensor("out_0_dram", given["x"].shape, F32, kind="ExternalOutput").ap()
    build(nc, args, out)
    r = _run(nc, [arrays], core_ids=[0])
    return r.results[0]["out_0_dram"]
```
